# Optimizing a Trainium2 kernel written in Bass

```python
import numpy as np
import jax
import jax.numpy as jnp

def _softmax(x, axis=-1):
    return jax.nn.softmax(x, axis=axis)

def _gelu(x):
    return jax.nn.gelu(x, approximate=True)

def _silu(x):
    return jax.nn.silu(x)

def _sigmoid(x):
    return jax.nn.sigmoid(x)

def _layernorm(x, axis=-1, eps=1e-05):
    m = jnp.mean(x, axis=axis, keepdims=True)
    v = jnp.var(x, axis=axis, keepdims=True)
    return (x - m) / jnp.sqrt(v + eps)

def _scatter_add(tgt, idx, src, axis=0):
    return tgt.at[idx].add(src)

def _segment_sum(src, seg, n):
    return jax.ops.segment_sum(src, seg, n)
kernel_name = 'mk_hybrid_d2_jaxref_r8_189a75'

def setup_inputs(seed: int=0):
    np.random.seed(seed)
    _w = jnp.asarray

    def _L0_attn_a_setup():
        import jax, jax.numpy as jnp
        import numpy as np
        MODEL_DIM = 128
        HEADS = 16
        HEAD_DIM = MODEL_DIM // HEADS
        B, T = (2, 256)
        TB_LEN = 500
        key = jax.random.key(seed)
        ks = jax.random.split(key, 12)
        s = 0.02
        d = MODEL_DIM
        return {'x': jax.random.normal(ks[0], (B, T, d), dtype=jnp.float32), 'Wq': jax.random.normal(ks[1], (d, d), dtype=jnp.float32) * s, 'bq': jnp.zeros((d,), jnp.float32), 'Wk': jax.random.normal(ks[2], (d, d), dtype=jnp.float32) * s, 'bk': jnp.zeros((d,), jnp.float32), 'Wv': jax.random.normal(ks[3], (d, d), dtype=jnp.float32) * s, 'bv': jnp.zeros((d,), jnp.float32), 'Wo': jax.random.normal(ks[4], (d, d), dtype=jnp.float32) * s, 'bo': jnp.zeros((d,), jnp.float32), 'et_gate': jax.random.normal(ks[5], (1, 1, 1), dtype=jnp.float32), 'is_gate': jax.random.normal(ks[6], (1, 1, 1), dtype=jnp.float32), 'time_bias': jnp.linspace(-1.0, 1.0, TB_LEN, dtype=jnp.float32).reshape(1, 1, TB_LEN)}
    _L0_attn_a_in = _L0_attn_a_setup()

    def _L0_attn_b_setup():
        import jax, jax.numpy as jnp
        import numpy as np
        EPS = 1e-08

        def rms_norm(x, scale):
            d = x.shape[-1]
            norm = jnp.linalg.norm(x, ord=2, axis=-1, keepdims=True)
            rms = norm * d ** (-0.5)
            return scale * (x / (rms + EPS))
        key = jax.random.key(seed)
        ks = jax.random.split(key, 4)
        B, N, C, H = (2, 256, 128, 16)
        hd = C // H
        x = jax.random.normal(ks[0], (B, N, C), dtype=jnp.float32)
        Wqkv = jax.random.normal(ks[1], (C, 3 * C), dtype=jnp.float32) * C ** (-0.5)
        Wproj = jax.random.normal(ks[2], (C, C), dtype=jnp.float32) * C ** (-0.5)
        bproj = jnp.zeros((C,), dtype=jnp.float32)
        q_scale = jnp.ones((hd,), dtype=jnp.float32)
        k_scale = jnp.ones((hd,), dtype=jnp.float32)
        return {'x': x, 'Wqkv': Wqkv, 'Wproj': Wproj, 'bproj': bproj, 'q_scale': q_scale, 'k_scale': k_scale}
    _L0_attn_b_in = _L0_attn_b_setup()

    def _L0_ffn_setup():
        import jax, jax.numpy as jnp
        import numpy as np
        IN_DIM = 128
        HIDDEN = 128
        OUT_DIM = 128
        NUM_EXPERTS = 16
        TOP_K = 2
        ROUTER_TEMP = 1.0
        LN_EPS = 1e-05

        def _layernorm(h, g, b):
            mu = jnp.mean(h, axis=-1, keepdims=True)
            var = jnp.mean(jnp.square(h - mu), axis=-1, keepdims=True)
            return (h - mu) * jax.lax.rsqrt(var + LN_EPS) * g + b
        key = jax.random.key(seed)
        ks = jax.random.split(key, 8)
        s_in = 1.0 / np.sqrt(IN_DIM)
        s_h = 1.0 / np.sqrt(HIDDEN)
        x = jax.random.normal(ks[0], (4, 256, IN_DIM), dtype=jnp.float32)
        Wr = jax.random.uniform(ks[1], (IN_DIM, NUM_EXPERTS), jnp.float32, -s_in, s_in)
        br = jax.random.uniform(ks[2], (NUM_EXPERTS,), jnp.float32, -s_in, s_in)
        W1 = jax.random.uniform(ks[3], (NUM_EXPERTS, IN_DIM, HIDDEN), jnp.float32, -s_in, s_in)
        b1 = jax.random.uniform(ks[4], (NUM_EXPERTS, HIDDEN), jnp.float32, -s_in, s_in)
        g1 = jnp.ones((NUM_EXPERTS, HIDDEN), jnp.float32)
        be1 = jnp.zeros((NUM_EXPERTS, HIDDEN), jnp.float32)
        W2 = jax.random.uniform(ks[5], (NUM_EXPERTS, HIDDEN, OUT_DIM), jnp.float32, -s_h, s_h)
        b2 = jax.random.uniform(ks[6], (NUM_EXPERTS, OUT_DIM), jnp.float32, -s_h, s_h)
        return {'x': x, 'Wr': Wr, 'br': br, 'W1': W1, 'b1': b1, 'g1': g1, 'be1': be1, 'W2': W2, 'b2': b2}
    _L0_ffn_in = _L0_ffn_setup()

    def _L1_attn_a_setup():
        import jax, jax.numpy as jnp
        import numpy as np
        D_MODEL = 128
        LN_EPS = 1e-05
        key = jax.random.key(seed)
        k_u, k_b, k_c = jax.random.split(key, 3)
        B, L, D = (8, 512, D_MODEL)
        u = jax.random.normal(k_u, (B, L, D), dtype=jnp.float32)
        log_a = jnp.log(jnp.linspace(0.9, 0.99, D, dtype=jnp.float32))
        bound = 1.0 / np.sqrt(D)
        W_b = jax.random.uniform(k_b, (D, D), minval=-bound, maxval=bound, dtype=jnp.float32)
        W_c = jax.random.uniform(k_c, (D, D), minval=-bound, maxval=bound, dtype=jnp.float32)
        gamma = jnp.ones((D,), dtype=jnp.float32)
        beta = jnp.zeros((D,), dtype=jnp.float32)
        return {'u': u, 'log_a': log_a, 'W_b': W_b, 'W_c': W_c, 'gamma': gamma, 'beta': beta}
    _L1_attn_a_in = _L1_attn_a_setup()

    def _L1_attn_b_setup():
        import jax, jax.numpy as jnp
        import numpy as np
        DIM = 128
        HEADS = 16
        HEAD_DIM = DIM // HEADS
        SCALE = float(HEAD_DIM ** (-0.25))
        ROPE_BASE = 10000.0

        def apply_rope(x):
            B, N, H, D = x.shape
            half = D // 2
            inv_freq = 1.0 / ROPE_BASE ** (jnp.arange(half, dtype=jnp.float32) / half)
            freqs = jnp.arange(N, dtype=jnp.float32)[:, None] * inv_freq[None, :]
            cos = jnp.cos(freqs)[None, :, None, :].astype(x.dtype)
            sin = jnp.sin(freqs)[None, :, None, :].astype(x.dtype)
            x1, x2 = (x[..., :half], x[..., half:])
            return jnp.concatenate([x1 * cos - x2 * sin, x1 * sin + x2 * cos], axis=-1)
        key = jax.random.key(seed)
        k1, k2, k3 = jax.random.split(key, 3)
        x = jax.random.normal(k1, (4, 512, DIM), dtype=jnp.float32)
        w_qkv = jax.random.normal(k2, (DIM, 3 * DIM), dtype=jnp.float32) * 0.02
        w_out = jax.random.normal(k3, (DIM, DIM), dtype=jnp.float32) * 0.02
        return {'x': x, 'w_qkv': w_qkv, 'w_out': w_out}
    _L1_attn_b_in = _L1_attn_b_setup()

    def _L1_ffn_setup():
        import jax, jax.numpy as jnp
        import numpy as np
        DIM = 128

        def _reference_tuple_inner(x, W_r, W_k, W_v, mu_r, mu_k):
            B, T, C = x.shape
            x_prev = jnp.concatenate([jnp.zeros((B, 1, C), x.dtype), x[:, :-1, :]], axis=1)
            xr = mu_r * x + (1.0 - mu_r) * x_prev
            xk = mu_k * x + (1.0 - mu_k) * x_prev
            r = jax.nn.sigmoid(jnp.einsum('btc,dc->btd', xr, W_r))
            k = jnp.einsum('btc,dc->btd', xk, W_k)
            k_act = jnp.square(jax.nn.relu(k))
            out = r * jnp.einsum('btc,dc->btd', k_act, W_v)
            new_state = x[:, -1, :]
            return (out, new_state)
        key = jax.random.key(seed)
        ks = jax.random.split(key, 6)
        B, T, C = (8, 256, DIM)
        x = jax.random.normal(ks[0], (B, T, C), dtype=jnp.float32)
        s = 1.0 / np.sqrt(C)
        W_r = jax.random.uniform(ks[1], (C, C), jnp.float32, -s, s)
        W_k = jax.random.uniform(ks[2], (C, C), jnp.float32, -s, s)
        W_v = jax.random.uniform(ks[3], (C, C), jnp.float32, -s, s)
        mu_r = jax.random.uniform(ks[4], (C,), jnp.float32)
        mu_k = jax.random.uniform(ks[5], (C,), jnp.float32)
        return {'x': x, 'W_r': W_r, 'W_k': W_k, 'W_v': W_v, 'mu_r': mu_r, 'mu_k': mu_k}
    _L1_ffn_in = _L1_ffn_setup()
    _d = {'L0_attn_a_x': _L0_attn_a_in['x'], 'L0_attn_a_Wq': _L0_attn_a_in['Wq'], 'L0_attn_a_bq': _L0_attn_a_in['bq'], 'L0_attn_a_Wk': _L0_attn_a_in['Wk'], 'L0_attn_a_bk': _L0_attn_a_in['bk'], 'L0_attn_a_Wv': _L0_attn_a_in['Wv'], 'L0_attn_a_bv': _L0_attn_a_in['bv'], 'L0_attn_a_Wo': _L0_attn_a_in['Wo'], 'L0_attn_a_bo': _L0_attn_a_in['bo'], 'L0_attn_a_et_gate': _L0_attn_a_in['et_gate'], 'L0_attn_a_is_gate': _L0_attn_a_in['is_gate'], 'L0_attn_a_time_bias': _L0_attn_a_in['time_bias'], 'L0_attn_b_Wqkv': _L0_attn_b_in['Wqkv'], 'L0_attn_b_Wproj': _L0_attn_b_in['Wproj'], 'L0_attn_b_bproj': _L0_attn_b_in['bproj'], 'L0_attn_b_q_scale': _L0_attn_b_in['q_scale'], 'L0_attn_b_k_scale': _L0_attn_b_in['k_scale'], 'L0_ffn_Wr': _L0_ffn_in['Wr'], 'L0_ffn_br': _L0_ffn_in['br'], 'L0_ffn_W1': _L0_ffn_in['W1'], 'L0_ffn_b1': _L0_ffn_in['b1'], 'L0_ffn_g1': _L0_ffn_in['g1'], 'L0_ffn_be1': _L0_ffn_in['be1'], 'L0_ffn_W2': _L0_ffn_in['W2'], 'L0_ffn_b2': _L0_ffn_in['b2'], 'L1_attn_a_log_a': _L1_attn_a_in['log_a'], 'L1_attn_a_W_b': _L1_attn_a_in['W_b'], 'L1_attn_a_W_c': _L1_attn_a_in['W_c'], 'L1_attn_a_gamma': _L1_attn_a_in['gamma'], 'L1_attn_a_beta': _L1_attn_a_in['beta'], 'L1_attn_b_w_qkv': _L1_attn_b_in['w_qkv'], 'L1_attn_b_w_out': _L1_attn_b_in['w_out'], 'L1_ffn_W_r': _L1_ffn_in['W_r'], 'L1_ffn_W_k': _L1_ffn_in['W_k'], 'L1_ffn_W_v': _L1_ffn_in['W_v'], 'L1_ffn_mu_r': _L1_ffn_in['mu_r'], 'L1_ffn_mu_k': _L1_ffn_in['mu_k']}
    _x0 = _d['L0_attn_a_x']
    _d['L0_attn_a_x'] = jax.random.normal(jax.random.fold_in(jax.random.key(seed), 1), (8, 256, 128), dtype=_x0.dtype)
    del _x0
    return _d

def reference(L0_attn_a_x, L0_attn_a_Wq, L0_attn_a_bq, L0_attn_a_Wk, L0_attn_a_bk, L0_attn_a_Wv, L0_attn_a_bv, L0_attn_a_Wo, L0_attn_a_bo, L0_attn_a_et_gate, L0_attn_a_is_gate, L0_attn_a_time_bias, L0_attn_b_Wqkv, L0_attn_b_Wproj, L0_attn_b_bproj, L0_attn_b_q_scale, L0_attn_b_k_scale, L0_ffn_Wr, L0_ffn_br, L0_ffn_W1, L0_ffn_b1, L0_ffn_g1, L0_ffn_be1, L0_ffn_W2, L0_ffn_b2, L1_attn_a_log_a, L1_attn_a_W_b, L1_attn_a_W_c, L1_attn_a_gamma, L1_attn_a_beta, L1_attn_b_w_qkv, L1_attn_b_w_out, L1_ffn_W_r, L1_ffn_W_k, L1_ffn_W_v, L1_ffn_mu_r, L1_ffn_mu_k):

    def _L0_attn_a_ref(x, Wq, bq, Wk, bk, Wv, bv, Wo, bo, et_gate, is_gate, time_bias):
        import jax, jax.numpy as jnp
        import numpy as np
        MODEL_DIM = 128
        HEADS = 16
        HEAD_DIM = MODEL_DIM // HEADS
        B, T = (2, 256)
        TB_LEN = 500
        Bb, Tt, D = x.shape
        H, hd = (HEADS, HEAD_DIM)
        Q = (x @ Wq.T + bq).reshape(Bb, Tt, H, hd).transpose(0, 2, 1, 3)
        K = (x @ Wk.T + bk).reshape(Bb, Tt, H, hd).transpose(0, 2, 1, 3)
        V = (x @ Wv.T + bv).reshape(Bb, Tt, H, hd).transpose(0, 2, 1, 3)
        scores = jnp.einsum('bhqd,bhkd->bhqk', Q, K) / jnp.sqrt(jnp.float32(hd))
        pos = jnp.arange(Tt)[None, :] - jnp.arange(Tt)[:, None]
        idx = jnp.clip(pos + TB_LEN // 2, 0, TB_LEN - 1)
        tp = time_bias[:, :, idx]
        tp = jnp.squeeze(tp, axis=1)[None, None]
        scores = scores + jax.nn.sigmoid(et_gate) * tp + is_gate
        attn = jax.nn.softmax(scores, axis=-1)
        context = jnp.matmul(attn, V)
        context = context.transpose(0, 2, 1, 3, 4).reshape(Bb, Tt, D)
        return context @ Wo.T + bo

    def _L0_attn_b_ref(x, Wqkv, Wproj, bproj, q_scale, k_scale):
        import jax, jax.numpy as jnp
        import numpy as np
        EPS = 1e-08

        def rms_norm(x, scale):
            d = x.shape[-1]
            norm = jnp.linalg.norm(x, ord=2, axis=-1, keepdims=True)
            rms = norm * d ** (-0.5)
            return scale * (x / (rms + EPS))
        B, N, C = x.shape
        H = 16
        hd = C // H
        scale = hd ** (-0.5)
        qkv = (x @ Wqkv).reshape(B, N, 3, H, hd)
        qkv = jnp.transpose(qkv, (2, 0, 3, 1, 4))
        q, k, v = (qkv[0], qkv[1], qkv[2])
        q = rms_norm(q, q_scale)
        k = rms_norm(k, k_scale)
        attn = jnp.einsum('bhnc,bhmc->bhnm', q, k) * scale
        attn = jax.nn.softmax(attn, axis=-1)
        out = jnp.einsum('bhnm,bhmc->bhnc', attn, v)
        out = jnp.transpose(out, (0, 2, 1, 3)).reshape(B, N, C)
        return out @ Wproj + bproj

    def _L0_ffn_ref(x, Wr, br, W1, b1, g1, be1, W2, b2):
        import jax, jax.numpy as jnp
        import numpy as np
        IN_DIM = 128
        HIDDEN = 128
        OUT_DIM = 128
        NUM_EXPERTS = 16
        TOP_K = 2
        ROUTER_TEMP = 1.0
        LN_EPS = 1e-05

        def _layernorm(h, g, b):
            mu = jnp.mean(h, axis=-1, keepdims=True)
            var = jnp.mean(jnp.square(h - mu), axis=-1, keepdims=True)
            return (h - mu) * jax.lax.rsqrt(var + LN_EPS) * g + b
        orig_shape = x.shape[:-1]
        x_flat = x.reshape(-1, x.shape[-1])
        logits = (x_flat @ Wr + br) / max(ROUTER_TEMP, 1e-06)
        probs = jax.nn.softmax(logits, axis=-1)
        topk_w, topk_idx = jax.lax.top_k(probs, TOP_K)
        topk_w = topk_w / jnp.clip(jnp.sum(topk_w, axis=-1, keepdims=True), 1e-09)
        h = jnp.einsum('nc,ech->neh', x_flat, W1) + b1
        h = _layernorm(h, g1, be1)
        h = jax.nn.gelu(h, approximate=False)
        expert_out = jnp.einsum('neh,eho->neo', h, W2) + b2
        sel = jnp.take_along_axis(expert_out, topk_idx[:, :, None], axis=1)
        y_flat = jnp.sum(sel * topk_w[:, :, None], axis=1)
        return y_flat.reshape(*orig_shape, y_flat.shape[-1])

    def _L1_attn_a_ref(u, log_a, W_b, W_c, gamma, beta):
        import jax, jax.numpy as jnp
        import numpy as np
        D_MODEL = 128
        LN_EPS = 1e-05
        B, L, D = u.shape
        a = jnp.exp(log_a)
        u_b = jnp.einsum('bld,ed->ble', u, W_b)

        def step(state, ub_t):
            state = a * state + ub_t
            return (state, state)
        init = jnp.zeros((B, D), dtype=u.dtype)
        _, states = jax.lax.scan(step, init, jnp.swapaxes(u_b, 0, 1))
        states = jnp.swapaxes(states, 0, 1)
        y = jnp.einsum('bld,ed->ble', states, W_c)
        mean = jnp.mean(y, axis=-1, keepdims=True)
        var = jnp.mean(jnp.square(y - mean), axis=-1, keepdims=True)
        return gamma * (y - mean) * jax.lax.rsqrt(var + LN_EPS) + beta

    def _L1_attn_b_ref(x, w_qkv, w_out):
        import jax, jax.numpy as jnp
        import numpy as np
        DIM = 128
        HEADS = 16
        HEAD_DIM = DIM // HEADS
        SCALE = float(HEAD_DIM ** (-0.25))
        ROPE_BASE = 10000.0

        def apply_rope(x):
            B, N, H, D = x.shape
            half = D // 2
            inv_freq = 1.0 / ROPE_BASE ** (jnp.arange(half, dtype=jnp.float32) / half)
            freqs = jnp.arange(N, dtype=jnp.float32)[:, None] * inv_freq[None, :]
            cos = jnp.cos(freqs)[None, :, None, :].astype(x.dtype)
            sin = jnp.sin(freqs)[None, :, None, :].astype(x.dtype)
            x1, x2 = (x[..., :half], x[..., half:])
            return jnp.concatenate([x1 * cos - x2 * sin, x1 * sin + x2 * cos], axis=-1)
        B, N, D = x.shape
        qkv = x @ w_qkv
        q, k, v = jnp.split(qkv, 3, axis=-1)
        q = q.reshape(B, N, HEADS, HEAD_DIM)
        k = k.reshape(B, N, HEADS, HEAD_DIM)
        v = v.reshape(B, N, HEADS, HEAD_DIM)
        q = apply_rope(q)
        k = apply_rope(k)
        q = jax.nn.elu(q * SCALE) + 1.0
        k = jax.nn.elu(k * SCALE) + 1.0
        qT = jnp.moveaxis(q, 1, 0)
        kT = jnp.moveaxis(k, 1, 0)
        vT = jnp.moveaxis(v, 1, 0)
        kv0 = jnp.zeros((B, HEADS, HEAD_DIM, HEAD_DIM), dtype=q.dtype)
        ks0 = jnp.zeros((B, HEADS, HEAD_DIM), dtype=q.dtype)

        def step(carry, qkv_t):
            kv, ks = carry
            qt, kt, vt = qkv_t
            kv = kv + jnp.einsum('bhd,bhm->bhdm', kt, vt)
            ks = ks + kt
            denom = jnp.maximum(jnp.einsum('bhd,bhd->bh', qt, ks), 1e-06)
            out_t = jnp.einsum('bhd,bhdm->bhm', qt, kv) / denom[..., None]
            return ((kv, ks), out_t)
        _, outT = jax.lax.scan(step, (kv0, ks0), (qT, kT, vT))
        out = jnp.moveaxis(outT, 0, 1).reshape(B, N, D)
        return out @ w_out

    def _L1_ffn_ref(x, W_r, W_k, W_v, mu_r, mu_k):
        import jax, jax.numpy as jnp
        import numpy as np
        DIM = 128

        def _reference_tuple_inner(x, W_r, W_k, W_v, mu_r, mu_k):
            B, T, C = x.shape
            x_prev = jnp.concatenate([jnp.zeros((B, 1, C), x.dtype), x[:, :-1, :]], axis=1)
            xr = mu_r * x + (1.0 - mu_r) * x_prev
            xk = mu_k * x + (1.0 - mu_k) * x_prev
            r = jax.nn.sigmoid(jnp.einsum('btc,dc->btd', xr, W_r))
            k = jnp.einsum('btc,dc->btd', xk, W_k)
            k_act = jnp.square(jax.nn.relu(k))
            out = r * jnp.einsum('btc,dc->btd', k_act, W_v)
            new_state = x[:, -1, :]
            return (out, new_state)
        return _reference_tuple_inner(x, W_r, W_k, W_v, mu_r, mu_k)[0]
    x = L0_attn_a_x
    x = x + _L0_attn_a_ref(_layernorm(x, axis=-1), L0_attn_a_Wq, L0_attn_a_bq, L0_attn_a_Wk, L0_attn_a_bk, L0_attn_a_Wv, L0_attn_a_bv, L0_attn_a_Wo, L0_attn_a_bo, L0_attn_a_et_gate, L0_attn_a_is_gate, L0_attn_a_time_bias)
    x = x + _L0_ffn_ref(_layernorm(x, axis=-1), L0_ffn_Wr, L0_ffn_br, L0_ffn_W1, L0_ffn_b1, L0_ffn_g1, L0_ffn_be1, L0_ffn_W2, L0_ffn_b2)
    x = x + _L0_attn_b_ref(_layernorm(x, axis=-1), L0_attn_b_Wqkv, L0_attn_b_Wproj, L0_attn_b_bproj, L0_attn_b_q_scale, L0_attn_b_k_scale)
    x = x + _L0_ffn_ref(_layernorm(x, axis=-1), L0_ffn_Wr, L0_ffn_br, L0_ffn_W1, L0_ffn_b1, L0_ffn_g1, L0_ffn_be1, L0_ffn_W2, L0_ffn_b2)
    x = x + _L1_attn_a_ref(_layernorm(x, axis=-1), L1_attn_a_log_a, L1_attn_a_W_b, L1_attn_a_W_c, L1_attn_a_gamma, L1_attn_a_beta)
    x = x + _L1_ffn_ref(_layernorm(x, axis=-1), L1_ffn_W_r, L1_ffn_W_k, L1_ffn_W_v, L1_ffn_mu_r, L1_ffn_mu_k)
    x = x + _L1_attn_b_ref(_layernorm(x, axis=-1), L1_attn_b_w_qkv, L1_attn_b_w_out)
    x = x + _L1_ffn_ref(_layernorm(x, axis=-1), L1_ffn_W_r, L1_ffn_W_k, L1_ffn_W_v, L1_ffn_mu_r, L1_ffn_mu_k)
    return x

_drawn_inputs = setup_inputs


def setup_inputs(seed=0):
    import zlib

    import numpy as np

    out = dict(_drawn_inputs(seed))
    spreads = {'L0_attn_a_bq': (0.0, 0.8),
     'L0_attn_a_bk': (0.0, 0.8),
     'L0_attn_a_bv': (0.0, 0.1),
     'L0_attn_a_bo': (0.0, 0.1),
     'L0_attn_b_bproj': (0.0, 0.1),
     'L0_attn_b_q_scale': (1.0, 0.2),
     'L0_attn_b_k_scale': (1.0, 0.2),
     'L0_ffn_g1': (1.0, 0.2),
     'L0_ffn_be1': (0.0, 0.1),
     'L1_attn_a_gamma': (1.0, 0.2),
     'L1_attn_a_beta': (0.0, 0.1)}
    factors = {'L0_attn_a_Wq': 7.256,
     'L0_attn_a_Wk': 8.0,
     'L0_attn_a_Wv': 2.984,
     'L0_attn_a_time_bias': 5.818,
     'L1_attn_b_w_qkv': 3.022,
     'L1_attn_b_w_out': 2.939,
     'L1_ffn_mu_r': 5.244}
    for name, (base, spread) in spreads.items():
        noise = np.random.default_rng([zlib.crc32(name.encode()), seed]).standard_normal(out[name].shape)
        drawn = base * np.exp(spread * noise) if base else spread * noise
        out[name] = jnp.asarray(drawn.astype(out[name].dtype))
    for name, factor in factors.items():
        out[name] = (out[name] * factor).astype(out[name].dtype)
    return out
```

```python
from contextlib import ExitStack

import concourse.bass as bass
from concourse import mybir

P = 128
NB = 8
TOK = 256
TILES = TOK // P
D = 128
H = 16
HD = D // H
HG = 4
E = 16
PAIRS = E // 2
STACK = 6 * HD
HEADROW = 64
LN_EPS = 1e-5
RMS_EPS = 1e-8

ALU = mybir.AluOpType
ACT = mybir.ActivationFunctionType
F32 = mybir.dt.float32
BF16 = mybir.dt.bfloat16
U32 = mybir.dt.uint32
AX = mybir.AxisListType

SPAN = D // HD
STAGES = ["attn_a", "out_a", "moe", "attn_b", "moe", "ssm", "mix", "attn_c", "mix"]

Q_PART = [0, 0, 1, 1, 0, 2]
K_PART = [0, 1, 0, 1, 2, 0]


class At:

    def __init__(self, reg, off, trips=None):
        self.reg, self.off, self.trips = reg, off, trips

    def __add__(self, d):
        return At(self.reg, self.off + d, self.trips)

    @property
    def par(self):
        return self.off % 2

    @property
    def ends(self):
        if self.reg is None:
            return (self.off, self.off)
        return (2 * self.trips[0] + self.off, 2 * (self.trips[1] - 1) + self.off)

    def has(self, d=0):
        return 0 <= self.ends[0] + d and self.ends[1] + d < NB

    def times(self, k, plus=0):
        if self.reg is None:
            return k * self.off + plus
        return self.reg * (2 * k) + (k * self.off + plus)

    def half(self, k, plus=0):
        if self.reg is None:
            return k * (self.off // 2) + plus
        return self.reg * k + (k * (self.off // 2) + plus)


def need(eng, sem, n):
    if isinstance(n, int) and n <= 0:
        return
    eng.wait_ge(sem, n)


class Ledger:

    def __init__(self, uses):
        self.uses, self.base, n = uses, [], 0
        for u in uses:
            self.base.append(n)
            n += NB * len(u)

    def at(self, stage, name, b):
        uses = self.uses[stage]
        names = [n for n, _ in uses]
        j = names.index(name)
        d = uses[j][1]

        def exact(t):
            return self.base[stage] + sum(min(max(t + di + (i <= j), 0), NB) for i, (_, di) in enumerate(uses))

        lo, hi = (e - d for e in b.ends)
        if b.reg is None:
            return exact(lo)
        c = len(uses)
        plus = self.base[stage] + sum(di + (i <= j) for i, (_, di) in enumerate(uses)) - c * d
        assert c * (lo + d) + plus == exact(lo) and c * (hi + d) + plus == exact(hi), (stage, name, lo, hi)
        return b.times(c, plus)


class Steps:

    def __init__(self, eng, sem):
        self.eng, self.sem, self.n = eng, sem, 0
        self.reg = None

    def loop(self, reg, first, per):
        self.reg, self.first, self.per, self.n0 = reg, first, per, self.n

    def end(self, trips):
        assert self.n - self.n0 == self.per, f"{self.sem}: {self.n - self.n0} steps in the loop's body"
        self.n = self.n0 + self.per * trips
        self.reg = None

    def value(self):
        if self.reg is None:
            return self.n
        return self.reg * self.per + (self.n - self.first * self.per)

    def then(self, ins):
        self.n += 1
        ins.then_inc(self.sem, 1)
        self.eng.wait_ge(self.sem, self.value())


def sweep(eng, steps, per, body, first, last, lo, trips):
    for t in range(first, lo):
        body(At(None, t))
    with eng.Fori(0, trips) as i:
        if steps:
            steps.loop(i, 0, per)
        for q in range(2):
            body(At(i, lo + q, (0, trips)))
        if steps:
            steps.end(trips)
    for t in range(lo + 2 * trips, last + 1):
        body(At(None, t))


USES_T = {
    "load": [("ln", 0)],
    "attn_a": [("qk", 1), ("ctx", -1), ("max", 1)],
    "out_a": [("ln", -1)],
    "attn_b": [("qk", 2), ("feat", 1), ("ctx", -1), ("ln", -1)],
    "attn_c": [("qk", 2), ("feat", 1), ("ctx", -1), ("ln", -1)],
    "moe": [("logits", 1), ("gate", 1), ("ln", -1)],
    "ssm": [("ln", -1)],
    "mix": [("ln", -1)],
}
USES_U = {
    "load": [],
    "attn_a": [("v", 1), ("ctx0", -1), ("ctx1", -1)],
    "out_a": [("update", 0)],
    "attn_b": [("v", 1), ("ctx0", -1), ("ctx1", -1), ("update", -1)],
    "attn_c": [("swapped", 2), ("v", 1), ("ctx0", -1), ("ctx1", -1), ("update", -1)],
    "moe": [("update", 0)],
    "ssm": [],
    "mix": [],
}
SWEEP = {
    "attn_a": (-1, 8, 2, 2),
    "out_a": (0, 8, 2, 2),
    "attn_b": (-2, 8, 2, 2),
    "attn_c": (-2, 8, 2, 2),
    "moe": (-1, 8, 2, 2),
    "ssm": (-1, 8, 2, 2),
    "mix": (-1, 8, 2, 2),
}


def hybrid_kernel(nc, io, out):
    led_t = Ledger([USES_T[k] for k in ["load"] + STAGES])
    led_u = Ledger([USES_U[k] for k in ["load"] + STAGES])
    with ExitStack() as ctx:
        def sb(name, shape, dt=F32):
            return ctx.enter_context(nc.sbuf_tensor(name, shape, dt))

        def ps(name, shape, dt=F32):
            return ctx.enter_context(nc.psum_tensor(name, shape, dt))

        def sem(name):
            return ctx.enter_context(nc.semaphore(name))

        ps_a = ps("ps_a", [P, 2, 512])
        ps_b = ps("ps_b", [P, 2, 512])
        ps_c = ps("ps_c", [P, 2, 512])
        ps_t = ps("ps_t", [P, 512])
        ps_u = ps("ps_u", [P, 512])

        x = sb("x", [P, NB * TILES, D])
        xnT = sb("xnT", [P, NB * TOK])
        xcur = [sb(f"xcur{i}", [P, TOK + 1]) for i in range(2)]
        xn = [sb(f"xn{i}", [P, TILES, D]) for i in range(2)]
        stats = [sb(f"stats{i}", [P, TILES, 6]) for i in range(2)]
        mv = [sb(f"mv{i}", [P, TILES, 2]) for i in range(2)]
        var_eps = [sb(f"var_eps{i}", [P, 4]) for i in range(2)]
        rstd = [sb(f"rstd{i}", [P, TILES]) for i in range(2)]
        x_new = [sb(f"x_new{i}", [P, TILES, D]) for i in range(2)]
        ln_eps = sb("ln_eps", [P, 4])
        half_neg = sb("half_neg", [P, 4])
        half_pos = sb("half_pos", [P, 4 * H])
        ident = sb("ident", [P, P])
        ident_b = sb("ident_b", [P, P], BF16)

        w = {}
        for name in ["a_wq", "a_wk", "a_wv", "a_wo", "b_wproj", "s_wb", "s_wc", "c_wout", "m_wr", "m_wk", "m_wv"]:
            w[name] = sb("w_" + name, [P, D])
        w["b_wqkv"] = sb("w_b_wqkv", [P, 3 * D])
        w["c_wqkv"] = sb("w_c_wqkv", [P, 3 * D])
        w["c_wswap"] = sb("w_c_wswap", [P, 2 * D])
        w["w1"] = sb("w_w1", [P, E, D])
        w["w2"] = sb("w_w2", [P, E, D])
        w["wr"] = sb("w_wr", [P, E])
        row = {}
        for name in ["a_bo", "a_bv", "b_bproj", "s_beta", "s_gamma"]:
            row[name] = sb("row_" + name, [P, D])
        row["br"] = sb("row_br", [P, E])
        row["qk_scale"] = sb("row_qk_scale", [P, 2, D])
        col = {}
        for name in ["a_bq", "a_bk", "et", "is", "log_a", "mu_r", "mu_k"]:
            col[name] = sb("col_" + name, [P, 1])
        g1 = sb("g1", [P, E])
        be1 = sb("be1", [P, E])
        b2_rows = sb("b2_rows", [96, D])
        b1_part = sb("b1_part", [1, 3, E * D], BF16)
        b1_rows = sb("b1_rows", [3, E * D], BF16)
        ones3 = sb("ones3", [3, P], BF16)
        gate_sel = sb("gate_sel", [96, E, P], BF16)
        decay = sb("decay", [P, 1])
        mu_r1 = sb("mu_r1", [P, 1])
        mu_k1 = sb("mu_k1", [P, 1])
        sig = sb("sig", [P, 2])
        bias_q = sb("bias_q", [P, TILES, TOK], BF16)
        bias_k = [sb(f"bias_k{i}", [P, TILES, TOK], BF16) for i in range(3)]
        bias_f = sb("bias_f", [P, 2, TILES, TOK])
        rope_cos = sb("rope_cos", [P, TILES, HD])
        rope_sin = sb("rope_sin", [P, TILES, HD])
        causal = sb("causal", [P, TILES, TOK])
        bound = sb("bound", [P, 4])

        qk32 = [sb(f"qk32_{i}", [P, 2, TOK]) for i in range(2)]
        rest = [sb(f"rest_{i}", [P, 2, TOK]) for i in range(2)]
        parts = [sb(f"parts_{i}", [P, 3, 2, TOK], BF16) for i in range(2)]
        stack_q = [sb(f"stack_q{i}", [P, H // 2, TOK], BF16) for i in range(2)]
        stack_k = [sb(f"stack_k{i}", [P, H // 2, TOK], BF16) for i in range(2)]
        v_aug = [sb(f"v_aug{i}", [P, TILES, H, 32]) for i in range(2)]
        probs_all = sb("probs_all", [P, 4, 4, TOK])
        probs = [probs_all[:, i] for i in range(4)]
        b1_f = probs_all[0:1].rearrange("p a b t -> p (a b t)")
        neg_max = sb("neg_max", [P, TILES, H])
        max_rows = sb("max_rows", [H, TOK], BF16)
        ctx_raw = sb("ctx_raw", [P, HG, TOK])
        ctx_n = sb("ctx_n", [P, TILES, D])
        ctx_T = sb("ctx_T", [P, TOK])
        ctx_flip = sb("ctx_flip", [P, H, NB, SPAN])
        den = sb("den", [P, TILES, H])
        qraw = [sb(f"qraw{i}", [P, TILES, 2, D]) for i in range(2)]
        qtmp = [sb(f"qtmp{i}", [P, TILES, 2, D]) for i in range(2)]
        feat = [sb(f"feat{i}", [P, TILES, 2, D]) for i in range(2)]
        ss = [sb(f"ss{i}", [P, 2 * TILES * H]) for i in range(2)]
        rms = [sb(f"rms{i}", [P, 2 * TILES * H]) for i in range(2)]

        lg = sb("lg", [P, TILES, 24])
        lgd = sb("lgd", [P, TILES, 18])
        lge = sb("lge", [P, TILES, 18])
        lidx = sb("lidx", [P, TILES, 8], U32)
        lidf = sb("lidf", [P, TILES, 2])
        lsum = sb("lsum", [P, TILES, 1])
        lw = sb("lw", [P, TILES, 2])
        lwt = sb("lwt", [P, TILES, 1])
        iota_e = sb("iota_e", [P, E])
        gates = sb("gates", [P, 3, TILES, E])
        gates_b = sb("gates_b", [P, 2, TILES, E], BF16)
        gate_pack = sb("gate_pack", [P, TILES, 96])
        gate_f = [sb(f"gate_f{i}", [96, TOK]) for i in range(2)]
        gate_b = [sb(f"gate_b{i}", [96, TOK], BF16) for i in range(2)]
        hst = [sb(f"hst{i}", [P, 4, 6]) for i in range(2)]
        hmv = [sb(f"hmv{i}", [P, 4, 2]) for i in range(2)]
        hve = [sb(f"hve{i}", [P, 4]) for i in range(2)]
        hrs = [sb(f"hrs{i}", [P, 4]) for i in range(2)]
        hn = [sb(f"hn{i}", [P, 2, TILES, D]) for i in range(2)]
        aT = [sb(f"aT{i}", [P, 2, TOK]) for i in range(2)]
        ag = [sb(f"ag{i}", [P, 2, TOK]) for i in range(2)]

        states = [sb(f"states{i}", [P, TOK]) for i in range(2)]
        yst = sb("yst", [P, TILES, 6])
        ymv = sb("ymv", [P, TILES, 2])
        yve = sb("yve", [P, TILES])
        yrs = sb("yrs", [P, TILES])
        yn = sb("yn", [P, TILES, D])
        upd = sb("upd", [P, TILES, D])
        mix_t = [sb(f"mix_t{i}", [P, 2, TOK]) for i in range(2)]
        mix_x = [sb(f"mix_x{i}", [P, 2, TOK]) for i in range(2)]
        r_exp = [sb(f"r_exp{i}", [P, TOK]) for i in range(2)]
        r_one = [sb(f"r_one{i}", [P, TOK]) for i in range(2)]
        k_relu = [sb(f"k_relu{i}", [P, TOK]) for i in range(2)]
        k_sq = [sb(f"k_sq{i}", [P, TOK]) for i in range(2)]

        loaded = sem("loaded")
        x_loaded = sem("x_loaded")
        setup_pool = sem("setup_pool")
        setup_dve = sem("setup_dve")
        setup_act = sem("setup_act")
        setup_dma = sem("setup_dma")
        setup_done = sem("setup_done")
        pool_step = sem("pool_step")
        dve_step = sem("dve_step")
        act_step = sem("act_step")
        stats_ready = sem("stats_ready")
        rstd_ready = sem("rstd_ready")
        xn_ready = sem("xn_ready")
        xnT_filled = sem("xnT_filled")
        t_drained = sem("t_drained")
        u_drained = sem("u_drained")
        xcur_ready = sem("xcur_ready")
        stored = sem("stored")
        first_x = sem("first_x")
        qk_filled = sem("qk_filled")
        swapped_filled = sem("swapped_filled")
        v_filled = sem("v_filled")
        rest1_ready = sem("rest1_ready")
        high_ready = sem("high_ready")
        mid_ready = sem("mid_ready")
        parts_ready = sem("parts_ready")
        q_scores_filled = sem("q_scores_filled")
        maxed = sem("maxed")
        max_filled = sem("max_filled")
        scores_filled = sem("scores_filled")
        probs_ready = sem("probs_ready")
        pv_done = sem("pv_done")
        ctx_copied = sem("ctx_copied")
        ctx_filled = sem("ctx_filled")
        ctx_ready = sem("ctx_ready")
        ctxT_filled = sem("ctxT_filled")
        ctx_sent = sem("ctx_sent")
        update_filled = sem("update_filled")
        qsq_ready = sem("qsq_ready")
        qss_ready = sem("qss_ready")
        qrms_ready = sem("qrms_ready")
        qinv_ready = sem("qinv_ready")
        feat_ready = sem("feat_ready")
        feat_filled = sem("feat_filled")
        qz_ready = sem("qz_ready")
        qzm_ready = sem("qzm_ready")
        qexp_ready = sem("qexp_ready")
        rot_ready = sem("rot_ready")
        logits_filled = sem("logits_filled")
        places_ready = sem("places_ready")
        lgd_ready = sem("lgd_ready")
        lge_ready = sem("lge_ready")
        pack_ready = sem("pack_ready")
        gate_filled = sem("gate_filled")
        gate_f_ready = sem("gate_f_ready")
        gate_ready = sem("gate_ready")
        h_filled = sem("h_filled")
        hst_ready = sem("hst_ready")
        hrs_ready = sem("hrs_ready")
        hn_ready = sem("hn_ready")
        hT_filled = sem("hT_filled")
        gelu_ready = sem("gelu_ready")
        wb_filled = sem("wb_filled")
        gated_ready = sem("gated_ready")
        w2_done = sem("w2_done")
        ub_filled = sem("ub_filled")
        scanned = sem("scanned")
        y_filled = sem("y_filled")
        yst_ready = sem("yst_ready")
        yrs_ready = sem("yrs_ready")
        mixt_ready = sem("mixt_ready")
        mixx_ready = sem("mixx_ready")
        rk_filled = sem("rk_filled")
        rexp_ready = sem("rexp_ready")
        krelu_ready = sem("krelu_ready")
        ksq_ready = sem("ksq_ready")
        o_filled = sem("o_filled")
        stack_loaded = [sem(f"stack_loaded{i}") for i in range(2)]
        max_loaded = [sem(f"max_loaded{i}") for i in range(2)]

        n_loads = [0]
        kinds = ["load"] + STAGES
        occ = [kinds[:n].count(k) for n, k in enumerate(kinds)]
        attn_no = [sum(k.startswith("attn") for k in kinds[:n]) for n in range(len(kinds))]
        ln_no = [sum(k != "attn_a" for k in kinds[:n]) for n in range(len(kinds) + 1)]
        cur_no = [sum(k not in ("load", "out_a") for k in kinds[:n]) for n in range(len(kinds))]

        block = ctx.enter_context(nc.Block())

        def xb(b):
            return x[:, bass.ds(b.times(TILES), TILES), :] if b.reg is not None else x[:, TILES * b.off:TILES * b.off + TILES, :]

        def xt(b, j):
            n = b.times(TILES, j)
            return x[:, bass.ds(n, 1), :].rearrange("p a d -> p (a d)") if b.reg is not None else x[:, n, :]

        def xnTb(b):
            return xnT[:, bass.ds(b.times(TOK), TOK)] if b.reg is not None else xnT[:, TOK * b.off:TOK * (b.off + 1)]

        def heads(a):
            return a[:, :, :, :].rearrange("p j i (o d g) -> p (j i o) d g", o=2, g=H // 2)

        def flat(a):
            return a[:, :, :, :].rearrange("p j i f -> p j (i f)")

        def rows(name, n):
            return row[name][:, :].unsqueeze(1).to_broadcast([P, n, D])

        def ln_stats(dve, st, k, b):
            nc.vector.bn_stats(stats[b.par][:, 0, :], x_new[b.par][:, 0, :])
            st.then(nc.vector.bn_stats(stats[b.par][:, 1, :], x_new[b.par][:, 1, :]))
            nc.vector.tensor_scalar_mul(xb(b), x_new[b.par][:, :, :], 1.0)
            for j in range(TILES):
                ins = nc.vector.bn_aggr(mv[b.par][:, j, :], stats[b.par][:, j, :])
            ins.then_inc(stats_ready, 1)

        def ln_rstd(pool, st, k, b):
            pool.wait_ge(stats_ready, b.times(1, NB * ln_no[k] + 1))
            st.then(nc.gpsimd.tensor_tensor(var_eps[b.par][:, 0:TILES], mv[b.par][:, :, 1], ln_eps[:, 0:TILES], ALU.add))
            nc.gpsimd.tensor_tensor(rstd[b.par][:, :], var_eps[b.par][:, 0:TILES], half_neg[:, 0:TILES], ALU.pow).then_inc(rstd_ready, 1)

        def ln_norm(dve, k, b):
            dve.wait_ge(stats_ready, b.times(1, NB * ln_no[k] + 1))
            dve.wait_ge(rstd_ready, b.times(1, NB * ln_no[k] + 1))
            need(dve, xnT_filled, b.times(1, NB * ln_no[k] - 1))
            for j in range(TILES):
                ins = nc.vector.tensor_scalar(xn[b.par][:, j, :], x_new[b.par][:, j, :], mv[b.par][:, j, 0:1], rstd[b.par][:, j:j + 1], ALU.subtract, ALU.mult)
            ins.then_inc(xn_ready, 1)

        def ln_transpose(pe, k, b):
            pe.wait_ge(xn_ready, b.times(1, NB * ln_no[k] + 1))
            need(pe, t_drained, fill_t(k, "ln", b, -1))
            for j in range(TILES):
                ins = nc.tensor.transpose(ps_t[:, j * P:(j + 1) * P], xn[b.par][:, j, :], ident[:, :])
            ins.then_inc(xnT_filled, 1)

        def ln_copy(act, k, b):
            act.wait_ge(xnT_filled, b.times(1, NB * ln_no[k] + 1))
            nc.scalar.copy(xnTb(b), ps_t[:, 0:TOK]).then_inc(t_drained, 1)

        def fill_t(k, name, b, d=0):
            return led_t.at(k, name, b) + d

        def fill_u(k, name, b, d=0):
            return led_u.at(k, name, b) + d

        def take_batch(pool, k, b, add):
            last, n = {"attn_a": (v_filled, 1), "attn_b": (v_filled, 1), "attn_c": (v_filled, 1),
                       "moe": (h_filled, PAIRS), "ssm": (ub_filled, 1), "mix": (mixx_ready, 1)}[kinds[k]]
            before = attn_no[k] if kinds[k].startswith("attn") else occ[k]
            need(pool, last, b.times(n, n * (NB * before - 1)))
            if kinds[k] == "mix":
                need(pool, mixt_ready, b.times(1, NB * before - 1))
            if add:
                nc.gpsimd.tensor_tensor(xb(b), xb(b), rows(add, TILES), ALU.add)
            if kinds[k] == "attn_a":
                nc.gpsimd.tensor_copy(xcur[b.par][:, 1:TOK + 1].rearrange("p (m n) -> p n m", m=SPAN), xnTb(b).rearrange("p (n m) -> p n m", m=SPAN)).then_inc(xcur_ready, 1)
            else:
                nc.gpsimd.tensor_copy(xcur[b.par][:, 1:TOK + 1], xnTb(b)).then_inc(xcur_ready, 1)

        def xc(b, j=None):
            if j is None:
                return xcur[b.par][:, 1:TOK + 1]
            return xcur[b.par][:, 1 + j * P:1 + (j + 1) * P]

        def has_cur(eng, k, b):
            eng.wait_ge(xcur_ready, b.times(1, NB * cur_no[k] + 1))

        @block.sync
        def _(sp):
            for t in range(4):
                sp.dma_start(x[:, 4 * t:4 * t + 4, :], io["x"].rearrange("b (t p) d -> p (b t) d", p=P)[:, 4 * t:4 * t + 4, :]).then_inc(x_loaded, 16)

            def load(dst, src):
                sp.dma_start(dst, src).then_inc(loaded, 16)
                n_loads[0] += 1

            for name in ["a_wq", "a_wk", "a_wv", "a_wo", "b_wproj", "b_wqkv", "c_wqkv", "c_wswap", "c_wout", "s_wb", "s_wc", "m_wr", "m_wk", "m_wv", "wr"]:
                load(w[name][:, :], io[name])
            for name in ["w1", "w2"]:
                load(w[name][:, :, :], io[name].rearrange("e c h -> c e h"))
            for name in ["a_bo", "a_bv", "b_bproj", "s_beta", "s_gamma", "br"]:
                load(row[name][:, :], io[name].unsqueeze(0).to_broadcast([P, io[name].shape[0]]))
            load(row["qk_scale"][:, :, :], io["qk_scale"].unsqueeze(0).to_broadcast([P, 2, D]))
            for name in ["a_bq", "a_bk", "log_a", "mu_r", "mu_k"]:
                load(col[name][:, :], io[name].unsqueeze(1))
            for name in ["et", "is"]:
                load(col[name][:, :], io[name].unsqueeze(1).to_broadcast([P, 1]))
            load(g1[:, :], io["g1"])
            load(be1[:, :], io["be1"])
            load(b1_f[:, 0:E * D], io["b1"].rearrange("e h -> (e h)").unsqueeze(0))
            load(bias_f[:, 0, :, :], io["bias_q"].rearrange("(t p) k -> p t k", p=P))
            load(bias_f[:, 1, :, :], io["bias_k"].rearrange("(t p) k -> p t k", p=P))
            load(rope_cos[:, :, :], io["rope_cos"].rearrange("(t p) d -> p t d", p=P))
            load(rope_sin[:, :, :], io["rope_sin"].rearrange("(t p) d -> p t d", p=P))
            sp.wait_ge(setup_pool, 1)
            for i in range(3):
                load(b2_rows[32 * i:32 * i + E, :], io["b2"])
            sp.wait_ge(setup_dve, 3)
            for i in range(3):
                sp.dma_start(b1_rows[i:i + 1, :], b1_part[:, i, :]).then_inc(setup_dma, 16)

            for k in range(1, len(kinds)):
                if not kinds[k].startswith("attn"):
                    continue
                a0 = attn_no[k] * NB

                def body(t):
                    if t.has(1):
                        b = t + 1
                        sp.wait_ge(parts_ready, b.times(1, a0 + 1))
                        for slot in range(6):
                            for dst, part, i in ((stack_q, Q_PART, 0), (stack_k, K_PART, 1)):
                                for odd in range(2):
                                    r0 = HEADROW * odd + HD * slot
                                    src = parts[b.par][HEADROW * odd:HEADROW * (odd + 1), part[slot], i, :]
                                    sp.dma_start(dst[b.par][r0:r0 + HD, :, :], src).then_inc(stack_loaded[b.par], 16)
                    if t.has(-1) and kinds[k] == "attn_a":
                        b = t + -1
                        sp.wait_ge(t_drained, fill_t(k, "ctx", b))
                        for m in range(SPAN):
                            dst = ctx_flip[HD * m:HD * (m + 1), :, bass.ds(b.times(1), 1), :] if b.reg is not None else ctx_flip[HD * m:HD * (m + 1), :, b.off, :]
                            sp.dma_start(dst, ctx_T[:, SPAN * m:SPAN * (m + 1)]).then_inc(ctx_sent, 16)
                    if t.has(1):
                        b = t + 1
                        if kinds[k] == "attn_a":
                            sp.wait_ge(t_drained, fill_t(k, "max", b))
                            for odd in range(2):
                                src = max_rows[odd:H:2, :]
                                r0 = HEADROW * odd + STACK
                                sp.dma_start(stack_q[b.par][r0:r0 + 1, :, :], src).then_inc(max_loaded[b.par], 16)
                f, l, lo, trips = SWEEP[kinds[k]]
                sweep(sp, None, 0, body, f, l, lo, trips)

            out_v = out.rearrange("b (t p) d -> p (b t) d", p=P)
            for b in range(NB):
                sp.wait_ge(stats_ready, NB * (ln_no[-1] - 1) + b + 1)
                sp.dma_start(out_v[:, TILES * b:TILES * (b + 1), :], x[:, TILES * b:TILES * (b + 1), :]).then_inc(stored, 16)
            sp.wait_ge(stored, 16 * NB)

        STACK_DMAS = 24

        @block.gpsimd
        def _(pool):
            st = Steps(pool, pool_step)
            nc.gpsimd.memset(b2_rows[:, :], 0.0).then_inc(setup_pool, 1)
            nc.gpsimd.memset(half_neg[:, :], -0.5)
            nc.gpsimd.memset(ln_eps[:, :], LN_EPS)
            nc.gpsimd.memset(half_pos[:, :], 0.5)
            nc.gpsimd.memset(ident[:, :], 0.0)
            nc.gpsimd.memset(ones3[:, :], 1.0)
            nc.gpsimd.memset(gate_sel[:, :, :], 0.0)
            nc.gpsimd.memset(causal[:, :, :], 1.0)
            nc.gpsimd.iota(iota_e[:, :], pattern=[[1, E]], base=0, channel_multiplier=0, allow_small_or_imprecise_dtypes=True)
            for i in range(2):
                nc.gpsimd.memset(xcur[i][:, 0:1], 0.0)
                nc.gpsimd.memset(v_aug[i][:, :, :, :], 0.0)
                nc.gpsimd.memset(stack_k[i][:, :, :], 1.0)
            st.then(nc.gpsimd.memset(gate_pack[:, :, :], 0.0))
            for i in range(2):
                nc.gpsimd.memset(v_aug[i][:, :, :, HD:HD + 1], 1.0)
            nc.gpsimd.affine_select(out=ident[:, :], in_=ident[:, :], compare_op=ALU.not_equal, fill=1.0, base=0, pattern=[[-1, P]], channel_multiplier=1)
            for j in range(TILES):
                nc.gpsimd.affine_select(out=causal[:, j, :], in_=causal[:, j, :], compare_op=ALU.is_ge, fill=0.0, base=-P * j, pattern=[[1, TOK]], channel_multiplier=-1)
            for i in range(3):
                st.then(nc.gpsimd.affine_select(out=gate_sel[:, :, :], in_=gate_sel[:, :, :], compare_op=ALU.not_equal, fill=1.0, base=-32 * i, pattern=[[-1, E], [0, P]], channel_multiplier=1))
            nc.gpsimd.tensor_copy(ident_b[:, :], ident[:, :]).then_inc(setup_pool, 1)

            def first_norm(t):
                if t.has(0):
                    ln_rstd(pool, st, 0, t)
            sweep(pool, st, 2, first_norm, 0, 7, 2, 2)

            for k in range(1, len(kinds)):
                kind = kinds[k]
                a0 = attn_no[k] * NB
                o0 = occ[k] * NB
                last = k == len(kinds) - 1

                def split(b):
                    pr = b.par
                    pool.wait_ge(high_ready, b.times(1, a0 + 1))
                    nc.gpsimd.tensor_tensor(rest[pr][:, :, :], qk32[pr][:, :, :], parts[pr][:, 0, :, :], ALU.subtract).then_inc(rest1_ready, 1)
                    pool.wait_ge(mid_ready, b.times(1, a0 + 1))
                    need(pool, pv_done, b.times(8, 8 * (a0 - 1)))
                    nc.gpsimd.tensor_tensor(parts[pr][:, 2, :, :], rest[pr][:, :, :], parts[pr][:, 1, :, :], ALU.subtract).then_inc(parts_ready, 1)

                def attn(t):
                    lead = 1 if kind == "attn_a" else 2
                    if t.has(lead):
                        take_batch(pool, k, t + lead, {"attn_a": "a_bo", "attn_b": "b_bproj"}.get(kind))
                    if kind == "attn_b" and t.has(2):
                        b = t + 2
                        pr = b.par
                        pool.wait_ge(t_drained, fill_t(k, "qk", b))
                        nc.gpsimd.tensor_tensor(qtmp[pr][:, :, :, :], qraw[pr][:, :, :, :], qraw[pr][:, :, :, :], ALU.mult).then_inc(qsq_ready, 1)
                    if t.has(1):
                        split(t + 1)
                    if kind == "attn_b" and t.has(2):
                        b = t + 2
                        pr = b.par
                        pool.wait_ge(qss_ready, b.times(1, 1))
                        nc.gpsimd.tensor_tensor(rms[pr][:, :], ss[pr][:, :], half_pos[:, :], ALU.pow).then_inc(qrms_ready, 1)
                    if t.has(-1) and kind != "attn_a":
                        ln_rstd(pool, st, k, t + -1)
                    if kind == "attn_b" and t.has(2):
                        b = t + 2
                        pr = b.par
                        pool.wait_ge(qinv_ready, b.times(1, 1))
                        need(pool, feat_filled, b.times(1, -1))
                        inv = rms[pr][:, :].rearrange("p (n g) -> p n g", g=H // 2).unsqueeze(2).to_broadcast([P, 4 * TILES, HD, H // 2])
                        st.then(nc.gpsimd.tensor_tensor(heads(qtmp[pr]), heads(qraw[pr]), inv, ALU.mult))
                        nc.gpsimd.tensor_tensor(flat(feat[pr]), flat(qtmp[pr]), row["qk_scale"][:, :, :].rearrange("p i f -> p (i f)").unsqueeze(1).to_broadcast([P, TILES, 2 * D]), ALU.mult).then_inc(feat_ready, 1)
                    if kind == "attn_c" and t.has(2):
                        b = t + 2
                        pr = b.par
                        pool.wait_ge(rot_ready, b.times(1, 1))
                        need(pool, feat_filled, b.times(1, NB - 1))
                        nc.gpsimd.tensor_tensor(flat(qraw[pr]), flat(qraw[pr]), flat(qtmp[pr]), ALU.add).then_inc(qz_ready, 1)
                        pool.wait_ge(qzm_ready, b.times(1, 1))
                        st.then(nc.gpsimd.tensor_tensor(flat(qraw[pr]), flat(qraw[pr]), flat(qtmp[pr]), ALU.add))
                        pool.wait_ge(qexp_ready, b.times(1, 1))
                        nc.gpsimd.tensor_tensor(flat(feat[pr]), flat(feat[pr]), flat(qraw[pr]), ALU.add).then_inc(feat_ready, 1)
                def out_a(t):
                    if t.has(0):
                        ln_rstd(pool, st, k, t)

                def moe(t):
                    if t.has(1):
                        take_batch(pool, k, t + 1, None)
                    for v in range(8):
                        b, u = (t, v + 1) if v < 7 else (t + 1, 0)
                        if b.has(0):
                            pr = u % 2
                            pool.wait_ge(hst_ready, b.times(8, 8 * o0 + u + 1))
                            need(pool, hn_ready, b.times(8, 8 * o0 + u - 1))
                            st.then(nc.gpsimd.tensor_tensor(hve[pr][:, :], hmv[pr][:, :, 1], ln_eps[:, :], ALU.add))
                            nc.gpsimd.tensor_tensor(hrs[pr][:, :], hve[pr][:, :], half_neg[:, :], ALU.pow).then_inc(hrs_ready, 1)
                        if v == 3 and t.has(-1):
                            ln_rstd(pool, st, k, t + -1)

                def ssm(t):
                    if t.has(1):
                        take_batch(pool, k, t + 1, "s_beta")
                    if t.has(0):
                        pool.wait_ge(yst_ready, t.times(1, 1))
                        st.then(nc.gpsimd.tensor_tensor(yve[:, :], ymv[:, :, 1], ln_eps[:, 0:TILES], ALU.add))
                        nc.gpsimd.tensor_tensor(yrs[:, :], yve[:, :], half_neg[:, 0:TILES], ALU.pow).then_inc(yrs_ready, 1)
                    if t.has(0):
                        ln_rstd(pool, st, k, t)

                def mix(t):
                    if t.has(1):
                        b = t + 1
                        take_batch(pool, k, b, None)
                        has_cur(pool, k, b)
                        need(pool, mixx_ready, b.times(1, o0 - 1))
                        for i, m in enumerate([mu_r1, mu_k1]):
                            ins = nc.gpsimd.tensor_tensor(mix_t[b.par][:, i, :], xcur[b.par][:, 0:TOK], m[:, :].to_broadcast([P, TOK]), ALU.mult)
                        ins.then_inc(mixt_ready, 1)
                    if t.has(0):
                        pool.wait_ge(krelu_ready, t.times(1, o0 + 1))
                        need(pool, o_filled, t.times(1, o0 - 1))
                        nc.gpsimd.tensor_tensor(k_sq[t.par][:, :], k_relu[t.par][:, :], k_relu[t.par][:, :], ALU.mult).then_inc(ksq_ready, 1)
                    if t.has(0) and not last:
                        ln_rstd(pool, st, k, t)

                if k == 1:
                    pool.wait_ge(loaded, 16 * n_loads[0])
                    pool.wait_ge(setup_done, 1)
                if kind != "out_a":
                    pool.wait_ge(t_drained, fill_t(k - 1, "ln", At(None, NB - 1)))
                body = {"out_a": out_a, "moe": moe, "ssm": ssm, "mix": mix}.get(kind, attn)
                per = {"attn_a": 0, "out_a": 2, "attn_b": 4, "attn_c": 4, "moe": 18, "ssm": 4, "mix": 2 * (not last)}[kind]
                f, l, lo, trips = SWEEP[kind]
                sweep(pool, st, per, body, f, l, lo, trips)

        @block.scalar
        def _(act):
            act.wait_ge(loaded, 16 * n_loads[0])
            nc.scalar.activation(decay[:, :], col["log_a"][:, :], ACT.Exp)
            nc.scalar.activation(sig[:, 0:1], col["et"][:, :], ACT.Exp, scale=-1.0).then_inc(setup_act, 1)

            def first_norm(t):
                if t.has(0):
                    ln_copy(act, 0, t)
            sweep(act, None, 0, first_norm, 0, 7, 2, 2)

            for k in range(1, len(kinds)):
                kind = kinds[k]
                a0 = attn_no[k] * NB
                o0 = occ[k] * NB
                last = k == len(kinds) - 1

                def high(b):
                    pr = b.par
                    if kind != "attn_a":
                        act.wait_ge(feat_filled, b.times(1, a0 - NB + 1))
                        nc.scalar.copy(qk32[pr][:, :, :], ps_t[:, :].rearrange("p (i t) -> p i t", i=2)).then_inc(t_drained, 1)
                        act.wait_ge(t_drained, fill_t(k, "feat", b))
                    else:
                        act.wait_ge(t_drained, fill_t(k, "qk", b))
                    need(act, stack_loaded[pr], b.half(16 * STACK_DMAS, 16 * STACK_DMAS * (a0 // 2)))
                    nc.scalar.copy(parts[pr][:, 0, :, :], qk32[pr][:, :, :]).then_inc(high_ready, 1)

                def mid(b):
                    act.wait_ge(rest1_ready, b.times(1, a0 + 1))
                    nc.scalar.copy(parts[b.par][:, 1, :, :], rest[b.par][:, :, :]).then_inc(mid_ready, 1)

                def attn(t):
                    if t.has(-1):
                        b = t + -1
                        act.wait_ge(pv_done, b.times(8, 8 * a0 + 8))
                        need(act, ctx_filled, b.times(2, 2 * a0))
                        nc.scalar.copy(ctx_raw[:, :, :], ps_c[:, :, :].rearrange("p a (b t) -> p (a b) t", t=TOK)).then_inc(ctx_copied, 1)
                    if kind == "attn_b" and t.has(2):
                        b = t + 2
                        act.wait_ge(qk_filled, b.times(1, a0 + 1))
                        need(act, feat_ready, b.times(1, -1))
                        nc.scalar.copy(qraw[b.par][:, :, :, :].rearrange("p j i d -> p (j i d)"), ps_t[:, :]).then_inc(t_drained, 1)
                    for i in range(8):
                        if t.has(0) and kind != "attn_c":
                            act.wait_ge(scores_filled, t.times(8, 8 * a0 + i + 1))
                            need(act, pv_done, t.times(8, 8 * a0 + i - 3))
                            src = (ps_b if kind == "attn_a" or i % 2 else ps_a)[:, :, :].rearrange("p a (b t) -> p (a b) t", t=TOK)
                            if kind == "attn_a":
                                ins = nc.scalar.activation(probs[i % 4][:, :, :], src, ACT.Exp)
                            else:
                                ins = nc.scalar.activation(probs[i % 4][:, :, :], src, ACT.Exp, bias=bound[:, 3:4])
                            ins.then_inc(probs_ready, 1)
                        if t.has(1):
                            if i == (0 if kind == "attn_a" else 1):
                                high(t + 1)
                            if i == (2 if kind == "attn_a" else 3):
                                mid(t + 1)
                        if kind == "attn_c" and t.has(2) and i == 5:
                            b = t + 2
                            act.wait_ge(qz_ready, b.times(1, 1))
                            nc.scalar.activation(flat(qtmp[b.par]), flat(qraw[b.par]), ACT.Relu, scale=-1.0).then_inc(qzm_ready, 1)
                            act.wait_ge(qzm_ready, b.times(1, 1))
                            nc.scalar.activation(flat(feat[b.par]), flat(qtmp[b.par]), ACT.Exp, scale=-1.0).then_inc(qexp_ready, 1)
                        if t.has(-1):
                            b = t + -1
                            if i == 4:
                                act.wait_ge(ctxT_filled, b.times(1, a0 + 1))
                                if kind == "attn_a":
                                    need(act, ctx_sent, b.times(16 * SPAN, 0))
                                else:
                                    need(act, update_filled, b.times(1, a0))
                                nc.scalar.copy(ctx_T[:, :], ps_t[:, 0:TOK]).then_inc(t_drained, 1)
                            if i == 7 and kind != "attn_a":
                                ln_copy(act, k, b)
                    if kind == "attn_a" and t.has(1):
                        b = t + 1
                        act.wait_ge(max_filled, b.times(1, 1))
                        for pr in range(2):
                            if pr != b.par:
                                need(act, max_loaded[pr], (b + -1).half(32, 32))
                        nc.scalar.copy(max_rows[:, :], ps_t[0:H, 0:TOK]).then_inc(t_drained, 1)

                def out_a(t):
                    if t.has(-1):
                        ln_copy(act, k, t + -1)

                def moe(t):
                    for v in range(8):
                        if t.has(0):
                            act.wait_ge(hT_filled, t.times(8, 8 * o0 + v + 1))
                            need(act, gated_ready, t.times(8, 8 * o0 + v - 1))
                            for e in range(2):
                                ex = 2 * v + e
                                ins = nc.scalar.activation(aT[v % 2][:, e, :], ps_b[:, v % 2, e * TOK:(e + 1) * TOK], ACT.Gelu, bias=be1[:, ex:ex + 1], scale=g1[:, ex:ex + 1])
                            ins.then_inc(gelu_ready, 1)
                        if t.has(1):
                            b = t + 1
                            if v == 3:
                                act.wait_ge(lgd_ready, b.times(1, o0 + 1))
                                nc.scalar.activation(lge[:, :, :], lgd[:, :, :], ACT.Exp).then_inc(lge_ready, 1)
                            if v == 5:
                                act.wait_ge(gate_filled, b.times(1, o0 + 1))
                                nc.scalar.copy(gate_f[b.par][:, :], ps_t[0:96, 0:TOK])
                                nc.scalar.copy(gate_b[b.par][:, :], ps_t[0:96, 0:TOK]).then_inc(t_drained, 1)
                        if v == 6 and t.has(-1):
                            ln_copy(act, k, t + -1)

                def ssm(t):
                    if t.has(-1):
                        ln_copy(act, k, t + -1)

                def mix(t):
                    if t.has(0):
                        act.wait_ge(rk_filled, t.times(1, o0 + 1))
                        need(act, o_filled, t.times(1, o0 - 1))
                        nc.scalar.activation(k_relu[t.par][:, :], ps_a[:, 1, 0:TOK], ACT.Relu).then_inc(krelu_ready, 1)
                        nc.scalar.activation(r_exp[t.par][:, :], ps_a[:, 0, 0:TOK], ACT.Exp, scale=-1.0).then_inc(rexp_ready, 1)
                    if t.has(-1) and not last:
                        ln_copy(act, k, t + -1)

                body = {"out_a": out_a, "moe": moe, "ssm": ssm, "mix": mix}.get(kind, attn)
                f, l, lo, trips = SWEEP[kind]
                sweep(act, None, 0, body, f, l, lo, trips)

        @block.vector
        def _(dve):
            st = Steps(dve, dve_step)
            dve.wait_ge(loaded, 16 * n_loads[0])
            for dst, m in ((mu_r1, col["mu_r"]), (mu_k1, col["mu_k"])):
                ins = nc.vector.tensor_scalar(dst[:, :], m[:, :], -1.0, 1.0, ALU.mult, ALU.add)
            ins.then_inc(setup_dve, 1)
            dve.wait_ge(setup_act, 1)
            st.then(nc.vector.tensor_scalar_add(sig[:, 1:2], sig[:, 0:1], 1.0))
            st.then(nc.vector.reciprocal(sig[:, 0:1], sig[:, 1:2]))
            st.then(nc.vector.tensor_scalar(bias_f[:, :, :, :], bias_f[:, :, :, :], sig[:, 0:1], col["is"][:, 0:1], ALU.mult, ALU.add))
            nc.vector.tensor_copy(bias_q[:, :, :], bias_f[:, 0, :, :])
            st.then(nc.vector.tensor_copy(bias_k[0][:, :, :], bias_f[:, 1, :, :]))
            st.then(nc.vector.tensor_tensor(bias_f[:, 0, :, :], bias_f[:, 1, :, :], bias_k[0][:, :, :], ALU.subtract))
            st.then(nc.vector.tensor_copy(bias_k[1][:, :, :], bias_f[:, 0, :, :]))
            nc.vector.tensor_tensor(bias_k[2][:, :, :], bias_f[:, 0, :, :], bias_k[1][:, :, :], ALU.subtract).then_inc(setup_dve, 1)
            n = E * D
            st.then(nc.vector.tensor_copy(b1_part[:, 0, :], b1_f[:, 0:n]))
            st.then(nc.vector.tensor_tensor(b1_f[:, n:2 * n], b1_f[:, 0:n], b1_part[:, 0, :], ALU.subtract))
            st.then(nc.vector.tensor_copy(b1_part[:, 1, :], b1_f[:, n:2 * n]))
            nc.vector.tensor_tensor(b1_part[:, 2, :], b1_f[:, n:2 * n], b1_part[:, 1, :], ALU.subtract).then_inc(setup_dve, 1)
            prod = upd[:, 0, :]
            st.then(nc.vector.tensor_tensor(prod, row["qk_scale"][:, 0, :], row["qk_scale"][:, 1, :], ALU.mult))
            st.then(nc.vector.tensor_reduce(bound[:, 0:1], prod, AX.X, ALU.max, apply_absolute_value=True))
            nc.vector.tensor_scalar_mul(bound[:, 3:4], bound[:, 0:1], -float(HD ** 0.5))
            st.then(nc.vector.tensor_scalar_mul(row["qk_scale"][:, 0, :], row["qk_scale"][:, 0, :], float(HD ** -0.5)))
            nc.vector.tensor_copy(bound[:, 1:2], bound[:, 0:1]).then_inc(setup_done, 1)

            def first_norm(t):
                if t.has(0):
                    nc.vector.tensor_scalar_mul(x_new[t.par][:, :, :], xb(t), 1.0).then_inc(first_x, 1)
                    dve.wait_ge(first_x, t.times(1, 1))
                    ln_stats(dve, st, 0, t)
                    ln_norm(dve, 0, t)
            dve.wait_ge(x_loaded, 64)
            sweep(dve, st, 2, first_norm, 0, 7, 2, 2)

            for k in range(1, len(kinds)):
                kind = kinds[k]
                a0 = attn_no[k] * NB
                o0 = occ[k] * NB
                last = k == len(kinds) - 1

                def residual(b, upd_ap, sem_, value):
                    ins = nc.vector.tensor_tensor(x_new[b.par][:, :, :], xb(b), upd_ap, ALU.add)
                    if sem_ is None:
                        st.then(ins)
                    else:
                        ins.then_inc(sem_, 1)
                        dve.wait_ge(sem_, value)

                def attn(t):
                    if t.has(1) and kind == "attn_a":
                        b = t + 1
                        pr = b.par
                        dve.wait_ge(qk_filled, b.times(1, a0 + 1))
                        need(dve, parts_ready, b.times(1, a0 - 1))
                        nc.vector.tensor_scalar(qk32[pr][:, 0, :], ps_t[:, 0:TOK], col["a_bq"][:, 0:1], float(HD ** -0.5), ALU.add, ALU.mult)
                        nc.vector.tensor_scalar(qk32[pr][:, 1, :], ps_t[:, TOK:2 * TOK], col["a_bk"][:, 0:1], None, ALU.add).then_inc(t_drained, 1)
                    if t.has(2) and kind == "attn_c":
                        b = t + 2
                        pr = b.par
                        for src, sm, n_, tab, dst, done in ((ps_t, qk_filled, a0 + 1, rope_cos, qraw, t_drained), (ps_u, swapped_filled, 1, rope_sin, qtmp, u_drained)):
                            dve.wait_ge(sm, b.times(1, n_))
                            need(dve, feat_ready, b.times(1, NB - 1))
                            for j in range(TILES):
                                tb = tab[:, j, :].unsqueeze(1).unsqueeze(3).to_broadcast([P, 4, HD, H // 2])
                                ins = nc.vector.tensor_tensor(heads(dst[pr])[:, 4 * j:4 * j + 4], src[:, j * TOK:(j + 1) * TOK].rearrange("p (n d g) -> p n d g", d=HD, g=H // 2), tb, ALU.mult)
                            ins.then_inc(done, 1)
                        nc.vector.tensor_copy(bound[:, 2:3], bound[:, 0:1]).then_inc(rot_ready, 1)
                    if t.has(1):
                        b = t + 1
                        dve.wait_ge(v_filled, b.times(1, a0 + 1))
                        need(dve, pv_done, b.times(8, 8 * (a0 - 1)))
                        dst = v_aug[b.par][:, :, :, 0:HD]
                        src = ps_u[:, 0:TILES * D].rearrange("p (j h d) -> p j h d", j=TILES, d=HD)
                        if kind == "attn_a":
                            bv = row["a_bv"][:, :].rearrange("p (h d) -> p h d", d=HD)
                            for j in range(TILES):
                                ins = nc.vector.tensor_tensor(dst[:, j], src[:, j], bv, ALU.add)
                            ins.then_inc(u_drained, 1)
                        else:
                            for j in range(TILES):
                                ins = nc.vector.tensor_copy(dst[:, j], src[:, j])
                            ins.then_inc(u_drained, 1)
                    for i in range(8):
                        if kind == "attn_c" and t.has(0):
                            dve.wait_ge(scores_filled, t.times(8, 8 * a0 + i + 1))
                            need(dve, pv_done, t.times(8, 8 * a0 + i - 3))
                            src = (ps_b if i % 2 else ps_a)[:, :, :].rearrange("p a (b t) -> p (a b) t", t=TOK)
                            m = causal[:, i % 2, :].unsqueeze(1).to_broadcast([P, 4, TOK])
                            nc.vector.tensor_tensor(probs[i % 4][:, :, :], src, m, ALU.mult).then_inc(probs_ready, 1)
                        if kind == "attn_b" and t.has(2):
                            b = t + 2
                            pr = b.par
                            if i == 1:
                                dve.wait_ge(qsq_ready, b.times(1, 1))
                                st.then(nc.vector.tensor_reduce(ss[pr][:, :], heads(qtmp[pr]).rearrange("p n d g -> p n g d"), AX.X, ALU.add))
                                nc.vector.tensor_scalar_mul(ss[pr][:, :], ss[pr][:, :], 1.0 / HD).then_inc(qss_ready, 1)
                            if i == 6:
                                dve.wait_ge(qrms_ready, b.times(1, 1))
                                st.then(nc.vector.tensor_scalar_add(rms[pr][:, :], rms[pr][:, :], RMS_EPS))
                                nc.vector.reciprocal(rms[pr][:, :], rms[pr][:, :]).then_inc(qinv_ready, 1)
                        if kind == "attn_a" and t.has(1) and i >= 4:
                            b = t + 1
                            for u in (2 * (i - 4), 2 * (i - 4) + 1):
                                dve.wait_ge(q_scores_filled, b.times(8, u + 1))
                                if u == 0:
                                    need(dve, max_filled, b.times(1, 0))
                                src = ps_a[:, :, :].rearrange("p a (b t) -> p (a b) t", t=TOK)
                                nc.vector.tensor_reduce(neg_max[:, u // HG, 4 * (u % HG):4 * (u % HG) + 4].rearrange("p (c odd) -> p odd c", odd=2), src.rearrange("p (odd c) t -> p odd c t", odd=2), AX.X, ALU.max, negate=True).then_inc(maxed, 1)
                        if t.has(-1):
                            b = t + -1
                            if i in (1, 2):
                                qt = i - 1
                                dve.wait_ge(ctx_filled, b.times(2, 2 * a0 + qt + 1))
                                need(dve, ctxT_filled, b.times(1, a0))
                                src = ps_u[:, :].rearrange("p (h r) -> p h r", r=32)
                                if kind == "attn_c":
                                    st.then(nc.vector.tensor_scalar_max(den[:, qt, :], src[:, :, HD:HD + 1].rearrange("p h r -> p (h r)"), 1e-6))
                                    st.then(nc.vector.reciprocal(den[:, qt, :], den[:, qt, :]))
                                else:
                                    st.then(nc.vector.reciprocal(den[:, qt, :], src[:, :, HD:HD + 1].rearrange("p h r -> p (h r)")))
                                order = "p (d h) -> p h d" if kind == "attn_a" else "p (h d) -> p h d"
                                nc.vector.tensor_tensor(ctx_n[:, qt, :].rearrange(order, d=HD), src[:, :, 0:HD], den[:, qt, :].unsqueeze(2).to_broadcast([P, H, HD]), ALU.mult).then_inc(u_drained, 1)
                            if i == 5 and kind != "attn_a":
                                dve.wait_ge(update_filled, b.times(1, a0 + 1))
                                residual(b, ps_u[:, 0:TILES * D].rearrange("p (j d) -> p j d", j=TILES), u_drained, fill_u(k, "update", b))
                                ln_stats(dve, st, k, b)
                            if i == 7 and kind != "attn_a":
                                ln_norm(dve, k, b)

                def out_a(t):
                    if t.has(-1):
                        ln_norm(dve, k, t + -1)
                    if t.has(0):
                        dve.wait_ge(update_filled, t.times(1, 1))
                        residual(t, ps_u[:, 0:TILES * D].rearrange("p (j d) -> p j d", j=TILES), u_drained, fill_u(k, "update", t))
                        ln_stats(dve, st, k, t)

                def moe(t):
                    for v in range(8):
                        b, u = (t, v + 1) if v < 7 else (t + 1, 0)
                        if b.has(0):
                            pr = u % 2
                            dve.wait_ge(h_filled, b.times(8, 8 * o0 + u + 1))
                            hv = ps_a[:, pr, :].rearrange("p (c d) -> p c d", d=D)
                            for c in range(4):
                                ins = nc.vector.bn_stats(hst[pr][:, c, :], hv[:, c, :])
                            st.then(ins)
                        if t.has(0):
                            pr = v % 2
                            dve.wait_ge(hst_ready, t.times(8, 8 * o0 + v + 1))
                            dve.wait_ge(hrs_ready, t.times(8, 8 * o0 + v + 1))
                            need(dve, hT_filled, t.times(8, 8 * o0 + v - 1))
                            hv = ps_a[:, pr, :].rearrange("p (c d) -> p c d", d=D)
                            for c in range(4):
                                j, e = c // 2, c % 2
                                ins = nc.vector.tensor_scalar(hn[pr][:, e, j, :], hv[:, c, :], hmv[pr][:, c, 0:1], hrs[pr][:, c:c + 1], ALU.subtract, ALU.mult)
                            ins.then_inc(hn_ready, 1)
                        b, u = (t, v + 1) if v < 7 else (t + 1, 0)
                        if b.has(0):
                            pr = u % 2
                            for c in range(4):
                                ins = nc.vector.bn_aggr(hmv[pr][:, c, :], hst[pr][:, c, :])
                            ins.then_inc(hst_ready, 1)
                        if v == 2 and t.has(1):
                            b = t + 1
                            dve.wait_ge(logits_filled, b.times(1, o0 + 1))
                            nc.vector.tensor_tensor(lg[:, :, 0:E], ps_t[:, 0:TILES * E].rearrange("p (j e) -> p j e", j=TILES), row["br"][:, :].unsqueeze(1).to_broadcast([P, TILES, E]), ALU.add).then_inc(t_drained, 1)
                            dve.wait_ge(t_drained, fill_t(k, "logits", b))
                        b, u = (t, v - 1) if v else (t + -1, 7)
                        if b.has(0):
                            dve.wait_ge(gelu_ready, b.times(8, 8 * o0 + u + 1))
                            dve.wait_ge(wb_filled, b.times(8, 8 * o0 + u + 1))
                            need(dve, w2_done, b.times(8, 8 * o0 + u - 1))
                            nc.vector.tensor_tensor(ag[u % 2][:, :, :].rearrange("p e t -> p (e t)"), ps_c[:, u % 2, :], aT[u % 2][:, :, :].rearrange("p e t -> p (e t)"), ALU.mult).then_inc(gated_ready, 1)
                        if v == 2 and t.has(1):
                            for j in range(TILES):
                                ins = nc.vector.max(lg[:, j, E:E + 8], lg[:, j, 0:E])
                            st.then(ins)
                            nc.vector.tensor_tensor(lgd[:, :, :], lg[:, :, 0:18], lg[:, :, E:E + 1].to_broadcast([P, TILES, 18]), ALU.subtract).then_inc(lgd_ready, 1)
                            for j in range(TILES):
                                ins = nc.vector.max_index(lidx[:, j, :], lg[:, j, E:E + 8], lg[:, j, 0:E])
                            ins.then_inc(places_ready, 1)
                        if v == 2 and t.has(-1):
                            b = t + -1
                            dve.wait_ge(w2_done, b.times(8, 8 * o0 + 8))
                            residual(b, ps_u[:, 0:TILES * D].rearrange("p (j d) -> p j d", j=TILES), u_drained, fill_u(k, "update", b))
                            ln_stats(dve, st, k, b)
                        if v == 5 and t.has(-1):
                            ln_norm(dve, k, t + -1)
                        if v == 4 and t.has(1):
                            b = t + 1
                            dve.wait_ge(places_ready, b.times(1, o0 + 1))
                            dve.wait_ge(lge_ready, b.times(1, o0 + 1))
                            nc.vector.tensor_copy(lidf[:, :, :], lidx[:, :, 0:2])
                            st.then(nc.vector.tensor_reduce(lsum[:, :, :].rearrange("p j o -> p (j o)"), lge[:, :, 0:E], AX.X, ALU.add))
                            st.then(nc.vector.reciprocal(lsum[:, :, :], lsum[:, :, :]))
                            st.then(nc.vector.tensor_tensor(lw[:, :, :], lge[:, :, E:E + 2], lsum[:, :, :].to_broadcast([P, TILES, 2]), ALU.mult))
                            st.then(nc.vector.tensor_tensor(lwt[:, :, :], lw[:, :, 0:1], lw[:, :, 1:2], ALU.add))
                            st.then(nc.vector.tensor_scalar_max(lwt[:, :, :], lwt[:, :, :], 1e-9))
                            st.then(nc.vector.reciprocal(lwt[:, :, :], lwt[:, :, :]))
                            st.then(nc.vector.tensor_tensor(lw[:, :, :], lw[:, :, :], lwt[:, :, :].to_broadcast([P, TILES, 2]), ALU.mult))
                            for j in range(TILES):
                                for c in range(2):
                                    ins = nc.vector.tensor_scalar(gates[:, c, j, :], iota_e[:, :], lidf[:, j, c:c + 1], lw[:, j, c:c + 1], ALU.is_equal, ALU.mult)
                            st.then(ins)
                            st.then(nc.vector.tensor_tensor(gates[:, 0], gates[:, 0], gates[:, 1], ALU.add))
                            need(dve, gate_filled, b.times(1, o0))
                            st.then(nc.vector.tensor_copy(gates_b[:, 0], gates[:, 0]))
                            nc.vector.tensor_copy(gate_pack[:, :, 0:E], gates_b[:, 0])
                            st.then(nc.vector.tensor_tensor(gates[:, 1], gates[:, 0], gates_b[:, 0], ALU.subtract))
                            st.then(nc.vector.tensor_copy(gates_b[:, 1], gates[:, 1]))
                            nc.vector.tensor_copy(gate_pack[:, :, 32:32 + E], gates_b[:, 1])
                            nc.vector.tensor_tensor(gate_pack[:, :, 64:64 + E], gates[:, 1], gates_b[:, 1], ALU.subtract).then_inc(pack_ready, 1)

                def ssm(t):
                    if t.has(1):
                        b = t + 1
                        dve.wait_ge(ub_filled, b.times(1, 1))
                        need(dve, y_filled, b.times(1, -1))
                        nc.vector.tensor_tensor_scan(states[b.par][:, :], decay[:, :].to_broadcast([P, TOK]), ps_a[:, b.par, 0:TOK], 0.0, ALU.mult, ALU.add).then_inc(scanned, 1)
                    if t.has(0):
                        dve.wait_ge(y_filled, t.times(1, 1))
                        for j in range(TILES):
                            ins = nc.vector.bn_stats(yst[:, j, :], ps_b[:, t.par, j * D:(j + 1) * D])
                        st.then(ins)
                    if t.has(-1):
                        ln_norm(dve, k, t + -1)
                    if t.has(0):
                        for j in range(TILES):
                            ins = nc.vector.bn_aggr(ymv[:, j, :], yst[:, j, :])
                        ins.then_inc(yst_ready, 1)
                        dve.wait_ge(yst_ready, t.times(1, 1))
                        dve.wait_ge(yrs_ready, t.times(1, 1))
                        for j in range(TILES):
                            ins = nc.vector.tensor_scalar(yn[:, j, :], ps_b[:, t.par, j * D:(j + 1) * D], ymv[:, j, 0:1], yrs[:, j:j + 1], ALU.subtract, ALU.mult)
                        st.then(ins)
                        st.then(nc.vector.tensor_tensor(upd[:, :, :], yn[:, :, :], rows("s_gamma", TILES), ALU.mult))
                        residual(t, upd[:, :, :], None, None)
                        ln_stats(dve, st, k, t)

                def mix(t):
                    if t.has(1):
                        b = t + 1
                        dve.wait_ge(mixt_ready, b.times(1, o0 + 1))
                        need(dve, rk_filled, b.times(1, o0 - 1))
                        for i, m in enumerate(["mu_r", "mu_k"]):
                            ins = nc.vector.scalar_tensor_tensor(mix_x[b.par][:, i, :], xc(b), col[m][:, 0:1], mix_t[b.par][:, i, :], ALU.mult, ALU.add)
                        ins.then_inc(mixx_ready, 1)
                    if t.has(-1) and not last:
                        ln_norm(dve, k, t + -1)
                    if t.has(0):
                        dve.wait_ge(rexp_ready, t.times(1, o0 + 1))
                        st.then(nc.vector.tensor_scalar_add(r_one[t.par][:, :], r_exp[t.par][:, :], 1.0))
                        st.then(nc.vector.reciprocal(r_one[t.par][:, :], r_one[t.par][:, :]))
                        dve.wait_ge(o_filled, t.times(1, o0 + 1))
                        st.then(nc.vector.tensor_tensor(upd[:, :, :].rearrange("p j d -> p (j d)"), ps_b[:, t.par, 0:TOK], r_one[t.par][:, :], ALU.mult))
                        if last:
                            nc.vector.tensor_tensor(xb(t), xb(t), upd[:, :, :], ALU.add).then_inc(stats_ready, 1)
                        else:
                            residual(t, upd[:, :, :], None, None)
                            ln_stats(dve, st, k, t)

                body = {"out_a": out_a, "moe": moe, "ssm": ssm, "mix": mix}.get(kind, attn)
                per = 2 * {"attn_a": 2, "out_a": 1, "attn_b": 5, "attn_c": 5, "moe": 22, "ssm": 5, "mix": 3 if last else 5}[kind]
                f, l, lo, trips = SWEEP[kind]
                sweep(dve, st, per, body, f, l, lo, trips)

        @block.tensor
        def _(pe):
            mm = nc.tensor.matmul
            pe.wait_ge(setup_pool, 2)

            def first_norm(t):
                if t.has(0):
                    ln_transpose(pe, 0, t)
            sweep(pe, None, 0, first_norm, 0, 7, 2, 2)
            pe.wait_ge(loaded, 16 * n_loads[0])
            pe.wait_ge(setup_dve, 3)
            pe.wait_ge(setup_done, 1)
            pe.wait_ge(setup_dma, 48)

            for k in range(1, len(kinds)):
                kind = kinds[k]
                a0 = attn_no[k] * NB
                o0 = occ[k] * NB
                last = k == len(kinds) - 1

                def head(stack, b, h, rows_):
                    r0 = HEADROW * (h % 2)
                    return stack[b.par][r0:r0 + rows_, h // 2, :]

                def attn(t):
                    rows_ = STACK + 1 if kind == "attn_a" else STACK
                    wqkv = {"attn_b": "b_wqkv", "attn_c": "c_wqkv"}.get(kind)
                    if kind == "attn_a" and t.has(1):
                        b = t + 1
                        has_cur(pe, k, b)
                        need(pe, t_drained, fill_t(k, "qk", b, -1))
                        mm(ps_t[:, 0:TOK], w["a_wq"][:, :], xc(b), start=True, stop=True)
                        mm(ps_t[:, TOK:2 * TOK], w["a_wk"][:, :], xc(b), start=True, stop=True).then_inc(qk_filled, 1)
                    if kind != "attn_a" and t.has(2):
                        b = t + 2
                        has_cur(pe, k, b)
                        need(pe, t_drained, fill_t(k, "qk", b, -1))
                        for j in range(TILES):
                            ins = mm(ps_t[:, j * TOK:(j + 1) * TOK], xc(b, j), w[wqkv][:, 0:2 * D], start=True, stop=True)
                        ins.then_inc(qk_filled, 1)
                        if kind == "attn_c":
                            need(pe, u_drained, fill_u(k, "swapped", b, -1))
                            for j in range(TILES):
                                ins = mm(ps_u[:, j * TOK:(j + 1) * TOK], xc(b, j), w["c_wswap"][:, :], start=True, stop=True)
                            ins.then_inc(swapped_filled, 1)
                    if t.has(1):
                        b = t + 1
                        need(pe, u_drained, fill_u(k, "v", b, -1))
                        for j in range(TILES):
                            wv = w["a_wv"][:, :] if kind == "attn_a" else w[wqkv][:, 2 * D:3 * D]
                            ins = mm(ps_u[:, j * D:(j + 1) * D], xc(b, j), wv, start=True, stop=True)
                        ins.then_inc(v_filled, 1)
                    if kind != "attn_a" and t.has(1):
                        b = t + 1
                        pe.wait_ge(feat_ready, b.times(1, a0 - NB + 1))
                        need(pe, t_drained, fill_t(k, "feat", b, -1))
                        need(pe, parts_ready, b.times(1, a0 - 1))
                        for i in range(2):
                            for j in range(TILES):
                                ins = nc.tensor.transpose(ps_t[:, i * TOK + j * P:i * TOK + (j + 1) * P], feat[b.par][:, j, i, :], ident[:, :])
                        ins.then_inc(feat_filled, 1)

                    def pv(i):
                        hg, kt = i // 2, i % 2
                        pe.wait_ge(probs_ready, t.times(8, 8 * a0 + i + 1))
                        if i == 0:
                            need(pe, ctx_copied, t.times(1, a0))
                            pe.wait_ge(u_drained, fill_u(k, "v", t))
                        for c in range(4):
                            ins = mm(ps_c[32 * c:32 * c + 32, hg // 2, (hg % 2) * TOK:(hg % 2 + 1) * TOK], v_aug[t.par][:, kt, 4 * hg + c, :], probs[i % 4][:, 2 * (c % 2) + c // 2, :], start=(kt == 0), stop=(kt == 1))
                        ins.then_inc(pv_done, 1)

                    for i in range(8):
                        if t.has(0):
                            hg, kt = i // 2, i % 2
                            if i == 0:
                                pe.wait_ge(stack_loaded[t.par], t.half(16 * STACK_DMAS, 16 * STACK_DMAS * (a0 // 2 + 1)))
                                if kind == "attn_a":
                                    pe.wait_ge(max_loaded[t.par], t.half(32, 32))
                            bank2 = ps_b if kind == "attn_a" or i % 2 else ps_a
                            if kind == "attn_a":
                                need(pe, probs_ready, t.times(8, 8 * a0 + i))
                            else:
                                need(pe, probs_ready, t.times(8, 8 * a0 + i - 1))
                            if kind == "attn_a":
                                for part in range(3):
                                    for odd in range(2):
                                        mm(bank2[:, odd, :], ident_b[:, :], bias_k[part][:, kt, :].unsqueeze(1).to_broadcast([P, 2, TOK]), start=(part == 0), stop=False, skip_group_check=True)
                            for c in range(2):
                                for odd in range(2):
                                    h = 4 * hg + 2 * c + odd
                                    ins = mm(bank2[:, odd, c * TOK:(c + 1) * TOK], head(stack_k, t, h, rows_)[:, kt * P:(kt + 1) * P], head(stack_q, t, h, rows_), start=(kind != "attn_a"), stop=True, skip_group_check=True)
                            ins.then_inc(scores_filled, 1)
                            if i:
                                pv(i - 1)
                        if kind == "attn_a" and t.has(1) and i >= 4:
                            b = t + 1
                            for u in (2 * (i - 4), 2 * (i - 4) + 1):
                                qt, hg = u // HG, u % HG
                                if u == 0:
                                    pe.wait_ge(stack_loaded[b.par], b.half(16 * STACK_DMAS, 16 * STACK_DMAS * (a0 // 2 + 1)))
                                need(pe, maxed, b.times(8, u))
                                for odd in range(2):
                                    mm(ps_a[:, odd, :], ident_b[:, :], bias_q[:, qt, :].unsqueeze(1).to_broadcast([P, 2, TOK]), start=True, stop=False, skip_group_check=True)
                                for c in range(2):
                                    for odd in range(2):
                                        h = 4 * hg + 2 * c + odd
                                        ins = mm(ps_a[:, odd, c * TOK:(c + 1) * TOK], head(stack_q, b, h, STACK)[:, qt * P:(qt + 1) * P], head(stack_k, b, h, STACK), start=False, stop=True, skip_group_check=True)
                                ins.then_inc(q_scores_filled, 1)
                        if t.has(-1):
                            b = t + -1
                            if i in (1, 2):
                                qt = i - 1
                                pe.wait_ge(ctx_copied, b.times(1, a0 + 1))
                                need(pe, u_drained, fill_u(k, f"ctx{qt}", b, -1))
                                for g in range(HG):
                                    ins = nc.tensor.transpose(ps_u[:, g * P:(g + 1) * P], ctx_raw[:, g, qt * P:(qt + 1) * P], ident[:, :])
                                ins.then_inc(ctx_filled, 1)
                            if i == 4:
                                pe.wait_ge(u_drained, fill_u(k, "ctx1", b))
                                need(pe, t_drained, fill_t(k, "ctx", b, -1))
                                for j in range(TILES):
                                    ins = nc.tensor.transpose(ps_t[:, j * P:(j + 1) * P], ctx_n[:, j, :], ident[:, :])
                                ins.then_inc(ctxT_filled, 1)
                            if i == 5 and kind != "attn_a":
                                pe.wait_ge(t_drained, fill_t(k, "ctx", b))
                                need(pe, u_drained, fill_u(k, "update", b, -1))
                                wo = w[{"attn_b": "b_wproj", "attn_c": "c_wout"}[kind]]
                                for j in range(TILES):
                                    ins = mm(ps_u[:, j * D:(j + 1) * D], ctx_T[:, j * P:(j + 1) * P], wo[:, :], start=True, stop=True)
                                ins.then_inc(update_filled, 1)
                            if i == 7 and kind != "attn_a":
                                ln_transpose(pe, k, b)
                    if t.has(0):
                        pv(7)
                    if kind == "attn_a" and t.has(1):
                        b = t + 1
                        pe.wait_ge(maxed, b.times(8, 8))
                        need(pe, t_drained, fill_t(k, "max", b, -1))
                        for j in range(TILES):
                            ins = nc.tensor.transpose(ps_t[0:H, j * P:(j + 1) * P], neg_max[:, j, :], ident[:, :])
                        ins.then_inc(max_filled, 1)

                def out_a(t):
                    if t.has(0):
                        need(pe, u_drained, fill_u(k, "update", t, -1))
                        for j in range(TILES):
                            ins = mm(ps_u[:, j * D:(j + 1) * D], ctx_flip[:, TILES * t.off + j, :, :].rearrange("p b n -> p (b n)"), w["a_wo"][:, :], start=True, stop=True)
                        ins.then_inc(update_filled, 1)
                    if t.has(-1):
                        ln_transpose(pe, k, t + -1)

                def moe(t):
                    for v in range(8):
                        b, u = (t, v + 1) if v < 7 else (t + 1, 0)
                        if b.has(0):
                            if u == 0:
                                has_cur(pe, k, b)
                            need(pe, hn_ready, b.times(8, 8 * o0 + u - 1))
                            for j in range(TILES):
                                o = ps_a[:, u % 2, j * TOK:(j + 1) * TOK]
                                mm(o, ones3[:, :], b1_rows[:, 2 * u * D:(2 * u + 2) * D], start=True, stop=False)
                                ins = mm(o, xc(b, j), w["w1"][:, 2 * u:2 * u + 2, :].rearrange("p e d -> p (e d)"), start=False, stop=True)
                            ins.then_inc(h_filled, 1)
                        b, u = (t, v - 2) if v >= 2 else (t + -1, v + 6)
                        if b.has(0):
                            if u == 0:
                                need(pe, u_drained, fill_u(k, "update", b, -1))
                                for j in range(TILES):
                                    mm(ps_u[:, j * D:(j + 1) * D], gate_f[b.par][:, j * P:(j + 1) * P], b2_rows[:, :], start=(j == 0), stop=False, skip_group_check=True)
                            pe.wait_ge(gated_ready, b.times(8, 8 * o0 + u + 1))
                            for e in range(2):
                                for j in range(TILES):
                                    ins = mm(ps_u[:, j * D:(j + 1) * D], ag[u % 2][:, e, j * P:(j + 1) * P], w["w2"][:, 2 * u + e, :], start=False, stop=(u == 7 and e == 1), skip_group_check=True)
                            ins.then_inc(w2_done, 1)
                        if t.has(0):
                            if v == 0:
                                pe.wait_ge(t_drained, fill_t(k, "gate", t))
                            need(pe, gated_ready, t.times(8, 8 * o0 + v - 1))
                            for e in range(2):
                                ins = mm(ps_c[:, v % 2, e * TOK:(e + 1) * TOK], gate_sel[:, 2 * v + e, :], gate_b[t.par][:, :], start=True, stop=True)
                            ins.then_inc(wb_filled, 1)
                            pe.wait_ge(hn_ready, t.times(8, 8 * o0 + v + 1))
                            need(pe, gelu_ready, t.times(8, 8 * o0 + v - 1))
                            for e in range(2):
                                for j in range(TILES):
                                    ins = nc.tensor.transpose(ps_b[:, v % 2, e * TOK + j * P:e * TOK + (j + 1) * P], hn[v % 2][:, e, j, :], ident[:, :])
                            ins.then_inc(hT_filled, 1)
                        if v == 1 and t.has(1):
                            b = t + 1
                            has_cur(pe, k, b)
                            need(pe, t_drained, fill_t(k, "logits", b, -1))
                            for j in range(TILES):
                                ins = mm(ps_t[:, j * E:(j + 1) * E], xc(b, j), w["wr"][:, :], start=True, stop=True)
                            ins.then_inc(logits_filled, 1)
                        if v == 5 and t.has(1):
                            b = t + 1
                            pe.wait_ge(pack_ready, b.times(1, o0 + 1))
                            need(pe, t_drained, fill_t(k, "gate", b, -1))
                            for j in range(TILES):
                                ins = nc.tensor.transpose(ps_t[0:96, j * P:(j + 1) * P], gate_pack[:, j, :], ident[:, :])
                            ins.then_inc(gate_filled, 1)
                        if v == 6 and t.has(-1):
                            ln_transpose(pe, k, t + -1)

                def ssm(t):
                    if t.has(1):
                        b = t + 1
                        has_cur(pe, k, b)
                        need(pe, scanned, b.times(1, -1))
                        mm(ps_a[:, b.par, 0:TOK], w["s_wb"][:, :], xc(b), start=True, stop=True).then_inc(ub_filled, 1)
                    if t.has(0):
                        pe.wait_ge(scanned, t.times(1, 1))
                        need(pe, stats_ready, t.times(1, NB * ln_no[k] - 1))
                        for j in range(TILES):
                            ins = mm(ps_b[:, t.par, j * D:(j + 1) * D], states[t.par][:, j * P:(j + 1) * P], w["s_wc"][:, :], start=True, stop=True)
                        ins.then_inc(y_filled, 1)
                    if t.has(-1):
                        ln_transpose(pe, k, t + -1)

                def mix(t):
                    if t.has(0):
                        b = t
                        pe.wait_ge(mixx_ready, b.times(1, o0 + 1))
                        need(pe, rexp_ready, b.times(1, o0))
                        need(pe, krelu_ready, b.times(1, o0))
                        for j in range(TILES):
                            mm(ps_a[:, 0, j * D:(j + 1) * D], mix_x[b.par][:, 0, j * P:(j + 1) * P], w["m_wr"][:, :], start=True, stop=True)
                        mm(ps_a[:, 1, 0:TOK], w["m_wk"][:, :], mix_x[b.par][:, 1, :], start=True, stop=True).then_inc(rk_filled, 1)
                    if t.has(-1) and not last:
                        ln_transpose(pe, k, t + -1)
                    if t.has(0):
                        pe.wait_ge(ksq_ready, t.times(1, o0 + 1))
                        need(pe, stats_ready, t.times(1, NB * ln_no[k] - 1))
                        for j in range(TILES):
                            ins = mm(ps_b[:, t.par, j * D:(j + 1) * D], k_sq[t.par][:, j * P:(j + 1) * P], w["m_wv"][:, :], start=True, stop=True)
                        ins.then_inc(o_filled, 1)

                body = {"out_a": out_a, "moe": moe, "ssm": ssm, "mix": mix}.get(kind, attn)
                f, l, lo, trips = SWEEP[kind]
                if kind == "out_a":
                    pe.wait_ge(ctx_sent, 16 * SPAN * NB)
                    for t in range(f, l + 1):
                        out_a(At(None, t))
                else:
                    sweep(pe, None, 0, body, f, l, lo, trips)


def kernel(**inputs):
    import numpy as _np
    import concourse.bacc as _bacc
    from concourse import mybir as _mybir
    from concourse.bass_utils import run_bass_kernel_spmd as _run

    a = {n: _np.asarray(v) for n, v in inputs.items()}
    tb_len = a["L0_attn_a_time_bias"].shape[-1]
    pos = _np.arange(TOK)
    idx = _np.clip(pos[None, :] - pos[:, None] + tb_len // 2, 0, tb_len - 1)
    order = pos.reshape(-1, SPAN).T.reshape(-1)
    idx = idx[order][:, order]
    tb = a["L0_attn_a_time_bias"].reshape(-1)
    perm = _np.arange(D).reshape(H // 2, 2, HD).transpose(1, 2, 0).reshape(-1)
    perm_qk = _np.concatenate([perm, D + perm])
    perm_qkv = _np.concatenate([perm_qk, _np.arange(2 * D, 3 * D)])
    qk_scale = _np.stack([_np.tile(a["L0_attn_b_q_scale"], H)[perm], _np.tile(a["L0_attn_b_k_scale"], H)[perm]])
    swap = _np.arange(2 * D).reshape(2 * H, 2, HD // 2)[:, ::-1].reshape(-1)
    inv_freq = (1.0 / _np.float32(10000.0) ** (_np.arange(HD // 2, dtype=_np.float32) / _np.float32(HD // 2))).astype(_np.float32)
    freqs = (_np.arange(TOK, dtype=_np.float32)[:, None] * inv_freq[None, :]).astype(_np.float32)
    turn = _np.float32(HD ** -0.25)
    cos, sin = (_np.cos(freqs) * turn).astype(_np.float32), (_np.sin(freqs) * turn).astype(_np.float32)
    arrays = {
        "x": a["L0_attn_a_x"],
        "a_wq": a["L0_attn_a_Wq"].T[:, perm], "a_wk": a["L0_attn_a_Wk"].T[:, perm], "a_wv": a["L0_attn_a_Wv"].T, "a_wo": a["L0_attn_a_Wo"].T,
        "a_bq": a["L0_attn_a_bq"][perm], "a_bk": a["L0_attn_a_bk"][perm], "a_bv": a["L0_attn_a_bv"], "a_bo": a["L0_attn_a_bo"],
        "et": a["L0_attn_a_et_gate"].reshape(1), "is": a["L0_attn_a_is_gate"].reshape(1),
        "bias_q": tb[idx], "bias_k": tb[idx.T],
        "b_wqkv": a["L0_attn_b_Wqkv"][:, perm_qkv], "b_wproj": a["L0_attn_b_Wproj"], "b_bproj": a["L0_attn_b_bproj"],
        "qk_scale": qk_scale,
        "wr": a["L0_ffn_Wr"], "br": a["L0_ffn_br"], "w1": a["L0_ffn_W1"], "b1": a["L0_ffn_b1"],
        "g1": a["L0_ffn_g1"].T, "be1": a["L0_ffn_be1"].T, "w2": a["L0_ffn_W2"], "b2": a["L0_ffn_b2"],
        "log_a": a["L1_attn_a_log_a"], "s_wb": a["L1_attn_a_W_b"].T, "s_wc": a["L1_attn_a_W_c"].T,
        "s_gamma": a["L1_attn_a_gamma"], "s_beta": a["L1_attn_a_beta"],
        "c_wqkv": a["L1_attn_b_w_qkv"][:, perm_qkv], "c_wswap": a["L1_attn_b_w_qkv"][:, swap][:, perm_qk], "c_wout": a["L1_attn_b_w_out"],
        "m_wr": a["L1_ffn_W_r"].T, "m_wk": a["L1_ffn_W_k"].T, "m_wv": a["L1_ffn_W_v"].T,
        "mu_r": a["L1_ffn_mu_r"], "mu_k": a["L1_ffn_mu_k"],
        "rope_cos": _np.concatenate([cos, cos], axis=1), "rope_sin": _np.concatenate([-sin, sin], axis=1),
    }
    nc = _bacc.Bacc("TRN2", target_bir_lowering=False, num_devices=1)
    io, ins = {}, {}
    for name, v in arrays.items():
        v = _np.ascontiguousarray(v)
        ins["in_" + name] = v
        io[name] = nc.dram_tensor("in_" + name, v.shape, _mybir.dt.from_np(v.dtype), kind="ExternalInput").ap()
    out = nc.dram_tensor("out_x", a["L0_attn_a_x"].shape, _mybir.dt.float32, kind="ExternalOutput").ap()
    hybrid_kernel(nc, io, out)
    r = _run(nc, [ins], core_ids=[0])
    return r.results[0]["out_x"]
```

```python
from contextlib import ExitStack

import concourse.bass as bass
from concourse import mybir

P = 128
NB = 8
TOK = 256
TILES = TOK // P
D = 128
H = 16
HD = D // H
HG = 4
E = 16
PAIRS = E // 2
STACK = 6 * HD
HEADROW = 64
LN_EPS = 1e-5
RMS_EPS = 1e-8

ALU = mybir.AluOpType
ACT = mybir.ActivationFunctionType
F32 = mybir.dt.float32
BF16 = mybir.dt.bfloat16
U32 = mybir.dt.uint32
AX = mybir.AxisListType

SPAN = D // HD
STAGES = ["attn_a", "out_a", "moe", "attn_b", "moe", "ssm", "mix", "attn_c", "mix"]

Q_PART = [0, 0, 1, 1, 0, 2]
K_PART = [0, 1, 0, 1, 2, 0]


class At:

    def __init__(self, reg, off, trips=None):
        self.reg, self.off, self.trips = reg, off, trips

    def __add__(self, d):
        return At(self.reg, self.off + d, self.trips)

    @property
    def par(self):
        return self.off % 2

    @property
    def ends(self):
        if self.reg is None:
            return (self.off, self.off)
        return (2 * self.trips[0] + self.off, 2 * (self.trips[1] - 1) + self.off)

    def has(self, d=0):
        return 0 <= self.ends[0] + d and self.ends[1] + d < NB

    def times(self, k, plus=0):
        if self.reg is None:
            return k * self.off + plus
        return self.reg * (2 * k) + (k * self.off + plus)

    def half(self, k, plus=0):
        if self.reg is None:
            return k * (self.off // 2) + plus
        return self.reg * k + (k * (self.off // 2) + plus)


def need(eng, sem, n):
    if isinstance(n, int) and n <= 0:
        return
    eng.wait_ge(sem, n)


class Ledger:

    def __init__(self, uses):
        self.uses, self.base, n = uses, [], 0
        for u in uses:
            self.base.append(n)
            n += NB * len(u)

    def at(self, stage, name, b):
        uses = self.uses[stage]
        names = [n for n, _ in uses]
        j = names.index(name)
        d = uses[j][1]

        def exact(t):
            return self.base[stage] + sum(min(max(t + di + (i <= j), 0), NB) for i, (_, di) in enumerate(uses))

        lo, hi = (e - d for e in b.ends)
        if b.reg is None:
            return exact(lo)
        c = len(uses)
        plus = self.base[stage] + sum(di + (i <= j) for i, (_, di) in enumerate(uses)) - c * d
        assert c * (lo + d) + plus == exact(lo) and c * (hi + d) + plus == exact(hi), (stage, name, lo, hi)
        return b.times(c, plus)


class Steps:

    def __init__(self, eng, sem):
        self.eng, self.sem, self.n = eng, sem, 0
        self.reg = None

    def loop(self, reg, first, per):
        self.reg, self.first, self.per, self.n0 = reg, first, per, self.n

    def end(self, trips):
        assert self.n - self.n0 == self.per, f"{self.sem}: {self.n - self.n0} steps in the loop's body"
        self.n = self.n0 + self.per * trips
        self.reg = None

    def value(self):
        if self.reg is None:
            return self.n
        return self.reg * self.per + (self.n - self.first * self.per)

    def then(self, ins):
        self.n += 1
        ins.then_inc(self.sem, 1)
        self.eng.wait_ge(self.sem, self.value())


def sweep(eng, steps, per, body, first, last, lo, trips):
    for t in range(first, lo):
        body(At(None, t))
    with eng.Fori(0, trips) as i:
        if steps:
            steps.loop(i, 0, per)
        for q in range(2):
            body(At(i, lo + q, (0, trips)))
        if steps:
            steps.end(trips)
    for t in range(lo + 2 * trips, last + 1):
        body(At(None, t))


USES_T = {
    "load": [("ln", 0)],
    "attn_a": [("qk", 2), ("ctx", -1), ("max", 1)],
    "out_a": [("ln", -1)],
    "attn_b": [("qk", 2), ("feat", 1), ("ctx", -1), ("ln", -1)],
    "attn_c": [("qk", 2), ("feat", 1), ("ctx", -1), ("ln", -1)],
    "moe": [("logits", 1), ("gate", 1), ("ln", -1)],
    "ssm": [("ln", -1)],
    "mix": [("ln", -1)],
}
USES_U = {
    "load": [],
    "attn_a": [("v", 1), ("ctx0", -1), ("ctx1", -1)],
    "out_a": [("update", 0)],
    "attn_b": [("v", 1), ("ctx0", -1), ("ctx1", -1), ("update", -1)],
    "attn_c": [("swapped", 2), ("v", 1), ("ctx0", -1), ("ctx1", -1), ("update", -1)],
    "moe": [("update", 0)],
    "ssm": [],
    "mix": [],
}
SWEEP = {
    "attn_a": (-2, 8, 2, 2),
    "out_a": (0, 8, 2, 2),
    "attn_b": (-2, 8, 2, 2),
    "attn_c": (-2, 8, 2, 2),
    "moe": (-1, 8, 2, 2),
    "ssm": (-2, 8, 2, 2),
    "mix": (-2, 8, 2, 2),
}


def hybrid_kernel(nc, io, out):
    led_t = Ledger([USES_T[k] for k in ["load"] + STAGES])
    led_u = Ledger([USES_U[k] for k in ["load"] + STAGES])
    with ExitStack() as ctx:
        def sb(name, shape, dt=F32):
            return ctx.enter_context(nc.sbuf_tensor(name, shape, dt))

        def ps(name, shape, dt=F32):
            return ctx.enter_context(nc.psum_tensor(name, shape, dt))

        def sem(name):
            return ctx.enter_context(nc.semaphore(name))

        ps_a = ps("ps_a", [P, 2, 512])
        ps_b = ps("ps_b", [P, 2, 512])
        ps_c = ps("ps_c", [P, 2, 512])
        ps_t = ps("ps_t", [P, 512])
        ps_u = ps("ps_u", [P, 512])

        x = sb("x", [P, NB * TILES, D])
        xnT = sb("xnT", [P, NB * TOK])
        xcur = [sb(f"xcur{i}", [P, TOK + 1]) for i in range(2)]
        xn = [sb(f"xn{i}", [P, TILES, D]) for i in range(2)]
        stats = [sb(f"stats{i}", [P, TILES, 6]) for i in range(2)]
        mv = [sb(f"mv{i}", [P, TILES, 2]) for i in range(2)]
        var_eps = [sb(f"var_eps{i}", [P, 4]) for i in range(2)]
        rstd = [sb(f"rstd{i}", [P, TILES]) for i in range(2)]
        x_new = [sb(f"x_new{i}", [P, TILES, D]) for i in range(2)]
        ln_eps = sb("ln_eps", [P, 4])
        idle = sb("idle", [P, 2])
        half_neg = sb("half_neg", [P, 4])
        ident = sb("ident", [P, P])
        ident_b = sb("ident_b", [P, P], BF16)

        w = {}
        for name in ["a_wq", "a_wk", "a_wv", "a_wo", "b_wproj", "s_wb", "s_wc", "c_wout", "m_wr", "m_wk", "m_wv"]:
            w[name] = sb("w_" + name, [P, D])
        w["b_wqkv"] = sb("w_b_wqkv", [P, 3 * D])
        w["c_wqkv"] = sb("w_c_wqkv", [P, 3 * D])
        w["c_wswap"] = sb("w_c_wswap", [P, 2 * D])
        w["w1"] = sb("w_w1", [P, E, D])
        w["w2"] = sb("w_w2", [P, E, D])
        w["wr"] = sb("w_wr", [P, E])
        row = {}
        for name in ["a_bo", "a_bv", "b_bproj", "s_beta", "s_gamma"]:
            row[name] = sb("row_" + name, [P, D])
        row["br"] = sb("row_br", [P, E])
        row["qk_scale"] = sb("row_qk_scale", [P, 2, D])
        col = {}
        for name in ["a_bq", "a_bk", "et", "is", "log_a", "mu_r", "mu_k"]:
            col[name] = sb("col_" + name, [P, 1])
        g1 = sb("g1", [P, E])
        be1 = sb("be1", [P, E])
        b2_rows = sb("b2_rows", [96, D])
        b1_f = sb("b1_f", [E, 2, D])
        b1_part = sb("b1_part", [E, 3, D], BF16)
        b1_rows = sb("b1_rows", [3, E * D], BF16)
        ones3 = sb("ones3", [3, P], BF16)
        gate_sel = sb("gate_sel", [96, E, P], BF16)
        decay = sb("decay", [P, 1])
        mu_r1 = sb("mu_r1", [P, 1])
        mu_k1 = sb("mu_k1", [P, 1])
        sig = sb("sig", [P, 2])
        bias_q = sb("bias_q", [P, TILES, TOK], BF16)
        bias_k = [sb(f"bias_k{i}", [P, TILES, TOK], BF16) for i in range(3)]
        bias_f = sb("bias_f", [P, 2, TILES, TOK])
        rope_cos = sb("rope_cos", [P, TILES, HD])
        rope_sin = sb("rope_sin", [P, TILES, HD])
        causal = sb("causal", [P, TILES, TOK])
        bound = sb("bound", [P, 4])

        qk32 = [sb(f"qk32_{i}", [P, 2, TOK]) for i in range(2)]
        rest = [sb(f"rest_{i}", [P, 2, TOK]) for i in range(2)]
        parts = [sb(f"parts_{i}", [P, 2, 3, TOK], BF16) for i in range(2)]
        stack = [sb(f"stack{i}", [P, H // 2, 2, TOK], BF16) for i in range(2)]
        stack_q = [stack[i][:, :, 0, :] for i in range(2)]
        stack_k = [stack[i][:, :, 1, :] for i in range(2)]
        v_aug = [sb(f"v_aug{i}", [P, TILES, H, 32]) for i in range(2)]
        probs = [sb(f"probs{i}", [P, 4, TOK]) for i in range(4)]
        neg_max = sb("neg_max", [P, TILES, H])
        max_rows = sb("max_rows", [H, TOK], BF16)
        ctx_raw = sb("ctx_raw", [P, HG, TOK])
        ctx_n = sb("ctx_n", [P, TILES, D])
        ctx_T = sb("ctx_T", [P, TOK])
        ctx_flip = sb("ctx_flip", [P, H, NB, SPAN])
        den = sb("den", [P, TILES, H])
        qraw = [sb(f"qraw{i}", [P, TILES, 2, D]) for i in range(2)]
        qtmp = [sb(f"qtmp{i}", [P, TILES, 2, D]) for i in range(2)]
        feat = [sb(f"feat{i}", [P, TILES, 2, D]) for i in range(2)]
        ss = [sb(f"ss{i}", [P, 2 * TILES * H]) for i in range(2)]
        rms_inv = sb("rms_inv", [P, 2 * TILES * H])
        rms = [sb(f"rms{i}", [P, 2 * TILES * H]) for i in range(2)]

        lg = sb("lg", [P, TILES, 24])
        lgd = sb("lgd", [P, TILES, 18])
        lge = sb("lge", [P, TILES, 18])
        lidx = sb("lidx", [P, TILES, 8], U32)
        lidf = sb("lidf", [P, TILES, 2])
        lsum = sb("lsum", [P, TILES, 1])
        lw = sb("lw", [P, TILES, 2])
        lwt = sb("lwt", [P, TILES, 1])
        iota_e = sb("iota_e", [P, E])
        gates = sb("gates", [P, 3, TILES, E])
        gates_b = sb("gates_b", [P, 2, TILES, E], BF16)
        gate_pack = sb("gate_pack", [P, TILES, 96])
        gate_f = [sb(f"gate_f{i}", [96, TOK]) for i in range(2)]
        gate_b = [sb(f"gate_b{i}", [96, TOK], BF16) for i in range(2)]
        h_sq = [sb(f"h_sq{i}", [P, 4, D], BF16) for i in range(2)]
        hvar = [sb(f"hvar{i}", [P, 4]) for i in range(2)]
        hve = [sb(f"hve{i}", [P, 4]) for i in range(2)]
        hrs = [sb(f"hrs{i}", [P, 4]) for i in range(2)]
        hn = [sb(f"hn{i}", [P, 2, TILES, D]) for i in range(2)]
        aT = [sb(f"aT{i}", [P, 2, TOK]) for i in range(2)]
        ag = [sb(f"ag{i}", [P, 2, TOK]) for i in range(2)]

        states = [sb(f"states{i}", [P, TOK]) for i in range(2)]
        yst = [sb(f"yst{i}", [P, TILES, 6]) for i in range(2)]
        ymv = [sb(f"ymv{i}", [P, TILES, 2]) for i in range(2)]
        yve = [sb(f"yve{i}", [P, TILES]) for i in range(2)]
        yrs = [sb(f"yrs{i}", [P, TILES]) for i in range(2)]
        yn = sb("yn", [P, TILES, D])
        upd = [sb(f"upd{i}", [P, TILES, D]) for i in range(2)]
        mix_t = [sb(f"mix_t{i}", [P, 2, TOK]) for i in range(2)]
        mix_x = [sb(f"mix_x{i}", [P, 2, TOK]) for i in range(2)]
        r_sig = [sb(f"r_sig{i}", [P, TOK]) for i in range(2)]
        k_relu = [sb(f"k_relu{i}", [P, TOK]) for i in range(2)]
        k_sq = [sb(f"k_sq{i}", [P, TOK]) for i in range(2)]

        loaded = sem("loaded")
        x_loaded = sem("x_loaded")
        setup_pool = sem("setup_pool")
        setup_dve = sem("setup_dve")
        setup_act = sem("setup_act")
        setup_dma = sem("setup_dma")
        setup_done = sem("setup_done")
        pool_step = sem("pool_step")
        dve_step = sem("dve_step")
        act_step = sem("act_step")
        stats_ready = sem("stats_ready")
        rstd_ready = sem("rstd_ready")
        xn_ready = sem("xn_ready")
        xnT_filled = sem("xnT_filled")
        t_drained = sem("t_drained")
        u_drained = sem("u_drained")
        xcur_ready = sem("xcur_ready")
        stored = sem("stored")
        first_x = sem("first_x")
        qk_filled = sem("qk_filled")
        swapped_filled = sem("swapped_filled")
        v_filled = sem("v_filled")
        rest1_ready = sem("rest1_ready")
        high_ready = sem("high_ready")
        mid_ready = sem("mid_ready")
        parts_ready = sem("parts_ready")
        q_scores_filled = sem("q_scores_filled")
        maxed = sem("maxed")
        max_filled = sem("max_filled")
        scores_filled = sem("scores_filled")
        probs_ready = sem("probs_ready")
        pv_done = sem("pv_done")
        ctx_copied = sem("ctx_copied")
        ctx_filled = sem("ctx_filled")
        ctx_ready = sem("ctx_ready")
        ctxT_filled = sem("ctxT_filled")
        ctx_sent = sem("ctx_sent")
        update_filled = sem("update_filled")
        qsq_ready = sem("qsq_ready")
        qss_ready = sem("qss_ready")
        qrms_ready = sem("qrms_ready")
        qinv_ready = sem("qinv_ready")
        feat_ready = sem("feat_ready")
        feat_filled = sem("feat_filled")
        qz_ready = sem("qz_ready")
        qzm_ready = sem("qzm_ready")
        qexp_ready = sem("qexp_ready")
        rot_ready = sem("rot_ready")
        logits_filled = sem("logits_filled")
        places_ready = sem("places_ready")
        lgd_ready = sem("lgd_ready")
        lge_ready = sem("lge_ready")
        pack_ready = sem("pack_ready")
        gate_filled = sem("gate_filled")
        gate_f_ready = sem("gate_f_ready")
        gate_ready = sem("gate_ready")
        h_filled = sem("h_filled")
        hvar_ready = sem("hvar_ready")
        hrs_ready = sem("hrs_ready")
        hn_ready = sem("hn_ready")
        hT_filled = sem("hT_filled")
        gelu_ready = sem("gelu_ready")
        wb_filled = sem("wb_filled")
        gated_ready = sem("gated_ready")
        w2_done = sem("w2_done")
        ub_filled = sem("ub_filled")
        scanned = sem("scanned")
        y_filled = sem("y_filled")
        yst_ready = sem("yst_ready")
        yrs_ready = sem("yrs_ready")
        mixt_ready = sem("mixt_ready")
        mixx_ready = sem("mixx_ready")
        rk_filled = sem("rk_filled")
        rsig_ready = sem("rsig_ready")
        krelu_ready = sem("krelu_ready")
        ksq_ready = sem("ksq_ready")
        o_filled = sem("o_filled")
        stack_free = sem("stack_free")
        stack_loaded = [sem(f"stack_loaded{i}") for i in range(2)]
        max_loaded = [sem(f"max_loaded{i}") for i in range(2)]

        n_loads = [0]
        kinds = ["load"] + STAGES
        occ = [kinds[:n].count(k) for n, k in enumerate(kinds)]
        attn_no = [sum(k.startswith("attn") for k in kinds[:n]) for n in range(len(kinds))]
        ln_no = [sum(k != "attn_a" for k in kinds[:n]) for n in range(len(kinds) + 1)]
        cur_no = [sum(k not in ("load", "out_a") for k in kinds[:n]) for n in range(len(kinds))]

        block = ctx.enter_context(nc.Block())

        def xb(b):
            return x[:, bass.ds(b.times(TILES), TILES), :] if b.reg is not None else x[:, TILES * b.off:TILES * b.off + TILES, :]

        def xt(b, j):
            n = b.times(TILES, j)
            return x[:, bass.ds(n, 1), :].rearrange("p a d -> p (a d)") if b.reg is not None else x[:, n, :]

        def xnTb(b):
            return xnT[:, bass.ds(b.times(TOK), TOK)] if b.reg is not None else xnT[:, TOK * b.off:TOK * (b.off + 1)]

        def heads(a):
            return a[:, :, :, :].rearrange("p j i (o d g) -> p (j i o) d g", o=2, g=H // 2)

        def flat(a):
            return a[:, :, :, :].rearrange("p j i f -> p j (i f)")

        def unit(t, v, d):
            return t + (v + d) // PAIRS, (v + d) % PAIRS

        def h_bank(u):
            return (ps_a if u % 4 < 2 else ps_c)[:, u % 2, :]

        def rows(name, n):
            return row[name][:, :].unsqueeze(1).to_broadcast([P, n, D])

        def ln_stats(dve, st, k, b):
            nc.vector.bn_stats(stats[b.par][:, 0, :], x_new[b.par][:, 0, :])
            st.then(nc.vector.bn_stats(stats[b.par][:, 1, :], x_new[b.par][:, 1, :]))
            nc.vector.tensor_scalar_mul(xb(b), x_new[b.par][:, :, :], 1.0)
            for j in range(TILES):
                ins = nc.vector.bn_aggr(mv[b.par][:, j, :], stats[b.par][:, j, :])
            ins.then_inc(stats_ready, 1)

        def ln_rstd(pool, st, k, b):
            pool.wait_ge(stats_ready, b.times(1, NB * ln_no[k] + 1))
            st.then(nc.gpsimd.tensor_tensor(var_eps[b.par][:, 0:TILES], mv[b.par][:, :, 1], ln_eps[:, 0:TILES], ALU.add))
            nc.gpsimd.tensor_tensor(rstd[b.par][:, :], var_eps[b.par][:, 0:TILES], half_neg[:, 0:TILES], ALU.pow).then_inc(rstd_ready, 1)

        def ln_norm(dve, k, b):
            dve.wait_ge(stats_ready, b.times(1, NB * ln_no[k] + 1))
            dve.wait_ge(rstd_ready, b.times(1, NB * ln_no[k] + 1))
            need(dve, xnT_filled, b.times(1, NB * ln_no[k] - 1))
            for j in range(TILES):
                ins = nc.vector.tensor_scalar(xn[b.par][:, j, :], x_new[b.par][:, j, :], mv[b.par][:, j, 0:1], rstd[b.par][:, j:j + 1], ALU.subtract, ALU.mult)
            ins.then_inc(xn_ready, 1)

        def ln_transpose(pe, k, b):
            pe.wait_ge(xn_ready, b.times(1, NB * ln_no[k] + 1))
            need(pe, t_drained, fill_t(k, "ln", b, -1))
            for j in range(TILES):
                ins = nc.tensor.transpose(ps_t[:, j * P:(j + 1) * P], xn[b.par][:, j, :], ident[:, :])
            ins.then_inc(xnT_filled, 1)

        def ln_copy(act, k, b):
            act.wait_ge(xnT_filled, b.times(1, NB * ln_no[k] + 1))
            nc.scalar.copy(xnTb(b), ps_t[:, 0:TOK]).then_inc(t_drained, 1)

        def fill_t(k, name, b, d=0):
            return led_t.at(k, name, b) + d

        def fill_u(k, name, b, d=0):
            return led_u.at(k, name, b) + d

        def take_batch(pool, k, b, add):
            last, n = {"attn_a": (v_filled, 1), "attn_b": (v_filled, 1), "attn_c": (v_filled, 1),
                       "moe": (h_filled, PAIRS), "ssm": (ub_filled, 1), "mix": (mixx_ready, 1)}[kinds[k]]
            before = attn_no[k] if kinds[k].startswith("attn") else occ[k]
            need(pool, last, b.times(n, n * (NB * before - 1)))
            if kinds[k] == "mix":
                need(pool, mixt_ready, b.times(1, NB * before - 1))
            if add:
                nc.gpsimd.tensor_tensor(xb(b), xb(b), rows(add, TILES), ALU.add)
            if kinds[k] == "attn_a":
                nc.gpsimd.tensor_copy(xcur[b.par][:, 1:TOK + 1].rearrange("p (m n) -> p n m", m=SPAN), xnTb(b).rearrange("p (n m) -> p n m", m=SPAN)).then_inc(xcur_ready, 1)
            else:
                nc.gpsimd.tensor_copy(xcur[b.par][:, 1:TOK + 1], xnTb(b)).then_inc(xcur_ready, 1)

        def xc(b, j=None):
            if j is None:
                return xcur[b.par][:, 1:TOK + 1]
            return xcur[b.par][:, 1 + j * P:1 + (j + 1) * P]

        def has_cur(eng, k, b):
            eng.wait_ge(xcur_ready, b.times(1, NB * cur_no[k] + 1))

        @block.sync
        def _(sp):
            for t in range(4):
                sp.dma_start(x[:, 4 * t:4 * t + 4, :], io["x"].rearrange("b (t p) d -> p (b t) d", p=P)[:, 4 * t:4 * t + 4, :]).then_inc(x_loaded, 16)

            def load(dst, src):
                sp.dma_start(dst, src).then_inc(loaded, 16)
                n_loads[0] += 1

            for name in ["a_wq", "a_wk", "a_wv", "a_wo", "b_wproj", "b_wqkv", "c_wqkv", "c_wswap", "c_wout", "s_wb", "s_wc", "m_wr", "m_wk", "m_wv", "wr"]:
                load(w[name][:, :], io[name])
            for name in ["w1", "w2"]:
                load(w[name][:, :, :], io[name].rearrange("e c h -> c e h"))
            for name in ["a_bo", "a_bv", "b_bproj", "s_beta", "s_gamma", "br"]:
                load(row[name][:, :], io[name].unsqueeze(0).to_broadcast([P, io[name].shape[0]]))
            load(row["qk_scale"][:, :, :], io["qk_scale"].unsqueeze(0).to_broadcast([P, 2, D]))
            for name in ["a_bq", "a_bk", "log_a", "mu_r", "mu_k"]:
                load(col[name][:, :], io[name].unsqueeze(1))
            for name in ["et", "is"]:
                load(col[name][:, :], io[name].unsqueeze(1).to_broadcast([P, 1]))
            load(g1[:, :], io["g1"])
            load(be1[:, :], io["be1"])
            load(b1_f[:, 0, :], io["b1"])
            load(bias_f[:, 0, :, :], io["bias_q"].rearrange("(t p) k -> p t k", p=P))
            load(bias_f[:, 1, :, :], io["bias_k"].rearrange("(t p) k -> p t k", p=P))
            load(rope_cos[:, :, :], io["rope_cos"].rearrange("(t p) d -> p t d", p=P))
            load(rope_sin[:, :, :], io["rope_sin"].rearrange("(t p) d -> p t d", p=P))
            sp.wait_ge(setup_pool, 1)
            for i in range(3):
                load(b2_rows[32 * i:32 * i + E, :], io["b2"])
            sp.wait_ge(setup_dve, 3)
            for i in range(3):
                sp.dma_start(b1_rows[i:i + 1, :], b1_part[:, i, :]).then_inc(setup_dma, 16)

            for k in range(1, len(kinds)):
                if not kinds[k].startswith("attn"):
                    continue
                a0 = attn_no[k] * NB

                def body(t):
                    if t.has(1):
                        b = t + 1
                        if kinds[k] == "attn_a":
                            sp.wait_ge(stack_free, b.times(1, 1))
                        else:
                            sp.wait_ge(parts_ready, b.times(1, a0 + 1))
                        for slot in range(6):
                            first, second = Q_PART[slot], 3 + K_PART[slot]
                            for odd in range(2):
                                r0 = HEADROW * odd + HD * slot
                                src = parts[b.par][HEADROW * odd:HEADROW * (odd + 1), :, :, :].rearrange("p i a t -> p (i a) t")[:, first:second + 1:second - first, :]
                                sp.dma_start(stack[b.par][r0:r0 + HD, :, :, :], src).then_inc(stack_loaded[b.par], 16)
                    if t.has(-1) and kinds[k] == "attn_a":
                        b = t + -1
                        sp.wait_ge(t_drained, fill_t(k, "ctx", b))
                        for m in range(SPAN):
                            dst = ctx_flip[HD * m:HD * (m + 1), :, bass.ds(b.times(1), 1), :] if b.reg is not None else ctx_flip[HD * m:HD * (m + 1), :, b.off, :]
                            sp.dma_start(dst, ctx_T[:, SPAN * m:SPAN * (m + 1)]).then_inc(ctx_sent, 16)
                    if t.has(1):
                        b = t + 1
                        if kinds[k] == "attn_a":
                            sp.wait_ge(t_drained, fill_t(k, "max", b))
                            for odd in range(2):
                                src = max_rows[odd:H:2, :]
                                r0 = HEADROW * odd + STACK
                                sp.dma_start(stack_q[b.par][r0:r0 + 1, :, :], src).then_inc(max_loaded[b.par], 16)
                f, l, lo, trips = SWEEP[kinds[k]]
                sweep(sp, None, 0, body, f, l, lo, trips)

            out_v = out.rearrange("b (t p) d -> p (b t) d", p=P)
            for b in range(NB):
                sp.wait_ge(stats_ready, NB * (ln_no[-1] - 1) + b + 1)
                sp.dma_start(out_v[:, TILES * b:TILES * (b + 1), :], x[:, TILES * b:TILES * (b + 1), :]).then_inc(stored, 16)
            sp.wait_ge(stored, 16 * NB)

        STACK_DMAS = 12

        @block.gpsimd
        def _(pool):
            st = Steps(pool, pool_step)
            nc.gpsimd.memset(b2_rows[:, :], 0.0).then_inc(setup_pool, 1)
            nc.gpsimd.memset(half_neg[:, :], -0.5)
            nc.gpsimd.memset(ln_eps[:, :], LN_EPS)
            st.then(nc.gpsimd.memset(ident[:, :], 0.0))
            nc.gpsimd.affine_select(out=ident[:, :], in_=ident[:, :], compare_op=ALU.not_equal, fill=1.0, base=0, pattern=[[-1, P]], channel_multiplier=1).then_inc(setup_pool, 1)

            def first_norm(t):
                if t.has(0):
                    ln_rstd(pool, st, 0, t)
            sweep(pool, st, 2, first_norm, 0, 7, 2, 2)


            nc.gpsimd.memset(ones3[:, :], 1.0)
            nc.gpsimd.memset(gate_sel[:, :, :], 0.0)
            nc.gpsimd.memset(causal[:, :, :], 1.0)
            nc.gpsimd.iota(iota_e[:, :], pattern=[[1, E]], base=0, channel_multiplier=0, allow_small_or_imprecise_dtypes=True)
            for i in range(2):
                nc.gpsimd.memset(xcur[i][:, 0:1], 0.0)
                nc.gpsimd.memset(v_aug[i][:, :, :, :], 0.0)
                nc.gpsimd.memset(stack[i][:, :, :, :], 1.0)
            st.then(nc.gpsimd.memset(gate_pack[:, :, :], 0.0))
            for i in range(2):
                nc.gpsimd.memset(v_aug[i][:, :, :, HD:HD + 1], 1.0)
            for j in range(TILES):
                nc.gpsimd.affine_select(out=causal[:, j, :], in_=causal[:, j, :], compare_op=ALU.is_ge, fill=0.0, base=-P * j, pattern=[[1, TOK]], channel_multiplier=-1)
            for i in range(3):
                st.then(nc.gpsimd.affine_select(out=gate_sel[:, :, :], in_=gate_sel[:, :, :], compare_op=ALU.not_equal, fill=1.0, base=-32 * i, pattern=[[-1, E], [0, P]], channel_multiplier=1))
            pool.wait_ge(setup_pool, 2)
            nc.gpsimd.tensor_copy(ident_b[:, :], ident[:, :]).then_inc(setup_pool, 1)

            for k in range(1, len(kinds)):
                kind = kinds[k]
                a0 = attn_no[k] * NB
                o0 = occ[k] * NB
                last = k == len(kinds) - 1

                def split(b):
                    pr = b.par
                    pool.wait_ge(high_ready, b.times(1, a0 + 1))
                    nc.gpsimd.tensor_tensor(rest[pr][:, :, :], qk32[pr][:, :, :], parts[pr][:, :, 0, :], ALU.subtract).then_inc(rest1_ready, 1)
                    pool.wait_ge(mid_ready, b.times(1, a0 + 1))
                    if kind != "attn_a":
                        need(pool, scores_filled, b.times(8, 8 * (a0 - 1)))
                    nc.gpsimd.tensor_tensor(parts[pr][:, :, 2, :], rest[pr][:, :, :], parts[pr][:, :, 1, :], ALU.subtract).then_inc(parts_ready, 1)

                def attn(t):
                    if t.has(1) and kind == "attn_a":
                        pool.wait_ge(parts_ready, (t + 1).times(1, 1))
                        need(pool, scores_filled, (t + 1).times(8, -8))
                        nc.gpsimd.tensor_tensor(idle[:, 0:1], ln_eps[:, 0:1], ln_eps[:, 1:2], ALU.add).then_inc(stack_free, 1)
                    if t.has(2):
                        take_batch(pool, k, t + 2, {"attn_a": "a_bo", "attn_b": "b_bproj"}.get(kind))
                    if kind == "attn_b" and t.has(2):
                        b = t + 2
                        pr = b.par
                        pool.wait_ge(t_drained, fill_t(k, "qk", b))
                        nc.gpsimd.tensor_tensor(qtmp[pr][:, :, :, :], qraw[pr][:, :, :, :], qraw[pr][:, :, :, :], ALU.mult).then_inc(qsq_ready, 1)
                    lead = 2 if kind == "attn_a" else 1
                    if t.has(lead):
                        split(t + lead)
                    if kind == "attn_b" and t.has(2):
                        b = t + 2
                        pr = b.par
                        pool.wait_ge(qinv_ready, b.times(1, 1))
                        need(pool, feat_filled, b.times(1, -1))
                        inv = rms[pr][:, :].rearrange("p (n g) -> p n g", g=H // 2).unsqueeze(2).to_broadcast([P, 4 * TILES, HD, H // 2])
                        st.then(nc.gpsimd.tensor_tensor(heads(qtmp[pr]), heads(qraw[pr]), inv, ALU.mult))
                        nc.gpsimd.tensor_tensor(flat(feat[pr]), flat(qtmp[pr]), row["qk_scale"][:, :, :].rearrange("p i f -> p (i f)").unsqueeze(1).to_broadcast([P, TILES, 2 * D]), ALU.mult).then_inc(feat_ready, 1)
                    if t.has(-1) and kind != "attn_a":
                        ln_rstd(pool, st, k, t + -1)
                    if kind == "attn_c" and t.has(2):
                        b = t + 2
                        pr = b.par
                        pool.wait_ge(rot_ready, b.times(1, 1))
                        need(pool, feat_filled, b.times(1, NB - 1))
                        nc.gpsimd.tensor_tensor(flat(qraw[pr]), flat(qraw[pr]), flat(qtmp[pr]), ALU.add).then_inc(qz_ready, 1)
                        pool.wait_ge(qzm_ready, b.times(1, 1))
                        st.then(nc.gpsimd.tensor_tensor(flat(qraw[pr]), flat(qraw[pr]), flat(qtmp[pr]), ALU.add))
                        pool.wait_ge(qexp_ready, b.times(1, 1))
                        nc.gpsimd.tensor_tensor(flat(feat[pr]), flat(feat[pr]), flat(qraw[pr]), ALU.add).then_inc(feat_ready, 1)
                def out_a(t):
                    if t.has(0):
                        ln_rstd(pool, st, k, t)

                def moe(t):
                    if t.has(1):
                        take_batch(pool, k, t + 1, None)
                    for v in range(8):
                        b, u = unit(t, v, 1)
                        if b.has(0):
                            pr = u % 2
                            pool.wait_ge(hvar_ready, b.times(8, 8 * o0 + u + 1))
                            need(pool, hn_ready, b.times(8, 8 * o0 + u - 1))
                            st.then(nc.gpsimd.tensor_tensor(hve[pr][:, :], hvar[pr][:, :], ln_eps[:, :], ALU.add))
                            nc.gpsimd.tensor_tensor(hrs[pr][:, :], hve[pr][:, :], half_neg[:, :], ALU.pow).then_inc(hrs_ready, 1)
                        if v == 3 and t.has(-1):
                            ln_rstd(pool, st, k, t + -1)

                def ssm(t):
                    if t.has(2):
                        take_batch(pool, k, t + 2, "s_beta")
                    if t.has(0):
                        ln_rstd(pool, st, k, t)
                    if t.has(1):
                        b = t + 1
                        pool.wait_ge(yst_ready, b.times(1, 1))
                        st.then(nc.gpsimd.tensor_tensor(yve[b.par][:, :], ymv[b.par][:, :, 1], ln_eps[:, 0:TILES], ALU.add))
                        nc.gpsimd.tensor_tensor(yrs[b.par][:, :], yve[b.par][:, :], half_neg[:, 0:TILES], ALU.pow).then_inc(yrs_ready, 1)

                def mix(t):
                    if t.has(2):
                        b = t + 2
                        take_batch(pool, k, b, None)
                        has_cur(pool, k, b)
                        need(pool, mixx_ready, b.times(1, o0 - 1))
                        for i, m in enumerate([mu_r1, mu_k1]):
                            ins = nc.gpsimd.tensor_tensor(mix_t[b.par][:, i, :], xcur[b.par][:, 0:TOK], m[:, :].to_broadcast([P, TOK]), ALU.mult)
                        ins.then_inc(mixt_ready, 1)
                    if t.has(1):
                        b = t + 1
                        pool.wait_ge(krelu_ready, b.times(1, o0 + 1))
                        need(pool, o_filled, b.times(1, o0 - 1))
                        nc.gpsimd.tensor_tensor(k_sq[b.par][:, :], k_relu[b.par][:, :], k_relu[b.par][:, :], ALU.mult).then_inc(ksq_ready, 1)
                    if t.has(0) and not last:
                        ln_rstd(pool, st, k, t)

                if k == 1:
                    pool.wait_ge(loaded, 16 * n_loads[0])
                    pool.wait_ge(setup_done, 1)
                if kind != "out_a":
                    pool.wait_ge(t_drained, fill_t(k - 1, "ln", At(None, NB - 1)))
                body = {"out_a": out_a, "moe": moe, "ssm": ssm, "mix": mix}.get(kind, attn)
                per = {"attn_a": 0, "out_a": 2, "attn_b": 4, "attn_c": 4, "moe": 18, "ssm": 4, "mix": 2 * (not last)}[kind]
                f, l, lo, trips = SWEEP[kind]
                sweep(pool, st, per, body, f, l, lo, trips)

        @block.scalar
        def _(act):
            def first_norm(t):
                if t.has(0):
                    ln_copy(act, 0, t)
            sweep(act, None, 0, first_norm, 0, 7, 2, 2)
            act.wait_ge(loaded, 16 * n_loads[0])
            nc.scalar.activation(decay[:, :], col["log_a"][:, :], ACT.Exp)
            nc.scalar.activation(sig[:, 0:1], col["et"][:, :], ACT.Exp, scale=-1.0).then_inc(setup_act, 1)

            for k in range(1, len(kinds)):
                kind = kinds[k]
                a0 = attn_no[k] * NB
                o0 = occ[k] * NB
                last = k == len(kinds) - 1

                def high(b):
                    pr = b.par
                    if kind != "attn_a":
                        act.wait_ge(feat_filled, b.times(1, a0 - NB + 1))
                        nc.scalar.copy(qk32[pr][:, :, :], ps_t[:, :].rearrange("p (i t) -> p i t", i=2)).then_inc(t_drained, 1)
                        act.wait_ge(t_drained, fill_t(k, "feat", b))
                    else:
                        act.wait_ge(t_drained, fill_t(k, "qk", b))
                    need(act, stack_loaded[pr], b.half(16 * STACK_DMAS, 16 * STACK_DMAS * (a0 // 2)))
                    nc.scalar.copy(parts[pr][:, :, 0, :], qk32[pr][:, :, :]).then_inc(high_ready, 1)

                def mid(b):
                    act.wait_ge(rest1_ready, b.times(1, a0 + 1))
                    nc.scalar.copy(parts[b.par][:, :, 1, :], rest[b.par][:, :, :]).then_inc(mid_ready, 1)

                def attn(t):
                    if t.has(-1):
                        b = t + -1
                        act.wait_ge(pv_done, b.times(8, 8 * a0 + 8))
                        need(act, ctx_filled, b.times(2, 2 * a0))
                        nc.scalar.copy(ctx_raw[:, :, :], ps_c[:, :, :].rearrange("p a (b t) -> p (a b) t", t=TOK)).then_inc(ctx_copied, 1)
                    if kind == "attn_b" and t.has(2):
                        b = t + 2
                        act.wait_ge(qk_filled, b.times(1, a0 + 1))
                        need(act, feat_ready, b.times(1, -1))
                        nc.scalar.copy(qraw[b.par][:, :, :, :].rearrange("p j i d -> p (j i d)"), ps_t[:, :]).then_inc(t_drained, 1)
                    if kind != "attn_a" and t.has(1):
                        high(t + 1)
                    for i in range(8):
                        if t.has(0) and kind != "attn_c":
                            act.wait_ge(scores_filled, t.times(8, 8 * a0 + i + 1))
                            need(act, pv_done, t.times(8, 8 * a0 + i - 3))
                            src = (ps_b if kind == "attn_a" or i % 2 else ps_a)[:, :, :].rearrange("p a (b t) -> p (a b) t", t=TOK)
                            if kind == "attn_a":
                                ins = nc.scalar.activation(probs[i % 4][:, :, :], src, ACT.Exp)
                            else:
                                ins = nc.scalar.activation(probs[i % 4][:, :, :], src, ACT.Exp, bias=bound[:, 3:4])
                            ins.then_inc(probs_ready, 1)
                        if kind == "attn_a" and t.has(2):
                            if i == 1:
                                high(t + 2)
                            if i == 3:
                                mid(t + 2)
                        if kind != "attn_a" and t.has(1) and i == 1:
                            mid(t + 1)
                        if kind == "attn_b" and t.has(2) and i == 2:
                            b = t + 2
                            act.wait_ge(qss_ready, b.times(1, 1))
                            nc.scalar.activation(rms[b.par][:, :], ss[b.par][:, :], ACT.Sqrt, scale=1.0 / HD).then_inc(qrms_ready, 1)
                        if kind == "attn_c" and t.has(2) and i == 5:
                            b = t + 2
                            act.wait_ge(qz_ready, b.times(1, 1))
                            nc.scalar.activation(flat(qtmp[b.par]), flat(qraw[b.par]), ACT.Relu, scale=-1.0).then_inc(qzm_ready, 1)
                            act.wait_ge(qzm_ready, b.times(1, 1))
                            nc.scalar.activation(flat(feat[b.par]), flat(qtmp[b.par]), ACT.Exp, scale=-1.0).then_inc(qexp_ready, 1)
                        if t.has(-1):
                            b = t + -1
                            if i == 4:
                                act.wait_ge(ctxT_filled, b.times(1, a0 + 1))
                                if kind == "attn_a":
                                    need(act, ctx_sent, b.times(16 * SPAN, 0))
                                else:
                                    need(act, update_filled, b.times(1, a0))
                                nc.scalar.copy(ctx_T[:, :], ps_t[:, 0:TOK]).then_inc(t_drained, 1)
                            if i == 7 and kind != "attn_a":
                                ln_copy(act, k, b)
                    if kind == "attn_a" and t.has(1):
                        b = t + 1
                        act.wait_ge(max_filled, b.times(1, 1))
                        for pr in range(2):
                            if pr != b.par:
                                need(act, max_loaded[pr], (b + -1).half(32, 32))
                        nc.scalar.copy(max_rows[:, :], ps_t[0:H, 0:TOK]).then_inc(t_drained, 1)

                def out_a(t):
                    if t.has(-1):
                        ln_copy(act, k, t + -1)

                def moe(t):
                    for v in range(8):
                        b, u = unit(t, v, 2)
                        if b.has(0):
                            act.wait_ge(h_filled, b.times(8, 8 * o0 + u + 1))
                            need(act, hrs_ready, b.times(8, 8 * o0 + u - 1))
                            hv = h_bank(u).rearrange("p (c d) -> p c d", d=D)
                            for c in range(4):
                                ins = nc.scalar.activation(h_sq[u % 2][:, c, :], hv[:, c, :], ACT.Square, scale=float(D ** -0.5), accum_out=hvar[u % 2][:, c:c + 1])
                            ins.then_inc(hvar_ready, 1)
                        if t.has(0):
                            act.wait_ge(hT_filled, t.times(8, 8 * o0 + v + 1))
                            need(act, gated_ready, t.times(8, 8 * o0 + v - 1))
                            for e in range(2):
                                ex = 2 * v + e
                                ins = nc.scalar.activation(aT[v % 2][:, e, :], ps_b[:, 0, e * TOK:(e + 1) * TOK], ACT.Gelu, bias=be1[:, ex:ex + 1], scale=g1[:, ex:ex + 1])
                            ins.then_inc(gelu_ready, 1)
                        if t.has(1):
                            b = t + 1
                            if v == 3:
                                act.wait_ge(lgd_ready, b.times(1, o0 + 1))
                                nc.scalar.activation(lge[:, :, :], lgd[:, :, :], ACT.Exp).then_inc(lge_ready, 1)
                            if v == 5:
                                act.wait_ge(gate_filled, b.times(1, o0 + 1))
                                nc.scalar.copy(gate_f[b.par][:, :], ps_t[0:96, 0:TOK])
                                nc.scalar.copy(gate_b[b.par][:, :], ps_t[0:96, 0:TOK]).then_inc(t_drained, 1)
                        if v == 6 and t.has(-1):
                            ln_copy(act, k, t + -1)

                def ssm(t):
                    if t.has(-1):
                        ln_copy(act, k, t + -1)

                def mix(t):
                    if t.has(1):
                        b = t + 1
                        act.wait_ge(rk_filled, b.times(1, o0 + 1))
                        need(act, o_filled, b.times(1, o0 - 1))
                        nc.scalar.activation(k_relu[b.par][:, :], ps_a[:, 1, 0:TOK], ACT.Relu).then_inc(krelu_ready, 1)
                        nc.scalar.activation(r_sig[b.par][:, :], ps_a[:, 0, 0:TOK], ACT.Sigmoid).then_inc(rsig_ready, 1)
                    if t.has(-1) and not last:
                        ln_copy(act, k, t + -1)

                body = {"out_a": out_a, "moe": moe, "ssm": ssm, "mix": mix}.get(kind, attn)
                f, l, lo, trips = SWEEP[kind]
                sweep(act, None, 0, body, f, l, lo, trips)

        @block.vector
        def _(dve):
            st = Steps(dve, dve_step)

            def first_norm(t):
                if t.has(0):
                    need(dve, xn_ready, t.times(1, -1))
                    nc.vector.tensor_scalar_mul(x_new[t.par][:, :, :], xb(t), 1.0).then_inc(first_x, 1)
                    dve.wait_ge(first_x, t.times(1, 1))
                    ln_stats(dve, st, 0, t)
                if t.has(-1):
                    ln_norm(dve, 0, t + -1)
            dve.wait_ge(x_loaded, 64)
            sweep(dve, st, 2, first_norm, 0, 8, 2, 2)

            dve.wait_ge(loaded, 16 * n_loads[0])
            for dst, m in ((mu_r1, col["mu_r"]), (mu_k1, col["mu_k"])):
                ins = nc.vector.tensor_scalar(dst[:, :], m[:, :], -1.0, 1.0, ALU.mult, ALU.add)
            ins.then_inc(setup_dve, 1)
            dve.wait_ge(setup_act, 1)
            st.then(nc.vector.tensor_scalar_add(sig[:, 1:2], sig[:, 0:1], 1.0))
            st.then(nc.vector.reciprocal(sig[:, 0:1], sig[:, 1:2]))
            st.then(nc.vector.tensor_scalar(bias_f[:, :, :, :], bias_f[:, :, :, :], sig[:, 0:1], col["is"][:, 0:1], ALU.mult, ALU.add))
            nc.vector.tensor_copy(bias_q[:, :, :], bias_f[:, 0, :, :])
            st.then(nc.vector.tensor_copy(bias_k[0][:, :, :], bias_f[:, 1, :, :]))
            st.then(nc.vector.tensor_tensor(bias_f[:, 0, :, :], bias_f[:, 1, :, :], bias_k[0][:, :, :], ALU.subtract))
            st.then(nc.vector.tensor_copy(bias_k[1][:, :, :], bias_f[:, 0, :, :]))
            nc.vector.tensor_tensor(bias_k[2][:, :, :], bias_f[:, 0, :, :], bias_k[1][:, :, :], ALU.subtract).then_inc(setup_dve, 1)
            w1_mean = upd[0][:, 0, 0:E]
            st.then(nc.vector.tensor_reduce(w1_mean, w["w1"][:, :, :], AX.X, ALU.add))
            st.then(nc.vector.tensor_scalar_mul(w1_mean, w1_mean, 1.0 / D))
            st.then(nc.vector.tensor_tensor(w["w1"][:, :, :], w["w1"][:, :, :], w1_mean.unsqueeze(2).to_broadcast([P, E, D]), ALU.subtract))
            b1_mean = upd[0][0:E, 0, E:E + 1]
            st.then(nc.vector.tensor_reduce(b1_mean, b1_f[:, 0, :], AX.X, ALU.add))
            st.then(nc.vector.tensor_scalar_mul(b1_mean, b1_mean, 1.0 / D))
            st.then(nc.vector.tensor_scalar(b1_f[:, 0, :], b1_f[:, 0, :], b1_mean, None, ALU.subtract))
            st.then(nc.vector.tensor_copy(b1_part[:, 0, :], b1_f[:, 0, :]))
            st.then(nc.vector.tensor_tensor(b1_f[:, 1, :], b1_f[:, 0, :], b1_part[:, 0, :], ALU.subtract))
            st.then(nc.vector.tensor_copy(b1_part[:, 1, :], b1_f[:, 1, :]))
            nc.vector.tensor_tensor(b1_part[:, 2, :], b1_f[:, 1, :], b1_part[:, 1, :], ALU.subtract).then_inc(setup_dve, 1)
            prod = upd[0][:, 0, :]
            st.then(nc.vector.tensor_tensor(prod, row["qk_scale"][:, 0, :], row["qk_scale"][:, 1, :], ALU.mult))
            st.then(nc.vector.tensor_reduce(bound[:, 0:1], prod, AX.X, ALU.max, apply_absolute_value=True))
            nc.vector.tensor_scalar_mul(bound[:, 3:4], bound[:, 0:1], -float(HD ** 0.5))
            st.then(nc.vector.tensor_scalar_mul(row["qk_scale"][:, 0, :], row["qk_scale"][:, 0, :], float(HD ** -0.5)))
            nc.vector.tensor_copy(bound[:, 1:2], bound[:, 0:1]).then_inc(setup_done, 1)

            for k in range(1, len(kinds)):
                kind = kinds[k]
                a0 = attn_no[k] * NB
                o0 = occ[k] * NB
                last = k == len(kinds) - 1

                def residual(b, upd_ap, sem_, value):
                    ins = nc.vector.tensor_tensor(x_new[b.par][:, :, :], xb(b), upd_ap, ALU.add)
                    if sem_ is None:
                        st.then(ins)
                    else:
                        ins.then_inc(sem_, 1)
                        dve.wait_ge(sem_, value)

                def attn(t):
                    if t.has(2) and kind == "attn_a":
                        b = t + 2
                        pr = b.par
                        dve.wait_ge(qk_filled, b.times(1, a0 + 1))
                        need(dve, parts_ready, b.times(1, a0 - 1))
                        nc.vector.tensor_scalar(qk32[pr][:, 0, :], ps_t[:, 0:TOK], col["a_bq"][:, 0:1], float(HD ** -0.5), ALU.add, ALU.mult)
                        nc.vector.tensor_scalar(qk32[pr][:, 1, :], ps_t[:, TOK:2 * TOK], col["a_bk"][:, 0:1], None, ALU.add).then_inc(t_drained, 1)
                    if t.has(2) and kind == "attn_c":
                        b = t + 2
                        pr = b.par
                        for src, sm, n_, tab, dst, done in ((ps_t, qk_filled, a0 + 1, rope_cos, qraw, t_drained), (ps_u, swapped_filled, 1, rope_sin, qtmp, u_drained)):
                            dve.wait_ge(sm, b.times(1, n_))
                            need(dve, feat_ready, b.times(1, NB - 1))
                            for j in range(TILES):
                                tb = tab[:, j, :].unsqueeze(1).unsqueeze(3).to_broadcast([P, 4, HD, H // 2])
                                ins = nc.vector.tensor_tensor(heads(dst[pr])[:, 4 * j:4 * j + 4], src[:, j * TOK:(j + 1) * TOK].rearrange("p (n d g) -> p n d g", d=HD, g=H // 2), tb, ALU.mult)
                            ins.then_inc(done, 1)
                        nc.vector.tensor_copy(bound[:, 2:3], bound[:, 0:1]).then_inc(rot_ready, 1)
                    if t.has(1):
                        b = t + 1
                        dve.wait_ge(v_filled, b.times(1, a0 + 1))
                        need(dve, pv_done, b.times(8, 8 * (a0 - 1)))
                        dst = v_aug[b.par][:, :, :, 0:HD]
                        src = ps_u[:, 0:TILES * D].rearrange("p (j h d) -> p j h d", j=TILES, d=HD)
                        if kind == "attn_a":
                            bv = row["a_bv"][:, :].rearrange("p (h d) -> p h d", d=HD)
                            for j in range(TILES):
                                ins = nc.vector.tensor_tensor(dst[:, j], src[:, j], bv, ALU.add)
                            ins.then_inc(u_drained, 1)
                        else:
                            for j in range(TILES):
                                ins = nc.vector.tensor_copy(dst[:, j], src[:, j])
                            ins.then_inc(u_drained, 1)
                    for i in range(8):
                        if kind == "attn_c" and t.has(0):
                            dve.wait_ge(scores_filled, t.times(8, 8 * a0 + i + 1))
                            need(dve, pv_done, t.times(8, 8 * a0 + i - 3))
                            src = (ps_b if i % 2 else ps_a)[:, :, :].rearrange("p a (b t) -> p (a b) t", t=TOK)
                            m = causal[:, i % 2, :].unsqueeze(1).to_broadcast([P, 4, TOK])
                            nc.vector.tensor_tensor(probs[i % 4][:, :, :], src, m, ALU.mult).then_inc(probs_ready, 1)
                        if kind == "attn_b" and t.has(2):
                            b = t + 2
                            pr = b.par
                            if i == 1:
                                dve.wait_ge(qsq_ready, b.times(1, 1))
                                nc.vector.tensor_reduce(ss[pr][:, :], heads(qtmp[pr]).rearrange("p n d g -> p n g d"), AX.X, ALU.add).then_inc(qss_ready, 1)
                            if i == 3:
                                dve.wait_ge(qrms_ready, b.times(1, 1))
                                st.then(nc.vector.tensor_scalar_max(rms[pr][:, :], rms[pr][:, :], 1e-30))
                                st.then(nc.vector.reciprocal(rms_inv[:, :], rms[pr][:, :]))
                                st.then(nc.vector.scalar_tensor_tensor(rms_inv[:, :], ss[pr][:, :], 1.0 / HD, rms_inv[:, :], ALU.mult, ALU.mult))
                                st.then(nc.vector.tensor_tensor(rms[pr][:, :], rms[pr][:, :], rms_inv[:, :], ALU.add))
                                st.then(nc.vector.tensor_scalar(rms[pr][:, :], rms[pr][:, :], 0.5, RMS_EPS, ALU.mult, ALU.add))
                                nc.vector.reciprocal(rms[pr][:, :], rms[pr][:, :]).then_inc(qinv_ready, 1)
                        if kind == "attn_a" and t.has(1) and i >= 4:
                            b = t + 1
                            for n in range(4 * (i - 4), 4 * (i - 4) + 4):
                                u, odd = n // 2, n % 2
                                dve.wait_ge(q_scores_filled, b.times(16, n + 1))
                                if n == 0:
                                    need(dve, max_filled, b.times(1, 0))
                                dst = neg_max[:, u // HG, 4 * (u % HG):4 * (u % HG) + 4].rearrange("p (c odd) -> p odd c", odd=2)[:, odd]
                                nc.vector.tensor_reduce(dst, ps_a[:, odd, :].rearrange("p (c t) -> p c t", t=TOK), AX.X, ALU.max, negate=True).then_inc(maxed, 1)
                        if t.has(-1):
                            b = t + -1
                            if i in (1, 2):
                                qt = i - 1
                                dve.wait_ge(ctx_filled, b.times(2, 2 * a0 + qt + 1))
                                need(dve, ctxT_filled, b.times(1, a0))
                                src = ps_u[:, :].rearrange("p (h r) -> p h r", r=32)
                                if kind == "attn_c":
                                    st.then(nc.vector.tensor_scalar_max(den[:, qt, :], src[:, :, HD:HD + 1].rearrange("p h r -> p (h r)"), 1e-6))
                                    st.then(nc.vector.reciprocal(den[:, qt, :], den[:, qt, :]))
                                else:
                                    st.then(nc.vector.reciprocal(den[:, qt, :], src[:, :, HD:HD + 1].rearrange("p h r -> p (h r)")))
                                order = "p (d h) -> p h d" if kind == "attn_a" else "p (h d) -> p h d"
                                nc.vector.tensor_tensor(ctx_n[:, qt, :].rearrange(order, d=HD), src[:, :, 0:HD], den[:, qt, :].unsqueeze(2).to_broadcast([P, H, HD]), ALU.mult).then_inc(u_drained, 1)
                            if i == 5 and kind != "attn_a":
                                dve.wait_ge(update_filled, b.times(1, a0 + 1))
                                residual(b, ps_u[:, 0:TILES * D].rearrange("p (j d) -> p j d", j=TILES), u_drained, fill_u(k, "update", b))
                                ln_stats(dve, st, k, b)
                            if i == 7 and kind != "attn_a":
                                ln_norm(dve, k, b)

                def out_a(t):
                    if t.has(-1):
                        ln_norm(dve, k, t + -1)
                    if t.has(0):
                        dve.wait_ge(update_filled, t.times(1, 1))
                        residual(t, ps_u[:, 0:TILES * D].rearrange("p (j d) -> p j d", j=TILES), u_drained, fill_u(k, "update", t))
                        ln_stats(dve, st, k, t)

                def moe(t):
                    for v in range(8):
                        if t.has(0):
                            pr = v % 2
                            dve.wait_ge(hrs_ready, t.times(8, 8 * o0 + v + 1))
                            need(dve, hT_filled, t.times(8, 8 * o0 + v - 1))
                            hv = h_bank(v).rearrange("p (j e d) -> p e j d", j=TILES, d=D)
                            rs = hrs[pr][:, :].rearrange("p (j e) -> p e j", j=TILES).unsqueeze(3).to_broadcast([P, 2, TILES, D])
                            nc.vector.tensor_tensor(hn[pr][:, :, :, :], hv, rs, ALU.mult).then_inc(hn_ready, 1)
                        if v == 2 and t.has(1):
                            b = t + 1
                            dve.wait_ge(logits_filled, b.times(1, o0 + 1))
                            nc.vector.tensor_tensor(lg[:, :, 0:E], ps_t[:, 0:TILES * E].rearrange("p (j e) -> p j e", j=TILES), row["br"][:, :].unsqueeze(1).to_broadcast([P, TILES, E]), ALU.add).then_inc(t_drained, 1)
                            dve.wait_ge(t_drained, fill_t(k, "logits", b))
                        b, u = unit(t, v, -1)
                        if b.has(0):
                            dve.wait_ge(gelu_ready, b.times(8, 8 * o0 + u + 1))
                            dve.wait_ge(wb_filled, b.times(8, 8 * o0 + u + 1))
                            need(dve, w2_done, b.times(8, 8 * o0 + u - 1))
                            nc.vector.tensor_tensor(ag[u % 2][:, :, :].rearrange("p e t -> p (e t)"), ps_b[:, 1, :], aT[u % 2][:, :, :].rearrange("p e t -> p (e t)"), ALU.mult).then_inc(gated_ready, 1)
                        if v == 2 and t.has(1):
                            for j in range(TILES):
                                ins = nc.vector.max(lg[:, j, E:E + 8], lg[:, j, 0:E])
                            st.then(ins)
                            nc.vector.tensor_tensor(lgd[:, :, :], lg[:, :, 0:18], lg[:, :, E:E + 1].to_broadcast([P, TILES, 18]), ALU.subtract).then_inc(lgd_ready, 1)
                            for j in range(TILES):
                                ins = nc.vector.max_index(lidx[:, j, :], lg[:, j, E:E + 8], lg[:, j, 0:E])
                            ins.then_inc(places_ready, 1)
                        if v == 2 and t.has(-1):
                            b = t + -1
                            dve.wait_ge(w2_done, b.times(8, 8 * o0 + 8))
                            residual(b, ps_u[:, 0:TILES * D].rearrange("p (j d) -> p j d", j=TILES), u_drained, fill_u(k, "update", b))
                            ln_stats(dve, st, k, b)
                        if v == 5 and t.has(-1):
                            ln_norm(dve, k, t + -1)
                        if v == 4 and t.has(1):
                            b = t + 1
                            dve.wait_ge(places_ready, b.times(1, o0 + 1))
                            dve.wait_ge(lge_ready, b.times(1, o0 + 1))
                            nc.vector.tensor_copy(lidf[:, :, :], lidx[:, :, 0:2])
                            st.then(nc.vector.tensor_reduce(lsum[:, :, :].rearrange("p j o -> p (j o)"), lge[:, :, 0:E], AX.X, ALU.add))
                            st.then(nc.vector.reciprocal(lsum[:, :, :], lsum[:, :, :]))
                            st.then(nc.vector.tensor_tensor(lw[:, :, :], lge[:, :, E:E + 2], lsum[:, :, :].to_broadcast([P, TILES, 2]), ALU.mult))
                            st.then(nc.vector.tensor_tensor(lwt[:, :, :], lw[:, :, 0:1], lw[:, :, 1:2], ALU.add))
                            st.then(nc.vector.tensor_scalar_max(lwt[:, :, :], lwt[:, :, :], 1e-9))
                            st.then(nc.vector.reciprocal(lwt[:, :, :], lwt[:, :, :]))
                            st.then(nc.vector.tensor_tensor(lw[:, :, :], lw[:, :, :], lwt[:, :, :].to_broadcast([P, TILES, 2]), ALU.mult))
                            for j in range(TILES):
                                for c in range(2):
                                    ins = nc.vector.tensor_scalar(gates[:, c, j, :], iota_e[:, :], lidf[:, j, c:c + 1], lw[:, j, c:c + 1], ALU.is_equal, ALU.mult)
                            st.then(ins)
                            st.then(nc.vector.tensor_tensor(gates[:, 0], gates[:, 0], gates[:, 1], ALU.add))
                            need(dve, gate_filled, b.times(1, o0))
                            st.then(nc.vector.tensor_copy(gates_b[:, 0], gates[:, 0]))
                            nc.vector.tensor_copy(gate_pack[:, :, 0:E], gates_b[:, 0])
                            st.then(nc.vector.tensor_tensor(gates[:, 1], gates[:, 0], gates_b[:, 0], ALU.subtract))
                            st.then(nc.vector.tensor_copy(gates_b[:, 1], gates[:, 1]))
                            nc.vector.tensor_copy(gate_pack[:, :, 32:32 + E], gates_b[:, 1])
                            nc.vector.tensor_tensor(gate_pack[:, :, 64:64 + E], gates[:, 1], gates_b[:, 1], ALU.subtract).then_inc(pack_ready, 1)

                def ssm(t):
                    if t.has(0):
                        dve.wait_ge(yst_ready, t.times(1, 1))
                        dve.wait_ge(yrs_ready, t.times(1, 1))
                        for j in range(TILES):
                            ins = nc.vector.tensor_scalar(yn[:, j, :], ps_b[:, t.par, j * D:(j + 1) * D], ymv[t.par][:, j, 0:1], yrs[t.par][:, j:j + 1], ALU.subtract, ALU.mult)
                        st.then(ins)
                        st.then(nc.vector.tensor_tensor(upd[t.par][:, :, :], yn[:, :, :], rows("s_gamma", TILES), ALU.mult))
                        residual(t, upd[t.par][:, :, :], None, None)
                        ln_stats(dve, st, k, t)
                    if t.has(-1):
                        ln_norm(dve, k, t + -1)
                    if t.has(1):
                        b = t + 1
                        dve.wait_ge(y_filled, b.times(1, 1))
                        for j in range(TILES):
                            ins = nc.vector.bn_stats(yst[b.par][:, j, :], ps_b[:, b.par, j * D:(j + 1) * D])
                        st.then(ins)
                    if t.has(2):
                        b = t + 2
                        dve.wait_ge(ub_filled, b.times(1, 1))
                        need(dve, y_filled, b.times(1, -1))
                        nc.vector.tensor_tensor_scan(states[b.par][:, :], decay[:, :].to_broadcast([P, TOK]), ps_a[:, b.par, 0:TOK], 0.0, ALU.mult, ALU.add).then_inc(scanned, 1)
                    if t.has(1):
                        b = t + 1
                        for j in range(TILES):
                            ins = nc.vector.bn_aggr(ymv[b.par][:, j, :], yst[b.par][:, j, :])
                        ins.then_inc(yst_ready, 1)

                def mix(t):
                    if t.has(-1) and not last:
                        ln_norm(dve, k, t + -1)
                    if t.has(0):
                        dve.wait_ge(rsig_ready, t.times(1, o0 + 1))
                        dve.wait_ge(o_filled, t.times(1, o0 + 1))
                        st.then(nc.vector.tensor_tensor(upd[t.par][:, :, :].rearrange("p j d -> p (j d)"), ps_b[:, t.par, 0:TOK], r_sig[t.par][:, :], ALU.mult))
                        if last:
                            nc.vector.tensor_tensor(xb(t), xb(t), upd[t.par][:, :, :], ALU.add).then_inc(stats_ready, 1)
                        else:
                            residual(t, upd[t.par][:, :, :], None, None)
                            ln_stats(dve, st, k, t)
                    if t.has(2):
                        b = t + 2
                        dve.wait_ge(mixt_ready, b.times(1, o0 + 1))
                        need(dve, rk_filled, b.times(1, o0 - 1))
                        for i, m in enumerate(["mu_r", "mu_k"]):
                            ins = nc.vector.scalar_tensor_tensor(mix_x[b.par][:, i, :], xc(b), col[m][:, 0:1], mix_t[b.par][:, i, :], ALU.mult, ALU.add)
                        ins.then_inc(mixx_ready, 1)

                body = {"out_a": out_a, "moe": moe, "ssm": ssm, "mix": mix}.get(kind, attn)
                per = 2 * {"attn_a": 2, "out_a": 1, "attn_b": 8, "attn_c": 5, "moe": 14, "ssm": 5, "mix": 1 if last else 3}[kind]
                f, l, lo, trips = SWEEP[kind]
                sweep(dve, st, per, body, f, l, lo, trips)

        @block.tensor
        def _(pe):
            mm = nc.tensor.matmul
            pe.wait_ge(setup_pool, 2)

            def first_norm(t):
                if t.has(0):
                    ln_transpose(pe, 0, t)
            sweep(pe, None, 0, first_norm, 0, 7, 2, 2)
            pe.wait_ge(loaded, 16 * n_loads[0])
            pe.wait_ge(setup_dve, 3)
            pe.wait_ge(setup_done, 1)
            pe.wait_ge(setup_dma, 48)
            pe.wait_ge(setup_pool, 3)

            for k in range(1, len(kinds)):
                kind = kinds[k]
                a0 = attn_no[k] * NB
                o0 = occ[k] * NB
                last = k == len(kinds) - 1

                def head(stack, b, h, rows_):
                    r0 = HEADROW * (h % 2)
                    return stack[b.par][r0:r0 + rows_, h // 2, :]

                def attn(t):
                    rows_ = STACK + 1 if kind == "attn_a" else STACK
                    wqkv = {"attn_b": "b_wqkv", "attn_c": "c_wqkv"}.get(kind)
                    if kind == "attn_a" and t.has(2):
                        b = t + 2
                        has_cur(pe, k, b)
                        need(pe, t_drained, fill_t(k, "qk", b, -1))
                        mm(ps_t[:, 0:TOK], w["a_wq"][:, :], xc(b), start=True, stop=True)
                        mm(ps_t[:, TOK:2 * TOK], w["a_wk"][:, :], xc(b), start=True, stop=True).then_inc(qk_filled, 1)
                    if kind != "attn_a" and t.has(2):
                        b = t + 2
                        has_cur(pe, k, b)
                        need(pe, t_drained, fill_t(k, "qk", b, -1))
                        for j in range(TILES):
                            ins = mm(ps_t[:, j * TOK:(j + 1) * TOK], xc(b, j), w[wqkv][:, 0:2 * D], start=True, stop=True)
                        ins.then_inc(qk_filled, 1)
                        if kind == "attn_c":
                            need(pe, u_drained, fill_u(k, "swapped", b, -1))
                            for j in range(TILES):
                                ins = mm(ps_u[:, j * TOK:(j + 1) * TOK], xc(b, j), w["c_wswap"][:, :], start=True, stop=True)
                            ins.then_inc(swapped_filled, 1)
                    if t.has(1):
                        b = t + 1
                        need(pe, u_drained, fill_u(k, "v", b, -1))
                        for j in range(TILES):
                            wv = w["a_wv"][:, :] if kind == "attn_a" else w[wqkv][:, 2 * D:3 * D]
                            ins = mm(ps_u[:, j * D:(j + 1) * D], xc(b, j), wv, start=True, stop=True)
                        ins.then_inc(v_filled, 1)
                    if kind != "attn_a" and t.has(1):
                        b = t + 1
                        pe.wait_ge(feat_ready, b.times(1, a0 - NB + 1))
                        need(pe, t_drained, fill_t(k, "feat", b, -1))
                        need(pe, parts_ready, b.times(1, a0 - 1))
                        for i in range(2):
                            for j in range(TILES):
                                ins = nc.tensor.transpose(ps_t[:, i * TOK + j * P:i * TOK + (j + 1) * P], feat[b.par][:, j, i, :], ident[:, :])
                        ins.then_inc(feat_filled, 1)

                    def pv(i):
                        hg, kt = i // 2, i % 2
                        pe.wait_ge(probs_ready, t.times(8, 8 * a0 + i + 1))
                        if i == 0:
                            need(pe, ctx_copied, t.times(1, a0))
                            pe.wait_ge(u_drained, fill_u(k, "v", t))
                        for c in range(4):
                            ins = mm(ps_c[32 * c:32 * c + 32, hg // 2, (hg % 2) * TOK:(hg % 2 + 1) * TOK], v_aug[t.par][:, kt, 4 * hg + c, :], probs[i % 4][:, 2 * (c % 2) + c // 2, :], start=(kt == 0), stop=(kt == 1))
                        ins.then_inc(pv_done, 1)

                    def query_scores(b, first):
                        for n in range(first, first + 2):
                            qt, hg, odd = n // (2 * HG), n // 2 % HG, n % 2
                            if n == 0:
                                pe.wait_ge(stack_loaded[b.par], b.half(16 * STACK_DMAS, 16 * STACK_DMAS * (a0 // 2 + 1)))
                            need(pe, maxed, b.times(16, n - 1))
                            mm(ps_a[:, odd, :], ident_b[:, :], bias_q[:, qt, :].unsqueeze(1).to_broadcast([P, 2, TOK]), start=True, stop=False, skip_group_check=True)
                            for c in range(2):
                                h = 4 * hg + 2 * c + odd
                                ins = mm(ps_a[:, odd, c * TOK:(c + 1) * TOK], head(stack_q, b, h, STACK)[:, qt * P:(qt + 1) * P], head(stack_k, b, h, STACK), start=False, stop=True, skip_group_check=True)
                            ins.then_inc(q_scores_filled, 1)

                    for i in range(8):
                        if t.has(0):
                            hg, kt = i // 2, i % 2
                            if i == 0:
                                pe.wait_ge(stack_loaded[t.par], t.half(16 * STACK_DMAS, 16 * STACK_DMAS * (a0 // 2 + 1)))
                                if kind == "attn_a":
                                    pe.wait_ge(max_loaded[t.par], t.half(32, 32))
                            bank2 = ps_b if kind == "attn_a" or i % 2 else ps_a
                            if kind == "attn_a":
                                need(pe, probs_ready, t.times(8, 8 * a0 + i))
                            else:
                                need(pe, probs_ready, t.times(8, 8 * a0 + i - 1))
                            if kind == "attn_a":
                                for part in range(3):
                                    for odd in range(2):
                                        mm(bank2[:, odd, :], ident_b[:, :], bias_k[part][:, kt, :].unsqueeze(1).to_broadcast([P, 2, TOK]), start=(part == 0), stop=False, skip_group_check=True)
                            for c in range(2):
                                for odd in range(2):
                                    h = 4 * hg + 2 * c + odd
                                    ins = mm(bank2[:, odd, c * TOK:(c + 1) * TOK], head(stack_k, t, h, rows_)[:, kt * P:(kt + 1) * P], head(stack_q, t, h, rows_), start=(kind != "attn_a"), stop=True, skip_group_check=True)
                            ins.then_inc(scores_filled, 1)
                        if kind == "attn_a" and t.has(1) and i >= 4:
                            query_scores(t + 1, 4 * (i - 4))
                        if t.has(0) and i:
                            pv(i - 1)
                        if kind == "attn_a" and t.has(1) and i >= 4:
                            query_scores(t + 1, 4 * (i - 4) + 2)
                        if t.has(-1):
                            b = t + -1
                            if i in (1, 2):
                                qt = i - 1
                                pe.wait_ge(ctx_copied, b.times(1, a0 + 1))
                                need(pe, u_drained, fill_u(k, f"ctx{qt}", b, -1))
                                for g in range(HG):
                                    ins = nc.tensor.transpose(ps_u[:, g * P:(g + 1) * P], ctx_raw[:, g, qt * P:(qt + 1) * P], ident[:, :])
                                ins.then_inc(ctx_filled, 1)
                            if i == 4:
                                pe.wait_ge(u_drained, fill_u(k, "ctx1", b))
                                need(pe, t_drained, fill_t(k, "ctx", b, -1))
                                for j in range(TILES):
                                    ins = nc.tensor.transpose(ps_t[:, j * P:(j + 1) * P], ctx_n[:, j, :], ident[:, :])
                                ins.then_inc(ctxT_filled, 1)
                            if i == 5 and kind != "attn_a":
                                pe.wait_ge(t_drained, fill_t(k, "ctx", b))
                                need(pe, u_drained, fill_u(k, "update", b, -1))
                                wo = w[{"attn_b": "b_wproj", "attn_c": "c_wout"}[kind]]
                                for j in range(TILES):
                                    ins = mm(ps_u[:, j * D:(j + 1) * D], ctx_T[:, j * P:(j + 1) * P], wo[:, :], start=True, stop=True)
                                ins.then_inc(update_filled, 1)
                            if i == 7 and kind != "attn_a":
                                ln_transpose(pe, k, b)
                    if t.has(0):
                        pv(7)
                    if kind == "attn_a" and t.has(1):
                        b = t + 1
                        pe.wait_ge(maxed, b.times(16, 16))
                        need(pe, t_drained, fill_t(k, "max", b, -1))
                        for j in range(TILES):
                            ins = nc.tensor.transpose(ps_t[0:H, j * P:(j + 1) * P], neg_max[:, j, :], ident[:, :])
                        ins.then_inc(max_filled, 1)

                def out_a(t):
                    if t.has(0):
                        need(pe, u_drained, fill_u(k, "update", t, -1))
                        for j in range(TILES):
                            ins = mm(ps_u[:, j * D:(j + 1) * D], ctx_flip[:, TILES * t.off + j, :, :].rearrange("p b n -> p (b n)"), w["a_wo"][:, :], start=True, stop=True)
                        ins.then_inc(update_filled, 1)
                    if t.has(-1):
                        ln_transpose(pe, k, t + -1)

                def moe(t):
                    for v in range(8):
                        b, u = unit(t, v, 2)
                        if b.has(0):
                            if u == 0:
                                has_cur(pe, k, b)
                            need(pe, hn_ready, b.times(8, 8 * o0 + u - 3))
                            for j in range(TILES):
                                o = h_bank(u)[:, j * TOK:(j + 1) * TOK]
                                mm(o, ones3[:, :], b1_rows[:, 2 * u * D:(2 * u + 2) * D], start=True, stop=False)
                                ins = mm(o, xc(b, j), w["w1"][:, 2 * u:2 * u + 2, :].rearrange("p e d -> p (e d)"), start=False, stop=True)
                            ins.then_inc(h_filled, 1)
                        b, u = unit(t, v, -2)
                        if b.has(0):
                            if u == 0:
                                need(pe, u_drained, fill_u(k, "update", b, -1))
                                for j in range(TILES):
                                    mm(ps_u[:, j * D:(j + 1) * D], gate_f[b.par][:, j * P:(j + 1) * P], b2_rows[:, :], start=(j == 0), stop=False, skip_group_check=True)
                            pe.wait_ge(gated_ready, b.times(8, 8 * o0 + u + 1))
                            for e in range(2):
                                for j in range(TILES):
                                    ins = mm(ps_u[:, j * D:(j + 1) * D], ag[u % 2][:, e, j * P:(j + 1) * P], w["w2"][:, 2 * u + e, :], start=False, stop=(u == 7 and e == 1), skip_group_check=True)
                            ins.then_inc(w2_done, 1)
                        if t.has(0):
                            pe.wait_ge(hn_ready, t.times(8, 8 * o0 + v + 1))
                            need(pe, gelu_ready, t.times(8, 8 * o0 + v))
                            for e in range(2):
                                for j in range(TILES):
                                    ins = nc.tensor.transpose(ps_b[:, 0, e * TOK + j * P:e * TOK + (j + 1) * P], hn[v % 2][:, e, j, :], ident[:, :])
                            ins.then_inc(hT_filled, 1)
                            if v == 0:
                                pe.wait_ge(t_drained, fill_t(k, "gate", t))
                            need(pe, gated_ready, t.times(8, 8 * o0 + v))
                            for e in range(2):
                                ins = mm(ps_b[:, 1, e * TOK:(e + 1) * TOK], gate_sel[:, 2 * v + e, :], gate_b[t.par][:, :], start=True, stop=True)
                            ins.then_inc(wb_filled, 1)
                        if v == 1 and t.has(1):
                            b = t + 1
                            has_cur(pe, k, b)
                            need(pe, t_drained, fill_t(k, "logits", b, -1))
                            for j in range(TILES):
                                ins = mm(ps_t[:, j * E:(j + 1) * E], xc(b, j), w["wr"][:, :], start=True, stop=True)
                            ins.then_inc(logits_filled, 1)
                        if v == 5 and t.has(1):
                            b = t + 1
                            pe.wait_ge(pack_ready, b.times(1, o0 + 1))
                            need(pe, t_drained, fill_t(k, "gate", b, -1))
                            for j in range(TILES):
                                ins = nc.tensor.transpose(ps_t[0:96, j * P:(j + 1) * P], gate_pack[:, j, :], ident[:, :])
                            ins.then_inc(gate_filled, 1)
                        if v == 6 and t.has(-1):
                            ln_transpose(pe, k, t + -1)

                def ssm(t):
                    if t.has(1):
                        b = t + 1
                        pe.wait_ge(scanned, b.times(1, 1))
                        need(pe, stats_ready, b.times(1, NB * ln_no[k] - 1))
                        for j in range(TILES):
                            ins = mm(ps_b[:, b.par, j * D:(j + 1) * D], states[b.par][:, j * P:(j + 1) * P], w["s_wc"][:, :], start=True, stop=True)
                        ins.then_inc(y_filled, 1)
                    if t.has(2):
                        b = t + 2
                        has_cur(pe, k, b)
                        need(pe, scanned, b.times(1, -1))
                        mm(ps_a[:, b.par, 0:TOK], w["s_wb"][:, :], xc(b), start=True, stop=True).then_inc(ub_filled, 1)
                    if t.has(-1):
                        ln_transpose(pe, k, t + -1)

                def mix(t):
                    if t.has(0):
                        pe.wait_ge(ksq_ready, t.times(1, o0 + 1))
                        need(pe, stats_ready, t.times(1, NB * ln_no[k] - 1))
                        for j in range(TILES):
                            ins = mm(ps_b[:, t.par, j * D:(j + 1) * D], k_sq[t.par][:, j * P:(j + 1) * P], w["m_wv"][:, :], start=True, stop=True)
                        ins.then_inc(o_filled, 1)
                    if t.has(1):
                        b = t + 1
                        pe.wait_ge(mixx_ready, b.times(1, o0 + 1))
                        need(pe, rsig_ready, b.times(1, o0))
                        need(pe, krelu_ready, b.times(1, o0))
                        for j in range(TILES):
                            mm(ps_a[:, 0, j * D:(j + 1) * D], mix_x[b.par][:, 0, j * P:(j + 1) * P], w["m_wr"][:, :], start=True, stop=True)
                        mm(ps_a[:, 1, 0:TOK], w["m_wk"][:, :], mix_x[b.par][:, 1, :], start=True, stop=True).then_inc(rk_filled, 1)
                    if t.has(-1) and not last:
                        ln_transpose(pe, k, t + -1)

                body = {"out_a": out_a, "moe": moe, "ssm": ssm, "mix": mix}.get(kind, attn)
                f, l, lo, trips = SWEEP[kind]
                if kind == "out_a":
                    pe.wait_ge(ctx_sent, 16 * SPAN * NB)
                    for t in range(f, l + 1):
                        out_a(At(None, t))
                else:
                    sweep(pe, None, 0, body, f, l, lo, trips)


def kernel(**inputs):
    import numpy as _np
    import concourse.bacc as _bacc
    from concourse import mybir as _mybir
    from concourse.bass_utils import run_bass_kernel_spmd as _run

    a = {n: _np.asarray(v) for n, v in inputs.items()}
    tb_len = a["L0_attn_a_time_bias"].shape[-1]
    pos = _np.arange(TOK)
    idx = _np.clip(pos[None, :] - pos[:, None] + tb_len // 2, 0, tb_len - 1)
    order = pos.reshape(-1, SPAN).T.reshape(-1)
    idx = idx[order][:, order]
    tb = a["L0_attn_a_time_bias"].reshape(-1)
    perm = _np.arange(D).reshape(H // 2, 2, HD).transpose(1, 2, 0).reshape(-1)
    perm_qk = _np.concatenate([perm, D + perm])
    perm_qkv = _np.concatenate([perm_qk, _np.arange(2 * D, 3 * D)])
    qk_scale = _np.stack([_np.tile(a["L0_attn_b_q_scale"], H)[perm], _np.tile(a["L0_attn_b_k_scale"], H)[perm]])
    swap = _np.arange(2 * D).reshape(2 * H, 2, HD // 2)[:, ::-1].reshape(-1)
    inv_freq = (1.0 / _np.float32(10000.0) ** (_np.arange(HD // 2, dtype=_np.float32) / _np.float32(HD // 2))).astype(_np.float32)
    freqs = (_np.arange(TOK, dtype=_np.float32)[:, None] * inv_freq[None, :]).astype(_np.float32)
    turn = _np.float32(HD ** -0.25)
    cos, sin = (_np.cos(freqs) * turn).astype(_np.float32), (_np.sin(freqs) * turn).astype(_np.float32)
    arrays = {
        "x": a["L0_attn_a_x"],
        "a_wq": a["L0_attn_a_Wq"].T[:, perm], "a_wk": a["L0_attn_a_Wk"].T[:, perm], "a_wv": a["L0_attn_a_Wv"].T, "a_wo": a["L0_attn_a_Wo"].T,
        "a_bq": a["L0_attn_a_bq"][perm], "a_bk": a["L0_attn_a_bk"][perm], "a_bv": a["L0_attn_a_bv"], "a_bo": a["L0_attn_a_bo"],
        "et": a["L0_attn_a_et_gate"].reshape(1), "is": a["L0_attn_a_is_gate"].reshape(1),
        "bias_q": tb[idx], "bias_k": tb[idx.T],
        "b_wqkv": a["L0_attn_b_Wqkv"][:, perm_qkv], "b_wproj": a["L0_attn_b_Wproj"], "b_bproj": a["L0_attn_b_bproj"],
        "qk_scale": qk_scale,
        "wr": a["L0_ffn_Wr"], "br": a["L0_ffn_br"], "w1": a["L0_ffn_W1"], "b1": a["L0_ffn_b1"],
        "g1": a["L0_ffn_g1"].T, "be1": a["L0_ffn_be1"].T, "w2": a["L0_ffn_W2"], "b2": a["L0_ffn_b2"],
        "log_a": a["L1_attn_a_log_a"], "s_wb": a["L1_attn_a_W_b"].T, "s_wc": a["L1_attn_a_W_c"].T,
        "s_gamma": a["L1_attn_a_gamma"], "s_beta": a["L1_attn_a_beta"],
        "c_wqkv": a["L1_attn_b_w_qkv"][:, perm_qkv], "c_wswap": a["L1_attn_b_w_qkv"][:, swap][:, perm_qk], "c_wout": a["L1_attn_b_w_out"],
        "m_wr": a["L1_ffn_W_r"].T, "m_wk": a["L1_ffn_W_k"].T, "m_wv": a["L1_ffn_W_v"].T,
        "mu_r": a["L1_ffn_mu_r"], "mu_k": a["L1_ffn_mu_k"],
        "rope_cos": _np.concatenate([cos, cos], axis=1), "rope_sin": _np.concatenate([-sin, sin], axis=1),
    }
    nc = _bacc.Bacc("TRN2", target_bir_lowering=False, num_devices=1)
    io, ins = {}, {}
    for name, v in arrays.items():
        v = _np.ascontiguousarray(v)
        ins["in_" + name] = v
        io[name] = nc.dram_tensor("in_" + name, v.shape, _mybir.dt.from_np(v.dtype), kind="ExternalInput").ap()
    out = nc.dram_tensor("out_x", a["L0_attn_a_x"].shape, _mybir.dt.float32, kind="ExternalOutput").ap()
    hybrid_kernel(nc, io, out)
    r = _run(nc, [ins], core_ids=[0])
    return r.results[0]["out_x"]
```

```python
import math
from contextlib import ExitStack

import concourse.bass as bass
from concourse import mybir

P = 128
NB = 8
TOK = 256
TILES = TOK // P
D = 128
H = 16
HD = D // H
HG = 4
E = 16
PAIRS = E // 2
SLOTS = 8
STACK = SLOTS * HD
SCALE = 1024.0
LN_EPS = 1e-5
RMS_EPS = 1e-8

ALU = mybir.AluOpType
ACT = mybir.ActivationFunctionType
F32 = mybir.dt.float32
BF16 = mybir.dt.bfloat16
F16 = mybir.dt.float16
U32 = mybir.dt.uint32
AX = mybir.AxisListType

SPAN = D // HD
STAGES = ["attn_a", "out_a", "moe", "attn_b", "moe", "ssm", "mix", "attn_c", "mix"]

Q_PART = [0, 0, 1, 1, 0, 2]
K_PART = [0, 1, 0, 1, 2, 0]


class At:

    def __init__(self, reg, off, trips=None):
        self.reg, self.off, self.trips = reg, off, trips

    def __add__(self, d):
        return At(self.reg, self.off + d, self.trips)

    @property
    def par(self):
        return self.off % 2

    @property
    def ends(self):
        if self.reg is None:
            return (self.off, self.off)
        return (2 * self.trips[0] + self.off, 2 * (self.trips[1] - 1) + self.off)

    def has(self, d=0):
        return 0 <= self.ends[0] + d and self.ends[1] + d < NB

    def times(self, k, plus=0):
        if self.reg is None:
            return k * self.off + plus
        return self.reg * (2 * k) + (k * self.off + plus)

    def half(self, k, plus=0):
        if self.reg is None:
            return k * (self.off // 2) + plus
        return self.reg * k + (k * (self.off // 2) + plus)


def need(eng, sem, n):
    if isinstance(n, int) and n <= 0:
        return
    eng.wait_ge(sem, n)


class Ledger:

    def __init__(self, uses):
        self.uses, self.base, n = uses, [], 0
        for u in uses:
            self.base.append(n)
            n += NB * len(u)

    def at(self, stage, name, b):
        uses = self.uses[stage]
        names = [n for n, _ in uses]
        j = names.index(name)
        d = uses[j][1]

        def exact(t):
            return self.base[stage] + sum(min(max(t + di + (i <= j), 0), NB) for i, (_, di) in enumerate(uses))

        lo, hi = (e - d for e in b.ends)
        if b.reg is None:
            return exact(lo)
        c = len(uses)
        plus = self.base[stage] + sum(di + (i <= j) for i, (_, di) in enumerate(uses)) - c * d
        assert c * (lo + d) + plus == exact(lo) and c * (hi + d) + plus == exact(hi), (stage, name, lo, hi)
        return b.times(c, plus)


class Steps:

    def __init__(self, eng, sem):
        self.eng, self.sem, self.n = eng, sem, 0
        self.reg = None

    def loop(self, reg, first, per):
        self.reg, self.first, self.per, self.n0 = reg, first, per, self.n

    def end(self, trips):
        assert self.n - self.n0 == self.per, f"{self.sem}: {self.n - self.n0} steps in the loop's body"
        self.n = self.n0 + self.per * trips
        self.reg = None

    def value(self):
        if self.reg is None:
            return self.n
        return self.reg * self.per + (self.n - self.first * self.per)

    def then(self, ins):
        self.n += 1
        ins.then_inc(self.sem, 1)
        self.eng.wait_ge(self.sem, self.value())


def sweep(eng, steps, per, body, first, last, lo, trips):
    for t in range(first, lo):
        body(At(None, t))
    with eng.Fori(0, trips) as i:
        if steps:
            steps.loop(i, 0, per)
        for q in range(2):
            body(At(i, lo + q, (0, trips)))
        if steps:
            steps.end(trips)
    for t in range(lo + 2 * trips, last + 1):
        body(At(None, t))


USES_T = {
    "load": [("ln", 0)],
    "attn_a": [("qk", 2), ("ctx", -1), ("max", 1)],
    "out_a": [("ln", -1)],
    "attn_b": [("qk", 2), ("feat", 1), ("ctx", -1), ("ln", -1)],
    "attn_c": [("qk", 2), ("feat", 1), ("ctx", -1), ("ln", -1)],
    "moe": [("logits", 1), ("gate", 1), ("ln", -1)],
    "ssm": [("ln", -1)],
    "mix": [("ln", -1)],
}
USES_U = {
    "load": [],
    "attn_a": [("ctx0", -1), ("ctx1", -1), ("v", 1)],
    "out_a": [("update", 1)],
    "attn_b": [("v", 1), ("ctx0", -1), ("ctx1", -1), ("update", -1)],
    "attn_c": [("swapped", 2), ("v", 1), ("ctx0", -1), ("ctx1", -1), ("update", -1)],
    "moe": [("update", 0)],
    "ssm": [],
    "mix": [],
}
QUERY_SLOTS = {2: (0, 4), 3: (4, 7), 4: (7, 10), 5: (10, 13), 6: (13, 16)}
SWEEP = {
    "attn_a": (-2, 8, 2, 2),
    "out_a": (-1, 8, 2, 2),
    "attn_b": (-2, 8, 2, 2),
    "attn_c": (-2, 8, 2, 2),
    "moe": (-1, 8, 2, 2),
    "ssm": (-2, 8, 2, 2),
    "mix": (-2, 8, 2, 2),
}


def hybrid_kernel(nc, io, out):
    led_t = Ledger([USES_T[k] for k in ["load"] + STAGES])
    led_u = Ledger([USES_U[k] for k in ["load"] + STAGES])
    with ExitStack() as ctx:
        def sb(name, shape, dt=F32):
            return ctx.enter_context(nc.sbuf_tensor(name, shape, dt))

        def ps(name, shape, dt=F32):
            return ctx.enter_context(nc.psum_tensor(name, shape, dt))

        def sem(name):
            return ctx.enter_context(nc.semaphore(name))

        ps_a = ps("ps_a", [P, 2, 512])
        ps_b = ps("ps_b", [P, 2, 512])
        ps_c = ps("ps_c", [P, 2, 512])
        ps_t = ps("ps_t", [P, 512])
        ps_u = ps("ps_u", [P, 512])

        x = sb("x", [P, NB * TILES, D])
        xnT = sb("xnT", [P, NB * TOK])
        xcur = [sb(f"xcur{i}", [P, TOK + 1]) for i in range(2)]
        xn = [sb(f"xn{i}", [P, TILES, D]) for i in range(2)]
        stats = [sb(f"stats{i}", [P, TILES, 6]) for i in range(2)]
        mv = [sb(f"mv{i}", [P, TILES, 2]) for i in range(2)]
        var_eps = [sb(f"var_eps{i}", [P, 4]) for i in range(2)]
        rstd = [sb(f"rstd{i}", [P, TILES]) for i in range(2)]
        x_new = [sb(f"x_new{i}", [P, TILES, D]) for i in range(2)]
        ln_eps = sb("ln_eps", [P, 4])
        idle = sb("idle", [P, 2])
        half_neg = sb("half_neg", [P, 4])
        ident = sb("ident", [P, P])
        ident_b = sb("ident_b", [P, P], BF16)

        w = {}
        for name in ["a_wq", "a_wk", "a_wv", "a_wo", "b_wproj", "s_wb", "s_wc", "c_wout", "m_wr", "m_wk", "m_wv"]:
            w[name] = sb("w_" + name, [P, D])
        w["b_wqkv"] = sb("w_b_wqkv", [P, 3 * D])
        w["c_wqkv"] = sb("w_c_wqkv", [P, 3 * D])
        w["c_wswap"] = sb("w_c_wswap", [P, 2 * D])
        w["w1"] = sb("w_w1", [P, E, D])
        w["w2"] = sb("w_w2", [P, E, D])
        w["wr"] = sb("w_wr", [P, E])
        row = {}
        for name in ["a_bo", "a_bv", "b_bproj", "s_beta", "s_gamma"]:
            row[name] = sb("row_" + name, [P, D])
        row["br"] = sb("row_br", [P, E])
        row["qk_scale"] = sb("row_qk_scale", [P, 2, D])
        col = {}
        for name in ["a_bq", "a_bk", "et", "is", "log_a", "mu_r", "mu_k"]:
            col[name] = sb("col_" + name, [P, 1])
        g1 = sb("g1", [P, E])
        be1 = sb("be1", [P, E])
        b2_rows = sb("b2_rows", [96, D])
        w1_part = [sb(f"w1_part{i}", [P, E, D], F16) for i in range(2)]
        x_part = [sb(f"x_part{i}", [P, 2, TOK], F16) for i in range(2)]
        x_big = [sb(f"x_big{i}", [P, TOK]) for i in range(2)]
        g1_small = sb("g1_small", [P, E])
        b1_f = sb("b1_f", [E, 2, D])
        b1_part = sb("b1_part", [E, 3, D], BF16)
        b1_rows = sb("b1_rows", [3, E * D], BF16)
        ones3 = sb("ones3", [3, P], BF16)
        gate_sel = sb("gate_sel", [96, E, P], BF16)
        decay = sb("decay", [P, 1])
        mu_r1 = sb("mu_r1", [P, 1])
        mu_k1 = sb("mu_k1", [P, 1])
        sig = sb("sig", [P, 2])
        bias_q = sb("bias_q", [P, TILES, TOK], BF16)
        bias_k = sb("bias_k", [P, TILES, TOK])
        bias_f = sb("bias_f", [P, TILES, TOK])
        rope_cos = sb("rope_cos", [P, TILES, HD])
        rope_sin = sb("rope_sin", [P, TILES, HD])
        causal = sb("causal", [P, P])
        bound = sb("bound", [P, 4])

        qk32 = [sb(f"qk32_{i}", [P, 2, TOK]) for i in range(2)]
        rest = [sb(f"rest_{i}", [P, 2, TOK]) for i in range(2)]
        parts = [sb(f"parts_{i}", [P, 2, 3, TOK], BF16) for i in range(2)]
        stack = [sb(f"stack{i}", [P, H // 2, 2, TOK], BF16) for i in range(2)]
        stack_q = [stack[i][:, :, 0, :] for i in range(2)]
        stack_k = [stack[i][:, :, 1, :] for i in range(2)]
        v_aug = [sb(f"v_aug{i}", [P, TILES, H, 32]) for i in range(2)]
        probs = [sb(f"probs{i}", [P, 4, TOK]) for i in range(4)]
        neg_max = sb("neg_max", [P, TILES, H])
        max_rows = sb("max_rows", [H, TOK], BF16)
        ctx_raw = sb("ctx_raw", [P, HG, TOK])
        ctx_n = sb("ctx_n", [P, TILES, D])
        ctx_T = [sb(f"ctx_T{i}", [P, TOK]) for i in range(2)]
        ctx_flip = sb("ctx_flip", [P, H, NB, SPAN])
        den = sb("den", [P, TILES, H])
        qraw = [sb(f"qraw{i}", [P, TILES, 2, D]) for i in range(2)]
        qtmp = [sb(f"qtmp{i}", [P, TILES, 2, D]) for i in range(2)]
        feat = [sb(f"feat{i}", [P, TILES, 2, D]) for i in range(2)]
        ss = [sb(f"ss{i}", [P, 2 * TILES * H]) for i in range(2)]
        rms_inv = sb("rms_inv", [P, 2 * TILES * H])
        rms = [sb(f"rms{i}", [P, 2 * TILES * H]) for i in range(2)]

        lg = sb("lg", [P, TILES, 24])
        lgd = sb("lgd", [P, TILES, 1])
        lge = sb("lge", [P, TILES, 1])
        euler = sb("euler", [P, TILES])
        scale_col = sb("scale_col", [P, 1])
        lidx = sb("lidx", [P, TILES, 8], U32)
        lidf = sb("lidf", [P, TILES, 2])
        lsum = sb("lsum", [P, TILES, 1])
        lw = sb("lw", [P, TILES, 2])
        iota_e = sb("iota_e", [P, E])
        gates = sb("gates", [P, 3, TILES, E])
        gates_b = sb("gates_b", [P, 2, TILES, E], BF16)
        gate_pack = sb("gate_pack", [P, TILES, 96])
        gate_f = [sb(f"gate_f{i}", [96, TOK]) for i in range(2)]
        gate_b = [sb(f"gate_b{i}", [96, TOK], BF16) for i in range(2)]
        h_sq = [sb(f"h_sq{i}", [P, 4, D], BF16) for i in range(2)]
        hvar = [sb(f"hvar{i}", [P, 4]) for i in range(2)]
        hve = [sb(f"hve{i}", [P, 4]) for i in range(2)]
        hrs = [sb(f"hrs{i}", [P, 4]) for i in range(2)]
        hn = [sb(f"hn{i}", [P, 2, TILES, D]) for i in range(2)]
        aT = [sb(f"aT{i}", [P, 2, TOK]) for i in range(2)]
        ag = [sb(f"ag{i}", [P, 2, TOK]) for i in range(2)]

        states = [sb(f"states{i}", [P, TOK]) for i in range(2)]
        yst = [sb(f"yst{i}", [P, TILES, 6]) for i in range(2)]
        ymv = [sb(f"ymv{i}", [P, TILES, 2]) for i in range(2)]
        yve = [sb(f"yve{i}", [P, TILES]) for i in range(2)]
        yrs = [sb(f"yrs{i}", [P, TILES]) for i in range(2)]
        yn = sb("yn", [P, TILES, D])
        upd = [sb(f"upd{i}", [P, TILES, D]) for i in range(2)]
        mix_t = [sb(f"mix_t{i}", [P, 2, TOK]) for i in range(2)]
        mix_x = [sb(f"mix_x{i}", [P, 2, TOK]) for i in range(2)]
        r_sig = [sb(f"r_sig{i}", [P, TOK]) for i in range(2)]
        k_relu = [sb(f"k_relu{i}", [P, TOK]) for i in range(2)]
        k_sq = [sb(f"k_sq{i}", [P, TOK]) for i in range(2)]

        loaded = sem("loaded")
        x_loaded = sem("x_loaded")
        setup_pool = sem("setup_pool")
        setup_dve = sem("setup_dve")
        setup_act = sem("setup_act")
        setup_dma = sem("setup_dma")
        setup_done = sem("setup_done")
        pool_step = sem("pool_step")
        dve_step = sem("dve_step")
        act_step = sem("act_step")
        stats_ready = sem("stats_ready")
        rstd_ready = sem("rstd_ready")
        xn_ready = sem("xn_ready")
        xnT_filled = sem("xnT_filled")
        t_drained = sem("t_drained")
        u_drained = sem("u_drained")
        xcur_ready = sem("xcur_ready")
        stored = sem("stored")
        first_x = sem("first_x")
        qk_filled = sem("qk_filled")
        swapped_filled = sem("swapped_filled")
        v_filled = sem("v_filled")
        rest1_ready = sem("rest1_ready")
        high_ready = sem("high_ready")
        mid_ready = sem("mid_ready")
        parts_ready = sem("parts_ready")
        q_scores_filled = sem("q_scores_filled")
        maxed = sem("maxed")
        max_filled = sem("max_filled")
        scores_filled = sem("scores_filled")
        probs_ready = sem("probs_ready")
        pv_done = sem("pv_done")
        ctx_copied = sem("ctx_copied")
        ctx_filled = sem("ctx_filled")
        ctx_ready = sem("ctx_ready")
        ctxT_filled = sem("ctxT_filled")
        ctx_sent = [sem(f"ctx_sent{i}") for i in range(2)]
        update_filled = sem("update_filled")
        qsq_ready = sem("qsq_ready")
        qss_ready = sem("qss_ready")
        qrms_ready = sem("qrms_ready")
        qinv_ready = sem("qinv_ready")
        feat_ready = sem("feat_ready")
        feat_filled = sem("feat_filled")
        qz_ready = sem("qz_ready")
        qzm_ready = sem("qzm_ready")
        qexp_ready = sem("qexp_ready")
        rot_ready = sem("rot_ready")
        logits_filled = sem("logits_filled")
        places_ready = sem("places_ready")
        lgd_ready = sem("lgd_ready")
        lge_ready = sem("lge_ready")
        pack_ready = sem("pack_ready")
        gate_filled = sem("gate_filled")
        gate_f_ready = sem("gate_f_ready")
        gate_ready = sem("gate_ready")
        h_filled = sem("h_filled")
        hvar_ready = sem("hvar_ready")
        hrs_ready = sem("hrs_ready")
        hn_ready = sem("hn_ready")
        hT_filled = sem("hT_filled")
        gelu_ready = sem("gelu_ready")
        wb_filled = sem("wb_filled")
        gated_ready = sem("gated_ready")
        w2_done = sem("w2_done")
        ub_filled = sem("ub_filled")
        scanned = sem("scanned")
        y_filled = sem("y_filled")
        yst_ready = sem("yst_ready")
        yrs_ready = sem("yrs_ready")
        mixt_ready = sem("mixt_ready")
        mixx_ready = sem("mixx_ready")
        rk_filled = sem("rk_filled")
        rsig_ready = sem("rsig_ready")
        krelu_ready = sem("krelu_ready")
        ksq_ready = sem("ksq_ready")
        o_filled = sem("o_filled")
        stack_free = sem("stack_free")
        xpart_ready = sem("xpart_ready")
        seen_ready = sem("seen_ready")
        biased_ready = sem("biased_ready")
        stack_loaded = [sem(f"stack_loaded{i}") for i in range(2)]
        max_loaded = [sem(f"max_loaded{i}") for i in range(2)]

        n_loads = [0]
        kinds = ["load"] + STAGES
        occ = [kinds[:n].count(k) for n, k in enumerate(kinds)]
        attn_no = [sum(k.startswith("attn") for k in kinds[:n]) for n in range(len(kinds))]
        ln_no = [sum(k != "attn_a" for k in kinds[:n]) for n in range(len(kinds) + 1)]
        cur_no = [sum(k not in ("load", "out_a") for k in kinds[:n]) for n in range(len(kinds))]

        block = ctx.enter_context(nc.Block())

        def xb(b):
            return x[:, bass.ds(b.times(TILES), TILES), :] if b.reg is not None else x[:, TILES * b.off:TILES * b.off + TILES, :]

        def xt(b, j):
            n = b.times(TILES, j)
            return x[:, bass.ds(n, 1), :].rearrange("p a d -> p (a d)") if b.reg is not None else x[:, n, :]

        def xnTb(b):
            return xnT[:, bass.ds(b.times(TOK), TOK)] if b.reg is not None else xnT[:, TOK * b.off:TOK * (b.off + 1)]

        def heads(a):
            return a[:, :, :, :].rearrange("p j i (o d g) -> p (j i o) d g", o=2, g=H // 2)

        def flat(a):
            return a[:, :, :, :].rearrange("p j i f -> p j (i f)")

        def unit(t, v, d):
            return t + (v + d) // PAIRS, (v + d) % PAIRS

        def h_bank(u):
            return (ps_a if u % 4 < 2 else ps_c)[:, u % 2, :]

        def rows(name, n):
            return row[name][:, :].unsqueeze(1).to_broadcast([P, n, D])

        def ln_stats(dve, st, k, b):
            nc.vector.bn_stats(stats[b.par][:, 0, :], x_new[b.par][:, 0, :])
            st.then(nc.vector.bn_stats(stats[b.par][:, 1, :], x_new[b.par][:, 1, :]))
            nc.vector.tensor_scalar_mul(xb(b), x_new[b.par][:, :, :], 1.0)
            for j in range(TILES):
                ins = nc.vector.bn_aggr(mv[b.par][:, j, :], stats[b.par][:, j, :])
            ins.then_inc(stats_ready, 1)

        def ln_rstd(pool, st, k, b):
            pool.wait_ge(stats_ready, b.times(1, NB * ln_no[k] + 1))
            st.then(nc.gpsimd.tensor_tensor(var_eps[b.par][:, 0:TILES], mv[b.par][:, :, 1], ln_eps[:, 0:TILES], ALU.add))
            nc.gpsimd.tensor_tensor(rstd[b.par][:, :], var_eps[b.par][:, 0:TILES], half_neg[:, 0:TILES], ALU.pow).then_inc(rstd_ready, 1)

        def ln_norm(dve, k, b):
            dve.wait_ge(stats_ready, b.times(1, NB * ln_no[k] + 1))
            dve.wait_ge(rstd_ready, b.times(1, NB * ln_no[k] + 1))
            need(dve, xnT_filled, b.times(1, NB * ln_no[k] - 1))
            for j in range(TILES):
                ins = nc.vector.tensor_scalar(xn[b.par][:, j, :], x_new[b.par][:, j, :], mv[b.par][:, j, 0:1], rstd[b.par][:, j:j + 1], ALU.subtract, ALU.mult)
            ins.then_inc(xn_ready, 1)

        def ln_transpose(pe, k, b):
            pe.wait_ge(xn_ready, b.times(1, NB * ln_no[k] + 1))
            need(pe, t_drained, fill_t(k, "ln", b, -1))
            for j in range(TILES):
                ins = nc.tensor.transpose(ps_t[:, j * P:(j + 1) * P], xn[b.par][:, j, :], ident[:, :])
            ins.then_inc(xnT_filled, 1)

        def ln_copy(act, k, b):
            act.wait_ge(xnT_filled, b.times(1, NB * ln_no[k] + 1))
            nc.scalar.copy(xnTb(b), ps_t[:, 0:TOK]).then_inc(t_drained, 1)

        def fill_t(k, name, b, d=0):
            return led_t.at(k, name, b) + d

        def fill_u(k, name, b, d=0):
            return led_u.at(k, name, b) + d

        def take_batch(pool, k, b, add):
            last, n = {"attn_a": (v_filled, 1), "attn_b": (v_filled, 1), "attn_c": (v_filled, 1),
                       "moe": (h_filled, PAIRS), "ssm": (ub_filled, 1), "mix": (mixx_ready, 1)}[kinds[k]]
            before = attn_no[k] if kinds[k].startswith("attn") else occ[k]
            need(pool, last, b.times(n, n * (NB * before - 1)))
            if kinds[k] == "mix":
                need(pool, mixt_ready, b.times(1, NB * before - 1))
            pool.wait_ge(t_drained, fill_t(k - 1, "ln", b if b.reg is None else At(None, NB - 1)))
            if add:
                nc.gpsimd.tensor_tensor(xb(b), xb(b), rows(add, TILES), ALU.add)
            if kinds[k] == "attn_a":
                nc.gpsimd.tensor_copy(xcur[b.par][:, 1:TOK + 1].rearrange("p (m n) -> p n m", m=SPAN), xnTb(b).rearrange("p (n m) -> p n m", m=SPAN)).then_inc(xcur_ready, 1)
            else:
                nc.gpsimd.tensor_copy(xcur[b.par][:, 1:TOK + 1], xnTb(b)).then_inc(xcur_ready, 1)

        def xc(b, j=None):
            if j is None:
                return xcur[b.par][:, 1:TOK + 1]
            return xcur[b.par][:, 1 + j * P:1 + (j + 1) * P]

        def has_cur(eng, k, b):
            eng.wait_ge(xcur_ready, b.times(1, NB * cur_no[k] + 1))

        @block.sync
        def _(sp):
            for t in range(4):
                sp.dma_start(x[:, 4 * t:4 * t + 4, :], io["x"].rearrange("b (t p) d -> p (b t) d", p=P)[:, 4 * t:4 * t + 4, :]).then_inc(x_loaded, 16)

            def load(dst, src):
                sp.dma_start(dst, src).then_inc(loaded, 16)
                n_loads[0] += 1

            for name in ["a_wq", "a_wk", "a_wv", "a_wo", "b_wproj", "b_wqkv", "c_wqkv", "c_wswap", "c_wout", "s_wb", "s_wc", "m_wr", "m_wk", "m_wv", "wr"]:
                load(w[name][:, :], io[name])
            for name in ["w1", "w2"]:
                load(w[name][:, :, :], io[name].rearrange("e c h -> c e h"))
            for name in ["a_bo", "a_bv", "b_bproj", "s_beta", "s_gamma", "br"]:
                load(row[name][:, :], io[name].unsqueeze(0).to_broadcast([P, io[name].shape[0]]))
            load(row["qk_scale"][:, :, :], io["qk_scale"].unsqueeze(0).to_broadcast([P, 2, D]))
            for name in ["a_bq", "a_bk", "log_a", "mu_r", "mu_k"]:
                load(col[name][:, :], io[name].unsqueeze(1))
            for name in ["et", "is"]:
                load(col[name][:, :], io[name].unsqueeze(1).to_broadcast([P, 1]))
            load(g1[:, :], io["g1"])
            load(be1[:, :], io["be1"])
            load(b1_f[:, 0, :], io["b1"])
            load(bias_f[:, :, :], io["bias_q"].rearrange("(t p) k -> p t k", p=P))
            load(bias_k[:, :, :], io["bias_k"].rearrange("(t p) k -> p t k", p=P))
            load(rope_cos[:, :, :], io["rope_cos"].rearrange("(t p) d -> p t d", p=P))
            load(rope_sin[:, :, :], io["rope_sin"].rearrange("(t p) d -> p t d", p=P))
            sp.wait_ge(setup_pool, 1)
            for i in range(3):
                load(b2_rows[32 * i:32 * i + E, :], io["b2"])
            for k in range(1, len(kinds)):
                if kinds[k] == "out_a":
                    sp.wait_ge(setup_dve, 2)
                    for i in range(3):
                        sp.dma_start(b1_rows[i:i + 1, :], b1_part[:, i, :]).then_inc(setup_dma, 16)
                if not kinds[k].startswith("attn"):
                    continue
                a0 = attn_no[k] * NB

                def send_contexts(b):
                    sp.wait_ge(t_drained, fill_t(k, "ctx", b))
                    for m in range(SPAN):
                        dst = ctx_flip[HD * m:HD * (m + 1), :, bass.ds(b.times(1), 1), :] if b.reg is not None else ctx_flip[HD * m:HD * (m + 1), :, b.off, :]
                        sp.dma_start(dst, ctx_T[b.par][:, SPAN * m:SPAN * (m + 1)]).then_inc(ctx_sent[b.par], 16)

                def body(t):
                    if t.has(1):
                        b = t + 1
                        if kinds[k] == "attn_a":
                            sp.wait_ge(stack_free, b.times(1, 1))
                        else:
                            sp.wait_ge(parts_ready, b.times(1, a0 + 1))
                        for slot in range(6):
                            first, second = Q_PART[slot], 3 + K_PART[slot]
                            src = parts[b.par][:, :, :, :].rearrange("p i a t -> p (i a) t")[:, first:second + 1:second - first, :]
                            sp.dma_start(stack[b.par][slot::SLOTS, :, :, :], src).then_inc(stack_loaded[b.par], 16)
                    if kinds[k] == "attn_a":
                        for d in ((-2, -1) if t.reg is None and t.off == NB else (-2,)):
                            if t.has(d):
                                send_contexts(t + d)
                    if t.has(1):
                        b = t + 1
                        if kinds[k] == "attn_a":
                            sp.wait_ge(t_drained, fill_t(k, "max", b))
                            sp.dma_start(stack_q[b.par][STACK - 1::STACK, :, :], max_rows[:, :]).then_inc(max_loaded[b.par], 16)
                f, l, lo, trips = SWEEP[kinds[k]]
                sweep(sp, None, 0, body, f, l, lo, trips)

            out_v = out.rearrange("b (t p) d -> p (b t) d", p=P)
            for b in range(NB):
                sp.wait_ge(stats_ready, NB * (ln_no[-1] - 1) + b + 1)
                sp.dma_start(out_v[:, TILES * b:TILES * (b + 1), :], x[:, TILES * b:TILES * (b + 1), :]).then_inc(stored, 16)
            sp.wait_ge(stored, 16 * NB)

        STACK_DMAS = 6

        @block.gpsimd
        def _(pool):
            st = Steps(pool, pool_step)
            nc.gpsimd.memset(b2_rows[:, :], 0.0).then_inc(setup_pool, 1)
            nc.gpsimd.memset(half_neg[:, :], -0.5)
            nc.gpsimd.memset(ln_eps[:, :], LN_EPS)
            nc.gpsimd.memset(euler[:, :], math.e)
            nc.gpsimd.memset(scale_col[:, :], SCALE)
            st.then(nc.gpsimd.memset(ident[:, :], 0.0))
            nc.gpsimd.affine_select(out=ident[:, :], in_=ident[:, :], compare_op=ALU.not_equal, fill=1.0, base=0, pattern=[[-1, P]], channel_multiplier=1).then_inc(setup_pool, 1)
            for i in range(2):
                nc.gpsimd.memset(stack_q[i], 0.0)
                nc.gpsimd.memset(stack_k[i], 1.0)

            def first_norm(t):
                if t.has(0):
                    ln_rstd(pool, st, 0, t)
            sweep(pool, st, 2, first_norm, 0, 7, 2, 2)


            for i in range(2):
                nc.gpsimd.memset(xcur[i][:, 0:1], 0.0)
            pool.wait_ge(setup_pool, 2)
            nc.gpsimd.tensor_copy(ident_b[:, :], ident[:, :]).then_inc(setup_pool, 1)

            def later_constants():
                nc.gpsimd.memset(ones3[:, :], 1.0)
                nc.gpsimd.memset(gate_sel[:, :, :], 0.0)
                nc.gpsimd.memset(causal[:, :], 1.0)
                nc.gpsimd.iota(iota_e[:, :], pattern=[[1, E]], base=0, channel_multiplier=0, allow_small_or_imprecise_dtypes=True)
                st.then(nc.gpsimd.memset(gate_pack[:, :, :], 0.0))
                nc.gpsimd.affine_select(out=causal[:, :], in_=causal[:, :], compare_op=ALU.is_ge, fill=0.0, base=0, pattern=[[1, P]], channel_multiplier=-1)
                for i in range(3):
                    ins = nc.gpsimd.affine_select(out=gate_sel[:, :, :], in_=gate_sel[:, :, :], compare_op=ALU.not_equal, fill=1.0, base=-32 * i, pattern=[[-1, E], [0, P]], channel_multiplier=1)
                    if i < 2:
                        st.then(ins)
                ins.then_inc(setup_pool, 1)

            for k in range(1, len(kinds)):
                kind = kinds[k]
                a0 = attn_no[k] * NB
                o0 = occ[k] * NB
                last = k == len(kinds) - 1

                def split(b):
                    pr = b.par
                    pool.wait_ge(high_ready, b.times(1, a0 + 1))
                    nc.gpsimd.tensor_tensor(rest[pr][:, :, :], qk32[pr][:, :, :], parts[pr][:, :, 0, :], ALU.subtract).then_inc(rest1_ready, 1)
                    pool.wait_ge(mid_ready, b.times(1, a0 + 1))
                    if kind != "attn_a":
                        need(pool, scores_filled, b.times(8, 8 * (a0 - 1)))
                    nc.gpsimd.tensor_tensor(parts[pr][:, :, 2, :], rest[pr][:, :, :], parts[pr][:, :, 1, :], ALU.subtract).then_inc(parts_ready, 1)

                def attn(t):
                    if t.has(1) and kind == "attn_a":
                        pool.wait_ge(parts_ready, (t + 1).times(1, 1))
                        need(pool, scores_filled, (t + 1).times(8, -8))
                        nc.gpsimd.tensor_tensor(idle[:, 0:1], ln_eps[:, 0:1], ln_eps[:, 1:2], ALU.add).then_inc(stack_free, 1)
                    if t.has(2):
                        take_batch(pool, k, t + 2, {"attn_a": "a_bo", "attn_b": "b_bproj"}.get(kind))
                    if kind == "attn_b" and t.has(2):
                        b = t + 2
                        pr = b.par
                        pool.wait_ge(t_drained, fill_t(k, "qk", b))
                        nc.gpsimd.tensor_tensor(qtmp[pr][:, :, :, :], qraw[pr][:, :, :, :], qraw[pr][:, :, :, :], ALU.mult).then_inc(qsq_ready, 1)
                    lead = 2 if kind == "attn_a" else 1
                    if t.has(lead):
                        split(t + lead)
                    if kind == "attn_b" and t.has(2):
                        b = t + 2
                        pr = b.par
                        pool.wait_ge(qinv_ready, b.times(1, 1))
                        need(pool, feat_filled, b.times(1, -1))
                        inv = rms[pr][:, :].rearrange("p (n g) -> p n g", g=H // 2).unsqueeze(2).to_broadcast([P, 4 * TILES, HD, H // 2])
                        st.then(nc.gpsimd.tensor_tensor(heads(qtmp[pr]), heads(qraw[pr]), inv, ALU.mult))
                        nc.gpsimd.tensor_tensor(flat(feat[pr]), flat(qtmp[pr]), row["qk_scale"][:, :, :].rearrange("p i f -> p (i f)").unsqueeze(1).to_broadcast([P, TILES, 2 * D]), ALU.mult).then_inc(feat_ready, 1)
                    if kind == "attn_c" and t.has(2):
                        b = t + 2
                        pr = b.par
                        pool.wait_ge(rot_ready, b.times(1, 1))
                        need(pool, feat_filled, b.times(1, NB - 1))
                        nc.gpsimd.tensor_tensor(flat(qraw[pr]), flat(qraw[pr]), flat(qtmp[pr]), ALU.add).then_inc(qz_ready, 1)
                        pool.wait_ge(qzm_ready, b.times(1, 1))
                        st.then(nc.gpsimd.tensor_tensor(flat(qraw[pr]), flat(qraw[pr]), flat(qtmp[pr]), ALU.add))
                        pool.wait_ge(qexp_ready, b.times(1, 1))
                        nc.gpsimd.tensor_tensor(flat(feat[pr]), flat(feat[pr]), flat(qraw[pr]), ALU.add).then_inc(feat_ready, 1)
                    if t.has(-1) and kind != "attn_a":
                        ln_rstd(pool, st, k, t + -1)

                def out_a(t):
                    if t.has(0):
                        ln_rstd(pool, st, k, t)

                def moe(t):
                    if t.has(1):
                        b = t + 1
                        take_batch(pool, k, b, None)
                        has_cur(pool, k, b)
                        nc.gpsimd.tensor_tensor(x_big[b.par][:, :], xc(b), scale_col[:, 0:1].to_broadcast([P, TOK]), ALU.mult)
                        st.then(nc.gpsimd.tensor_tensor(x_part[b.par][:, 0, :], xc(b), scale_col[:, 0:1].to_broadcast([P, TOK]), ALU.mult))
                        nc.gpsimd.tensor_tensor(x_part[b.par][:, 1, :], x_big[b.par][:, :], x_part[b.par][:, 0, :], ALU.subtract).then_inc(xpart_ready, 1)
                    for v in range(8):
                        b, u = unit(t, v, 1)
                        if b.has(0):
                            pr = u % 2
                            pool.wait_ge(hvar_ready, b.times(8, 8 * o0 + u + 1))
                            need(pool, hn_ready, b.times(8, 8 * o0 + u - 1))
                            st.then(nc.gpsimd.tensor_tensor(hve[pr][:, :], hvar[pr][:, :], ln_eps[:, :], ALU.add))
                            nc.gpsimd.tensor_tensor(hrs[pr][:, :], hve[pr][:, :], half_neg[:, :], ALU.pow).then_inc(hrs_ready, 1)
                        if v == 3 and t.has(1):
                            b = t + 1
                            pool.wait_ge(lgd_ready, b.times(1, o0 + 1))
                            nc.gpsimd.tensor_tensor(lge[:, :, :], euler[:, :].unsqueeze(2), lgd[:, :, :], ALU.pow).then_inc(lge_ready, 1)
                        if v == 3 and t.has(-1):
                            ln_rstd(pool, st, k, t + -1)

                def ssm(t):
                    if t.has(2):
                        take_batch(pool, k, t + 2, "s_beta")
                    if t.has(0):
                        ln_rstd(pool, st, k, t)
                    if t.has(1):
                        b = t + 1
                        pool.wait_ge(yst_ready, b.times(1, 1))
                        st.then(nc.gpsimd.tensor_tensor(yve[b.par][:, :], ymv[b.par][:, :, 1], ln_eps[:, 0:TILES], ALU.add))
                        nc.gpsimd.tensor_tensor(yrs[b.par][:, :], yve[b.par][:, :], half_neg[:, 0:TILES], ALU.pow).then_inc(yrs_ready, 1)

                def mix(t):
                    if t.has(2):
                        b = t + 2
                        take_batch(pool, k, b, None)
                        has_cur(pool, k, b)
                        need(pool, mixx_ready, b.times(1, o0 - 1))
                        for i, m in enumerate([mu_r1, mu_k1]):
                            ins = nc.gpsimd.tensor_tensor(mix_t[b.par][:, i, :], xcur[b.par][:, 0:TOK], m[:, :].to_broadcast([P, TOK]), ALU.mult)
                        ins.then_inc(mixt_ready, 1)
                    if t.has(1):
                        b = t + 1
                        pool.wait_ge(krelu_ready, b.times(1, o0 + 1))
                        need(pool, o_filled, b.times(1, o0 - 1))
                        nc.gpsimd.tensor_tensor(k_sq[b.par][:, :], k_relu[b.par][:, :], k_relu[b.par][:, :], ALU.mult).then_inc(ksq_ready, 1)
                    if t.has(0) and not last:
                        ln_rstd(pool, st, k, t)

                if k == 1:
                    pool.wait_ge(loaded, 16 * n_loads[0])
                if kind == "out_a":
                    later_constants()
                if k == 3:
                    pool.wait_ge(setup_done, 1)
                body = {"out_a": out_a, "moe": moe, "ssm": ssm, "mix": mix}.get(kind, attn)
                per = {"attn_a": 0, "out_a": 2, "attn_b": 4, "attn_c": 4, "moe": 20, "ssm": 4, "mix": 2 * (not last)}[kind]
                f, l, lo, trips = SWEEP[kind]
                sweep(pool, st, per, body, f, l, lo, trips)

        @block.scalar
        def _(act):
            def first_norm(t):
                if t.has(0):
                    ln_copy(act, 0, t)
            sweep(act, None, 0, first_norm, 0, 7, 2, 2)
            act.wait_ge(loaded, 16 * n_loads[0])
            nc.scalar.activation(decay[:, :], col["log_a"][:, :], ACT.Exp)
            nc.scalar.activation(sig[:, 0:1], col["et"][:, :], ACT.Exp, scale=-1.0).then_inc(setup_act, 1)

            for k in range(1, len(kinds)):
                kind = kinds[k]
                a0 = attn_no[k] * NB
                o0 = occ[k] * NB
                last = k == len(kinds) - 1

                def high(b):
                    pr = b.par
                    if kind != "attn_a":
                        act.wait_ge(feat_filled, b.times(1, a0 - NB + 1))
                        nc.scalar.copy(qk32[pr][:, :, :], ps_t[:, :].rearrange("p (i t) -> p i t", i=2)).then_inc(t_drained, 1)
                        act.wait_ge(t_drained, fill_t(k, "feat", b))
                    else:
                        act.wait_ge(t_drained, fill_t(k, "qk", b))
                    need(act, stack_loaded[pr], b.half(16 * STACK_DMAS, 16 * STACK_DMAS * (a0 // 2)))
                    nc.scalar.copy(parts[pr][:, :, 0, :], qk32[pr][:, :, :]).then_inc(high_ready, 1)

                def mid(b):
                    act.wait_ge(rest1_ready, b.times(1, a0 + 1))
                    nc.scalar.copy(parts[b.par][:, :, 1, :], rest[b.par][:, :, :]).then_inc(mid_ready, 1)

                def attn(t):
                    if t.has(-1):
                        b = t + -1
                        act.wait_ge(pv_done, b.times(8, 8 * a0 + 8))
                        need(act, ctx_filled, b.times(2, 2 * a0))
                        nc.scalar.copy(ctx_raw[:, :, :], ps_c[:, :, :].rearrange("p a (b t) -> p (a b) t", t=TOK)).then_inc(ctx_copied, 1)
                    if kind == "attn_b" and t.has(2):
                        b = t + 2
                        act.wait_ge(qk_filled, b.times(1, a0 + 1))
                        need(act, feat_ready, b.times(1, -1))
                        nc.scalar.copy(qraw[b.par][:, :, :, :].rearrange("p j i d -> p (j i d)"), ps_t[:, :]).then_inc(t_drained, 1)
                    if kind != "attn_a" and t.has(1):
                        high(t + 1)
                    for i in range(8):
                        if kind == "attn_a" and t.has(1) and i == 7:
                            b = t + 1
                            act.wait_ge(max_filled, b.times(1, 1))
                            for pr in range(2):
                                if pr != b.par:
                                    need(act, max_loaded[pr], (b + -1).half(16, 16))
                            nc.scalar.copy(max_rows[:, :], ps_t[0:H, 0:TOK]).then_inc(t_drained, 1)
                        if t.has(0) and kind == "attn_a":
                            act.wait_ge(biased_ready, t.times(8, i + 1))
                            nc.scalar.activation(probs[i % 4][:, :, :], probs[i % 4][:, :, :], ACT.Exp).then_inc(probs_ready, 1)
                        if t.has(0) and kind == "attn_c" and i % 2 == 0:
                            act.wait_ge(probs_ready, t.times(8, 8 * a0 + i + 1))
                            need(act, pv_done, t.times(8, 8 * a0 + i - 3))
                            nc.scalar.copy(probs[i % 4][:, :, P:TOK], ps_a[:, :, :].rearrange("p a (b t) -> p (a b) t", t=TOK)[:, :, P:TOK]).then_inc(seen_ready, 1)
                        if t.has(0) and kind == "attn_b":
                            act.wait_ge(scores_filled, t.times(8, 8 * a0 + i + 1))
                            need(act, pv_done, t.times(8, 8 * a0 + i - 3))
                            src = (ps_b if i % 2 else ps_a)[:, :, :].rearrange("p a (b t) -> p (a b) t", t=TOK)
                            nc.scalar.activation(probs[i % 4][:, :, :], src, ACT.Exp, bias=bound[:, 3:4]).then_inc(probs_ready, 1)
                        if kind == "attn_a" and t.has(2):
                            if i == 2:
                                high(t + 2)
                            if i == 4:
                                mid(t + 2)
                        if kind != "attn_a" and t.has(1) and i == 1:
                            mid(t + 1)
                        if kind == "attn_b" and t.has(2) and i == 2:
                            b = t + 2
                            act.wait_ge(qss_ready, b.times(1, 1))
                            nc.scalar.activation(rms[b.par][:, :], ss[b.par][:, :], ACT.Sqrt, scale=1.0 / HD).then_inc(qrms_ready, 1)
                        if kind == "attn_c" and t.has(2) and i == 3:
                            b = t + 2
                            act.wait_ge(qz_ready, b.times(1, 1))
                            nc.scalar.activation(flat(qtmp[b.par]), flat(qraw[b.par]), ACT.Relu, scale=-1.0).then_inc(qzm_ready, 1)
                            act.wait_ge(qzm_ready, b.times(1, 1))
                            nc.scalar.activation(flat(feat[b.par]), flat(qtmp[b.par]), ACT.Exp, scale=-1.0).then_inc(qexp_ready, 1)
                        if t.has(-1):
                            b = t + -1
                            if i == 4:
                                act.wait_ge(ctxT_filled, b.times(1, a0 + 1))
                                if kind == "attn_a":
                                    need(act, ctx_sent[b.par], b.half(16 * SPAN))
                                else:
                                    need(act, update_filled, b.times(1, a0 - 1))
                                nc.scalar.copy(ctx_T[b.par][:, :], ps_t[:, 0:TOK]).then_inc(t_drained, 1)
                            if i == 7 and kind != "attn_a":
                                ln_copy(act, k, b)

                def out_a(t):
                    if t.has(-1):
                        ln_copy(act, k, t + -1)

                def moe(t):
                    for v in range(8):
                        b, u = unit(t, v, 2)
                        if b.has(0):
                            act.wait_ge(h_filled, b.times(8, 8 * o0 + u + 1))
                            need(act, hrs_ready, b.times(8, 8 * o0 + u - 1))
                            hv = h_bank(u).rearrange("p (c d) -> p c d", d=D)
                            for c in range(4):
                                ins = nc.scalar.activation(h_sq[u % 2][:, c, :], hv[:, c, :], ACT.Square, scale=float(D ** -0.5 / SCALE ** 2), accum_out=hvar[u % 2][:, c:c + 1])
                            ins.then_inc(hvar_ready, 1)
                        if t.has(0):
                            act.wait_ge(hT_filled, t.times(8, 8 * o0 + v + 1))
                            need(act, gated_ready, t.times(8, 8 * o0 + v - 1))
                            for e in range(2):
                                ex = 2 * v + e
                                ins = nc.scalar.activation(aT[v % 2][:, e, :], ps_b[:, 0, e * TOK:(e + 1) * TOK], ACT.Gelu, bias=be1[:, ex:ex + 1], scale=g1_small[:, ex:ex + 1])
                            ins.then_inc(gelu_ready, 1)
                        if t.has(1):
                            b = t + 1
                            if v == 5:
                                act.wait_ge(gate_filled, b.times(1, o0 + 1))
                                nc.scalar.copy(gate_f[b.par][:, :], ps_t[0:96, 0:TOK])
                                nc.scalar.copy(gate_b[b.par][:, :], ps_t[0:96, 0:TOK]).then_inc(t_drained, 1)
                        if v == 6 and t.has(-1):
                            ln_copy(act, k, t + -1)

                def ssm(t):
                    if t.has(-1):
                        ln_copy(act, k, t + -1)

                def mix(t):
                    if t.has(1):
                        b = t + 1
                        act.wait_ge(rk_filled, b.times(1, o0 + 1))
                        need(act, o_filled, b.times(1, o0 - 1))
                        nc.scalar.activation(k_relu[b.par][:, :], ps_a[:, 1, 0:TOK], ACT.Relu).then_inc(krelu_ready, 1)
                        nc.scalar.activation(r_sig[b.par][:, :], ps_a[:, 0, 0:TOK], ACT.Sigmoid).then_inc(rsig_ready, 1)
                    if t.has(-1) and not last:
                        ln_copy(act, k, t + -1)

                if k == 3:
                    act.wait_ge(setup_done, 1)
                body = {"out_a": out_a, "moe": moe, "ssm": ssm, "mix": mix}.get(kind, attn)
                f, l, lo, trips = SWEEP[kind]
                sweep(act, None, 0, body, f, l, lo, trips)

        @block.vector
        def _(dve):
            st = Steps(dve, dve_step)

            def first_norm(t):
                if t.has(0):
                    need(dve, xn_ready, t.times(1, -1))
                    nc.vector.tensor_scalar_mul(x_new[t.par][:, :, :], xb(t), 1.0).then_inc(first_x, 1)
                    dve.wait_ge(first_x, t.times(1, 1))
                    ln_stats(dve, st, 0, t)
                if t.has(-1):
                    ln_norm(dve, 0, t + -1)
            for i in range(2):
                ins = nc.vector.memset(v_aug[i][:, :, :, :], 0.0)
            st.then(ins)
            for i in range(2):
                ins = nc.vector.memset(v_aug[i][:, :, :, HD:HD + 1], 1.0)
            st.then(ins)
            dve.wait_ge(x_loaded, 64)
            sweep(dve, st, 2, first_norm, 0, 8, 2, 2)

            dve.wait_ge(loaded, 16 * n_loads[0])
            dve.wait_ge(setup_act, 1)
            st.then(nc.vector.tensor_scalar_add(sig[:, 1:2], sig[:, 0:1], 1.0))
            st.then(nc.vector.reciprocal(sig[:, 0:1], sig[:, 1:2]))
            nc.vector.tensor_scalar(bias_q[:, :, :], bias_f[:, :, :], sig[:, 0:1], col["is"][:, 0:1], ALU.mult, ALU.add)
            st.then(nc.vector.tensor_scalar(bias_k[:, :, :], bias_k[:, :, :], sig[:, 0:1], col["is"][:, 0:1], ALU.mult, ALU.add))
            nc.vector.tensor_copy(bound[:, 2:3], sig[:, 0:1]).then_inc(setup_dve, 1)
            def later_constants():
                for dst, m in ((mu_r1, col["mu_r"]), (mu_k1, col["mu_k"])):
                    nc.vector.tensor_scalar(dst[:, :], m[:, :], -1.0, 1.0, ALU.mult, ALU.add)
                w1_mean = upd[0][:, 0, 0:E]
                st.then(nc.vector.tensor_reduce(w1_mean, w["w1"][:, :, :], AX.X, ALU.add))
                st.then(nc.vector.tensor_scalar_mul(w1_mean, w1_mean, 1.0 / D))
                st.then(nc.vector.tensor_tensor(w["w1"][:, :, :], w["w1"][:, :, :], w1_mean.unsqueeze(2).to_broadcast([P, E, D]), ALU.subtract))
                st.then(nc.vector.tensor_scalar_mul(w["w1"][:, :, :], w["w1"][:, :, :], SCALE))
                st.then(nc.vector.tensor_copy(w1_part[0][:, :, :], w["w1"][:, :, :]))
                nc.vector.tensor_tensor(w1_part[1][:, :, :], w["w1"][:, :, :], w1_part[0][:, :, :], ALU.subtract)
                nc.vector.tensor_scalar_mul(g1_small[:, :], g1[:, :], SCALE ** -2)
                b1_mean = upd[0][0:E, 0, E:E + 1]
                st.then(nc.vector.tensor_reduce(b1_mean, b1_f[:, 0, :], AX.X, ALU.add))
                st.then(nc.vector.tensor_scalar_mul(b1_mean, b1_mean, 1.0 / D))
                st.then(nc.vector.tensor_scalar(b1_f[:, 0, :], b1_f[:, 0, :], b1_mean, SCALE ** 2, ALU.subtract, ALU.mult))
                st.then(nc.vector.tensor_copy(b1_part[:, 0, :], b1_f[:, 0, :]))
                st.then(nc.vector.tensor_tensor(b1_f[:, 1, :], b1_f[:, 0, :], b1_part[:, 0, :], ALU.subtract))
                st.then(nc.vector.tensor_copy(b1_part[:, 1, :], b1_f[:, 1, :]))
                nc.vector.tensor_tensor(b1_part[:, 2, :], b1_f[:, 1, :], b1_part[:, 1, :], ALU.subtract).then_inc(setup_dve, 1)
                prod = upd[0][:, 0, :]
                st.then(nc.vector.tensor_tensor(prod, row["qk_scale"][:, 0, :], row["qk_scale"][:, 1, :], ALU.mult))
                st.then(nc.vector.tensor_reduce(bound[:, 0:1], prod, AX.X, ALU.max, apply_absolute_value=True))
                nc.vector.tensor_scalar_mul(bound[:, 3:4], bound[:, 0:1], -float(HD ** 0.5))
                st.then(nc.vector.tensor_scalar_mul(row["qk_scale"][:, 0, :], row["qk_scale"][:, 0, :], float(HD ** -0.5)))
                nc.vector.tensor_copy(bound[:, 1:2], bound[:, 0:1]).then_inc(setup_done, 1)

            for k in range(1, len(kinds)):
                kind = kinds[k]
                a0 = attn_no[k] * NB
                o0 = occ[k] * NB
                last = k == len(kinds) - 1

                def residual(b, upd_ap, sem_, value):
                    ins = nc.vector.tensor_tensor(x_new[b.par][:, :, :], xb(b), upd_ap, ALU.add)
                    if sem_ is None:
                        st.then(ins)
                    else:
                        ins.then_inc(sem_, 1)
                        dve.wait_ge(sem_, value)

                def attn(t):
                    if t.has(2) and kind == "attn_c":
                        b = t + 2
                        pr = b.par
                        for src, sm, n_, tab, dst, done in ((ps_t, qk_filled, a0 + 1, rope_cos, qraw, t_drained), (ps_u, swapped_filled, 1, rope_sin, qtmp, u_drained)):
                            dve.wait_ge(sm, b.times(1, n_))
                            need(dve, feat_ready, b.times(1, NB - 1))
                            for j in range(TILES):
                                tb = tab[:, j, :].unsqueeze(1).unsqueeze(3).to_broadcast([P, 4, HD, H // 2])
                                ins = nc.vector.tensor_tensor(heads(dst[pr])[:, 4 * j:4 * j + 4], src[:, j * TOK:(j + 1) * TOK].rearrange("p (n d g) -> p n d g", d=HD, g=H // 2), tb, ALU.mult)
                            ins.then_inc(done, 1)
                        nc.vector.tensor_copy(bound[:, 2:3], bound[:, 0:1]).then_inc(rot_ready, 1)
                    def values():
                        b = t + 1
                        dve.wait_ge(v_filled, b.times(1, a0 + 1))
                        need(dve, pv_done, b.times(8, 8 * (a0 - 1)))
                        dst = v_aug[b.par][:, :, :, 0:HD]
                        src = ps_u[:, 0:TILES * D].rearrange("p (j h d) -> p j h d", j=TILES, d=HD)
                        if kind == "attn_a":
                            bv = row["a_bv"][:, :].rearrange("p (h d) -> p h d", d=HD)
                            for j in range(TILES):
                                ins = nc.vector.tensor_tensor(dst[:, j], src[:, j], bv, ALU.add)
                            ins.then_inc(u_drained, 1)
                        else:
                            for j in range(TILES):
                                ins = nc.vector.tensor_copy(dst[:, j], src[:, j])
                            ins.then_inc(u_drained, 1)

                    def query_and_key():
                        b = t + 2
                        pr = b.par
                        dve.wait_ge(qk_filled, b.times(1, a0 + 1))
                        need(dve, parts_ready, b.times(1, a0 - 1))
                        nc.vector.tensor_scalar(qk32[pr][:, 0, :], ps_t[:, 0:TOK], col["a_bq"][:, 0:1], float(HD ** -0.5), ALU.add, ALU.mult)
                        nc.vector.tensor_scalar(qk32[pr][:, 1, :], ps_t[:, TOK:2 * TOK], col["a_bk"][:, 0:1], None, ALU.add).then_inc(t_drained, 1)

                    if kind != "attn_a" and t.has(1):
                        values()
                    for i in range(8):
                        if kind == "attn_a" and t.has(0):
                            dve.wait_ge(scores_filled, t.times(8, i + 1))
                            need(dve, pv_done, t.times(8, i - 3))
                            src = (ps_a if i == 1 else ps_b)[:, :, :].rearrange("p a (b t) -> p (a b) t", t=TOK)
                            nc.vector.tensor_tensor(probs[i % 4][:, :, :], src, bias_k[:, i % 2, :].unsqueeze(1).to_broadcast([P, 4, TOK]), ALU.add).then_inc(biased_ready, 1)
                        if kind == "attn_a" and t.has(2) and i == 1:
                            query_and_key()
                        if kind == "attn_a" and t.has(1) and i == 7:
                            values()
                        if kind == "attn_c" and t.has(0):
                            dve.wait_ge(scores_filled, t.times(8, 8 * a0 + i + 1))
                            need(dve, pv_done, t.times(8, 8 * a0 + i - 3))
                            src = (ps_b if i % 2 else ps_a)[:, :, :].rearrange("p a (b t) -> p (a b) t", t=TOK)
                            q0 = P * (i % 2)
                            m = causal[:, :].unsqueeze(1).to_broadcast([P, 4, P])
                            nc.vector.tensor_tensor(probs[i % 4][:, :, q0:q0 + P], src[:, :, q0:q0 + P], m, ALU.mult).then_inc(probs_ready, 1)
                        if kind == "attn_b" and t.has(2):
                            b = t + 2
                            pr = b.par
                            if i == 1:
                                dve.wait_ge(qsq_ready, b.times(1, 1))
                                nc.vector.tensor_reduce(ss[pr][:, :], heads(qtmp[pr]).rearrange("p n d g -> p n g d"), AX.X, ALU.add).then_inc(qss_ready, 1)
                            if i == 3:
                                dve.wait_ge(qrms_ready, b.times(1, 1))
                                st.then(nc.vector.tensor_scalar_max(rms[pr][:, :], rms[pr][:, :], 1e-30))
                                st.then(nc.vector.reciprocal(rms_inv[:, :], rms[pr][:, :]))
                                st.then(nc.vector.scalar_tensor_tensor(rms_inv[:, :], ss[pr][:, :], 1.0 / HD, rms_inv[:, :], ALU.mult, ALU.mult))
                                st.then(nc.vector.tensor_tensor(rms[pr][:, :], rms[pr][:, :], rms_inv[:, :], ALU.add))
                                st.then(nc.vector.tensor_scalar(rms[pr][:, :], rms[pr][:, :], 0.5, RMS_EPS, ALU.mult, ALU.add))
                                nc.vector.reciprocal(rms[pr][:, :], rms[pr][:, :]).then_inc(qinv_ready, 1)
                        if kind == "attn_a" and t.has(1):
                            b = t + 1
                            for n in range(*QUERY_SLOTS.get(i, (0, 0))):
                                u, odd = n // 2, n % 2
                                dve.wait_ge(q_scores_filled, b.times(16, n + 1))
                                if n == 0:
                                    need(dve, max_filled, b.times(1, 0))
                                dst = neg_max[:, u // HG, odd * (H // 2) + 2 * (u % HG):odd * (H // 2) + 2 * (u % HG) + 2]
                                nc.vector.tensor_reduce(dst, ps_a[:, odd, :].rearrange("p (c t) -> p c t", t=TOK), AX.X, ALU.max, negate=True).then_inc(maxed, 1)
                        if t.has(-1):
                            b = t + -1
                            if i in (1, 2):
                                qt = i - 1
                                dve.wait_ge(ctx_filled, b.times(2, 2 * a0 + qt + 1))
                                need(dve, ctxT_filled, b.times(1, a0))
                                src = ps_u[:, :].rearrange("p (h r) -> p h r", r=32)
                                if kind == "attn_c":
                                    st.then(nc.vector.tensor_scalar_max(den[:, qt, :], src[:, :, HD:HD + 1].rearrange("p h r -> p (h r)"), 1e-6))
                                    st.then(nc.vector.reciprocal(den[:, qt, :], den[:, qt, :]))
                                else:
                                    st.then(nc.vector.reciprocal(den[:, qt, :], src[:, :, HD:HD + 1].rearrange("p h r -> p (h r)")))
                                order = "p (d h) -> p h d" if kind == "attn_a" else "p (h d) -> p h d"
                                nc.vector.tensor_tensor(ctx_n[:, qt, :].rearrange(order, d=HD), src[:, :, 0:HD], den[:, qt, :].unsqueeze(2).to_broadcast([P, H, HD]), ALU.mult).then_inc(u_drained, 1)
                            if i == 5 and kind != "attn_a":
                                dve.wait_ge(update_filled, b.times(1, a0 + 1))
                                residual(b, ps_u[:, 0:TILES * D].rearrange("p (j d) -> p j d", j=TILES), u_drained, fill_u(k, "update", b))
                                ln_stats(dve, st, k, b)
                            if i == 7 and kind != "attn_a":
                                ln_norm(dve, k, b)

                def out_a(t):
                    if t.has(0):
                        need(dve, xn_ready, t.times(1, NB * ln_no[k] - 1))
                        dve.wait_ge(update_filled, t.times(1, 1))
                        residual(t, ps_u[:, 0:TILES * D].rearrange("p (j d) -> p j d", j=TILES), u_drained, fill_u(k, "update", t))
                        ln_stats(dve, st, k, t)
                    if t.has(-1):
                        ln_norm(dve, k, t + -1)

                def moe(t):
                    for v in range(8):
                        if v == 2 and t.has(-1):
                            b = t + -1
                            dve.wait_ge(w2_done, b.times(8, 8 * o0 + 8))
                            residual(b, ps_u[:, 0:TILES * D].rearrange("p (j d) -> p j d", j=TILES), u_drained, fill_u(k, "update", b))
                        if t.has(0):
                            pr = v % 2
                            dve.wait_ge(hrs_ready, t.times(8, 8 * o0 + v + 1))
                            need(dve, hT_filled, t.times(8, 8 * o0 + v - 1))
                            hv = h_bank(v).rearrange("p (j e d) -> p e j d", j=TILES, d=D)
                            rs = hrs[pr][:, :].rearrange("p (j e) -> p e j", j=TILES).unsqueeze(3).to_broadcast([P, 2, TILES, D])
                            nc.vector.tensor_tensor(hn[pr][:, :, :, :], hv, rs, ALU.mult).then_inc(hn_ready, 1)
                        if v == 2 and t.has(1):
                            b = t + 1
                            dve.wait_ge(logits_filled, b.times(1, o0 + 1))
                            nc.vector.tensor_tensor(lg[:, :, 0:E], ps_t[:, 0:TILES * E].rearrange("p (j e) -> p j e", j=TILES), row["br"][:, :].unsqueeze(1).to_broadcast([P, TILES, E]), ALU.add).then_inc(t_drained, 1)
                            dve.wait_ge(t_drained, fill_t(k, "logits", b))
                        b, u = unit(t, v, -1)
                        if b.has(0):
                            dve.wait_ge(gelu_ready, b.times(8, 8 * o0 + u + 1))
                            dve.wait_ge(wb_filled, b.times(8, 8 * o0 + u + 1))
                            need(dve, w2_done, b.times(8, 8 * o0 + u - 1))
                            nc.vector.tensor_tensor(ag[u % 2][:, :, :].rearrange("p e t -> p (e t)"), ps_b[:, 1, :], aT[u % 2][:, :, :].rearrange("p e t -> p (e t)"), ALU.mult).then_inc(gated_ready, 1)
                        if v == 2 and t.has(1):
                            for j in range(TILES):
                                ins = nc.vector.max(lg[:, j, E:E + 8], lg[:, j, 0:E])
                            st.then(ins)
                            nc.vector.tensor_tensor(lgd[:, :, :], lg[:, :, E + 1:E + 2], lg[:, :, E:E + 1], ALU.subtract).then_inc(lgd_ready, 1)
                            for j in range(TILES):
                                ins = nc.vector.max_index(lidx[:, j, :], lg[:, j, E:E + 8], lg[:, j, 0:E])
                            ins.then_inc(places_ready, 1)
                        if v == 2 and t.has(-1):
                            ln_stats(dve, st, k, t + -1)
                        if v == 5 and t.has(-1):
                            ln_norm(dve, k, t + -1)
                        if v == 4 and t.has(1):
                            b = t + 1
                            dve.wait_ge(places_ready, b.times(1, o0 + 1))
                            dve.wait_ge(lge_ready, b.times(1, o0 + 1))
                            nc.vector.tensor_copy(lidf[:, :, :], lidx[:, :, 0:2])
                            st.then(nc.vector.tensor_scalar_add(lsum[:, :, :], lge[:, :, :], 1.0))
                            st.then(nc.vector.reciprocal(lw[:, :, 0:1], lsum[:, :, :]))
                            st.then(nc.vector.tensor_tensor(lw[:, :, 1:2], lge[:, :, :], lw[:, :, 0:1], ALU.mult))
                            for j in range(TILES):
                                for c in range(2):
                                    ins = nc.vector.tensor_scalar(gates[:, c, j, :], iota_e[:, :], lidf[:, j, c:c + 1], lw[:, j, c:c + 1], ALU.is_equal, ALU.mult)
                            st.then(ins)
                            st.then(nc.vector.tensor_tensor(gates[:, 0], gates[:, 0], gates[:, 1], ALU.add))
                            need(dve, gate_filled, b.times(1, o0))
                            st.then(nc.vector.tensor_copy(gates_b[:, 0], gates[:, 0]))
                            nc.vector.tensor_copy(gate_pack[:, :, 0:E], gates_b[:, 0])
                            st.then(nc.vector.tensor_tensor(gates[:, 1], gates[:, 0], gates_b[:, 0], ALU.subtract))
                            st.then(nc.vector.tensor_copy(gates_b[:, 1], gates[:, 1]))
                            nc.vector.tensor_copy(gate_pack[:, :, 32:32 + E], gates_b[:, 1])
                            nc.vector.tensor_tensor(gate_pack[:, :, 64:64 + E], gates[:, 1], gates_b[:, 1], ALU.subtract).then_inc(pack_ready, 1)

                def ssm(t):
                    if t.has(0):
                        dve.wait_ge(yst_ready, t.times(1, 1))
                        dve.wait_ge(yrs_ready, t.times(1, 1))
                        for j in range(TILES):
                            ins = nc.vector.tensor_scalar(yn[:, j, :], ps_b[:, t.par, j * D:(j + 1) * D], ymv[t.par][:, j, 0:1], yrs[t.par][:, j:j + 1], ALU.subtract, ALU.mult)
                        st.then(ins)
                        st.then(nc.vector.tensor_tensor(upd[t.par][:, :, :], yn[:, :, :], rows("s_gamma", TILES), ALU.mult))
                        residual(t, upd[t.par][:, :, :], None, None)
                        ln_stats(dve, st, k, t)
                    if t.has(-1):
                        ln_norm(dve, k, t + -1)
                    if t.has(1):
                        b = t + 1
                        dve.wait_ge(y_filled, b.times(1, 1))
                        for j in range(TILES):
                            ins = nc.vector.bn_stats(yst[b.par][:, j, :], ps_b[:, b.par, j * D:(j + 1) * D])
                        st.then(ins)
                    if t.has(2):
                        b = t + 2
                        dve.wait_ge(ub_filled, b.times(1, 1))
                        need(dve, y_filled, b.times(1, -1))
                        nc.vector.tensor_tensor_scan(states[b.par][:, :], decay[:, :].to_broadcast([P, TOK]), ps_a[:, b.par, 0:TOK], 0.0, ALU.mult, ALU.add).then_inc(scanned, 1)
                    if t.has(1):
                        b = t + 1
                        for j in range(TILES):
                            ins = nc.vector.bn_aggr(ymv[b.par][:, j, :], yst[b.par][:, j, :])
                        ins.then_inc(yst_ready, 1)

                def mix(t):
                    if t.has(-1) and not last:
                        ln_norm(dve, k, t + -1)
                    if t.has(0):
                        dve.wait_ge(rsig_ready, t.times(1, o0 + 1))
                        dve.wait_ge(o_filled, t.times(1, o0 + 1))
                        st.then(nc.vector.tensor_tensor(upd[t.par][:, :, :].rearrange("p j d -> p (j d)"), ps_b[:, t.par, 0:TOK], r_sig[t.par][:, :], ALU.mult))
                        if last:
                            nc.vector.tensor_tensor(xb(t), xb(t), upd[t.par][:, :, :], ALU.add).then_inc(stats_ready, 1)
                        else:
                            residual(t, upd[t.par][:, :, :], None, None)
                            ln_stats(dve, st, k, t)
                    if t.has(2):
                        b = t + 2
                        dve.wait_ge(mixt_ready, b.times(1, o0 + 1))
                        need(dve, rk_filled, b.times(1, o0 - 1))
                        for i, m in enumerate(["mu_r", "mu_k"]):
                            ins = nc.vector.scalar_tensor_tensor(mix_x[b.par][:, i, :], xc(b), col[m][:, 0:1], mix_t[b.par][:, i, :], ALU.mult, ALU.add)
                        ins.then_inc(mixx_ready, 1)

                if kind == "out_a":
                    later_constants()
                if k == 3:
                    dve.wait_ge(setup_pool, 4)
                body = {"out_a": out_a, "moe": moe, "ssm": ssm, "mix": mix}.get(kind, attn)
                per = 2 * {"attn_a": 2, "out_a": 1, "attn_b": 8, "attn_c": 5, "moe": 10, "ssm": 5, "mix": 1 if last else 3}[kind]
                f, l, lo, trips = SWEEP[kind]
                sweep(dve, st, per, body, f, l, lo, trips)

        @block.tensor
        def _(pe):
            mm = nc.tensor.matmul
            pe.wait_ge(setup_pool, 2)

            def first_norm(t):
                if t.has(0):
                    ln_transpose(pe, 0, t)
            sweep(pe, None, 0, first_norm, 0, 7, 2, 2)
            pe.wait_ge(loaded, 16 * n_loads[0])
            pe.wait_ge(setup_dve, 1)
            pe.wait_ge(setup_pool, 3)

            for k in range(1, len(kinds)):
                kind = kinds[k]
                a0 = attn_no[k] * NB
                o0 = occ[k] * NB
                last = k == len(kinds) - 1

                def head(stack, b, h, rows_):
                    r0 = STACK * (h % 2)
                    return stack[b.par][r0:r0 + rows_, h // 2, :]

                def attn(t):
                    rows_ = STACK if kind == "attn_a" else STACK - 1
                    wqkv = {"attn_b": "b_wqkv", "attn_c": "c_wqkv"}.get(kind)
                    if kind != "attn_a" and t.has(2):
                        b = t + 2
                        has_cur(pe, k, b)
                        need(pe, t_drained, fill_t(k, "qk", b, -1))
                        for j in range(TILES):
                            ins = mm(ps_t[:, j * TOK:(j + 1) * TOK], xc(b, j), w[wqkv][:, 0:2 * D], start=True, stop=True)
                        ins.then_inc(qk_filled, 1)
                        if kind == "attn_c":
                            need(pe, u_drained, fill_u(k, "swapped", b, -1))
                            for j in range(TILES):
                                ins = mm(ps_u[:, j * TOK:(j + 1) * TOK], xc(b, j), w["c_wswap"][:, :], start=True, stop=True)
                            ins.then_inc(swapped_filled, 1)
                    def values():
                        b = t + 1
                        need(pe, u_drained, fill_u(k, "v", b, -1))
                        for j in range(TILES):
                            wv = w["a_wv"][:, :] if kind == "attn_a" else w[wqkv][:, 2 * D:3 * D]
                            ins = mm(ps_u[:, j * D:(j + 1) * D], xc(b, j), wv, start=True, stop=True)
                        ins.then_inc(v_filled, 1)

                    def query_and_key():
                        b = t + 2
                        has_cur(pe, k, b)
                        need(pe, t_drained, fill_t(k, "qk", b, -1))
                        mm(ps_t[:, 0:TOK], w["a_wq"][:, :], xc(b), start=True, stop=True)
                        mm(ps_t[:, TOK:2 * TOK], w["a_wk"][:, :], xc(b), start=True, stop=True).then_inc(qk_filled, 1)

                    if kind != "attn_a" and t.has(1):
                        values()
                    if kind != "attn_a" and t.has(1):
                        b = t + 1
                        pe.wait_ge(feat_ready, b.times(1, a0 - NB + 1))
                        need(pe, t_drained, fill_t(k, "feat", b, -1))
                        need(pe, parts_ready, b.times(1, a0 - 1))
                        for i in range(2):
                            for j in range(TILES):
                                ins = nc.tensor.transpose(ps_t[:, i * TOK + j * P:i * TOK + (j + 1) * P], feat[b.par][:, j, i, :], ident[:, :])
                        ins.then_inc(feat_filled, 1)

                    def pv(i):
                        hg, kt = i // 2, i % 2
                        pe.wait_ge(probs_ready, t.times(8, 8 * a0 + i + 1))
                        if i == 0:
                            need(pe, ctx_copied, t.times(1, a0))
                            pe.wait_ge(u_drained, fill_u(k, "v", t))
                        if kind == "attn_c" and kt == 0:
                            pe.wait_ge(seen_ready, t.times(4, hg + 1))
                        q0 = P * kt if kind == "attn_c" else 0
                        for c in range(4):
                            ins = mm(ps_c[32 * c:32 * c + 32, hg // 2, (hg % 2) * TOK + q0:(hg % 2 + 1) * TOK], v_aug[t.par][:, kt, 4 * hg + c, :], probs[i % 4][:, 2 * (c % 2) + c // 2, q0:TOK], start=(kt == 0), stop=(kt == 1), skip_group_check=True)
                        ins.then_inc(pv_done, 1)

                    def query_scores(b, first, end):
                        for n in range(first, end):
                            qt, hg, odd = n // (2 * HG), n // 2 % HG, n % 2
                            if n == 0:
                                need(pe, biased_ready, t.times(8, 2))
                                pe.wait_ge(stack_loaded[b.par], b.half(16 * STACK_DMAS, 16 * STACK_DMAS * (a0 // 2 + 1)))
                            need(pe, maxed, b.times(16, n - 1))
                            mm(ps_a[:, odd, :], ident_b[:, :], bias_q[:, qt, :].unsqueeze(1).to_broadcast([P, 2, TOK]), start=True, stop=False, skip_group_check=True)
                            for c in range(2):
                                h = 4 * hg + 2 * c + odd
                                ins = mm(ps_a[:, odd, c * TOK:(c + 1) * TOK], head(stack_q, b, h, STACK - 1)[:, qt * P:(qt + 1) * P], head(stack_k, b, h, STACK - 1), start=False, stop=True, skip_group_check=True)
                            ins.then_inc(q_scores_filled, 1)

                    for i in range(8):
                        if t.has(0):
                            hg, kt = i // 2, i % 2
                            if i == 0:
                                pe.wait_ge(stack_loaded[t.par], t.half(16 * STACK_DMAS, 16 * STACK_DMAS * (a0 // 2 + 1)))
                                if kind == "attn_a":
                                    pe.wait_ge(max_loaded[t.par], t.half(16, 16))
                            bank2 = (ps_a if i == 1 else ps_b) if kind == "attn_a" else (ps_b if i % 2 else ps_a)
                            if kind == "attn_a":
                                need(pe, biased_ready, t.times(8, i - 1 if i in (1, 2) else i))
                            else:
                                need(pe, probs_ready, t.times(8, 8 * a0 + i - 1))
                                if kind == "attn_c" and i % 2 == 0:
                                    need(pe, seen_ready, t.times(4, i // 2))
                            q0 = P * kt if kind == "attn_c" else 0
                            for c in range(2):
                                for odd in range(2):
                                    h = 4 * hg + 2 * c + odd
                                    ins = mm(bank2[:, odd, c * TOK + q0:(c + 1) * TOK], head(stack_k, t, h, rows_)[:, kt * P:(kt + 1) * P], head(stack_q, t, h, rows_)[:, q0:TOK], start=True, stop=True, skip_group_check=True)
                            ins.then_inc(scores_filled, 1)
                        first, end = QUERY_SLOTS.get(i, (0, 0))
                        if kind == "attn_a" and t.has(1):
                            query_scores(t + 1, first, first + (end - first) // 2)
                        if kind == "attn_a" and t.has(2) and i == 1:
                            query_and_key()
                        if t.has(0) and i:
                            pv(i - 1)
                        if kind == "attn_a" and t.has(1):
                            query_scores(t + 1, first + (end - first) // 2, end)
                        if kind == "attn_a" and t.has(1) and i == 7:
                            b = t + 1
                            pe.wait_ge(maxed, b.times(16, 16))
                            need(pe, t_drained, fill_t(k, "max", b, -1))
                            for j in range(TILES):
                                ins = nc.tensor.transpose(ps_t[0:H, j * P:(j + 1) * P], neg_max[:, j, :], ident[:, :])
                            ins.then_inc(max_filled, 1)
                            values()
                        if t.has(-1):
                            b = t + -1
                            if i in (1, 2):
                                qt = i - 1
                                pe.wait_ge(ctx_copied, b.times(1, a0 + 1))
                                need(pe, u_drained, fill_u(k, f"ctx{qt}", b, -1))
                                for g in range(HG):
                                    ins = nc.tensor.transpose(ps_u[:, g * P:(g + 1) * P], ctx_raw[:, g, qt * P:(qt + 1) * P], ident[:, :])
                                ins.then_inc(ctx_filled, 1)
                            if i == 4:
                                pe.wait_ge(u_drained, fill_u(k, "ctx1", b))
                                need(pe, t_drained, fill_t(k, "ctx", b, -1))
                                for j in range(TILES):
                                    ins = nc.tensor.transpose(ps_t[:, j * P:(j + 1) * P], ctx_n[:, j, :], ident[:, :])
                                ins.then_inc(ctxT_filled, 1)
                            if i == 5 and kind != "attn_a":
                                pe.wait_ge(t_drained, fill_t(k, "ctx", b))
                                need(pe, u_drained, fill_u(k, "update", b, -1))
                                wo = w[{"attn_b": "b_wproj", "attn_c": "c_wout"}[kind]]
                                for j in range(TILES):
                                    ins = mm(ps_u[:, j * D:(j + 1) * D], ctx_T[b.par][:, j * P:(j + 1) * P], wo[:, :], start=True, stop=True)
                                ins.then_inc(update_filled, 1)
                            if i == 7 and kind != "attn_a":
                                ln_transpose(pe, k, b)
                    if t.has(0):
                        pv(7)
                def out_a(t):
                    if t.has(1):
                        need(pe, u_drained, fill_u(k, "update", t + 1, -1))
                        for j in range(TILES):
                            ins = mm(ps_u[:, j * D:(j + 1) * D], ctx_flip[:, TILES * (t.off + 1) + j, :, :].rearrange("p b n -> p (b n)"), w["a_wo"][:, :], start=True, stop=True)
                        ins.then_inc(update_filled, 1)
                    if t.has(-1):
                        ln_transpose(pe, k, t + -1)

                def moe(t):
                    for v in range(8):
                        b, u = unit(t, v, 2)
                        if b.has(0):
                            if u == 0:
                                pe.wait_ge(xpart_ready, b.times(1, o0 + 1))
                            need(pe, hn_ready, b.times(8, 8 * o0 + u - 3))
                            for j in range(TILES):
                                o = h_bank(u)[:, j * TOK:(j + 1) * TOK]
                                mm(o, ones3[:, :], b1_rows[:, 2 * u * D:(2 * u + 2) * D], start=True, stop=False)
                                for xp, wp in ((0, 0), (0, 1), (1, 0)):
                                    ins = mm(o, x_part[b.par][:, xp, j * P:(j + 1) * P], w1_part[wp][:, 2 * u:2 * u + 2, :].rearrange("p e d -> p (e d)"), start=False, stop=(xp == 1))
                            ins.then_inc(h_filled, 1)
                        b, u = unit(t, v, -2)
                        if b.has(0):
                            if u == 0:
                                need(pe, u_drained, fill_u(k, "update", b, -1))
                                for j in range(TILES):
                                    mm(ps_u[:, j * D:(j + 1) * D], gate_f[b.par][:, j * P:(j + 1) * P], b2_rows[:, :], start=(j == 0), stop=False, skip_group_check=True)
                            pe.wait_ge(gated_ready, b.times(8, 8 * o0 + u + 1))
                            for e in range(2):
                                for j in range(TILES):
                                    ins = mm(ps_u[:, j * D:(j + 1) * D], ag[u % 2][:, e, j * P:(j + 1) * P], w["w2"][:, 2 * u + e, :], start=False, stop=(u == 7 and e == 1), skip_group_check=True)
                            ins.then_inc(w2_done, 1)
                        if t.has(0):
                            pe.wait_ge(hn_ready, t.times(8, 8 * o0 + v + 1))
                            need(pe, gelu_ready, t.times(8, 8 * o0 + v))
                            for e in range(2):
                                for j in range(TILES):
                                    ins = nc.tensor.transpose(ps_b[:, 0, e * TOK + j * P:e * TOK + (j + 1) * P], hn[v % 2][:, e, j, :], ident[:, :])
                            ins.then_inc(hT_filled, 1)
                            if v == 0:
                                pe.wait_ge(t_drained, fill_t(k, "gate", t))
                            need(pe, gated_ready, t.times(8, 8 * o0 + v))
                            for e in range(2):
                                ins = mm(ps_b[:, 1, e * TOK:(e + 1) * TOK], gate_sel[:, 2 * v + e, :], gate_b[t.par][:, :], start=True, stop=True)
                            ins.then_inc(wb_filled, 1)
                        if v == 1 and t.has(1):
                            b = t + 1
                            has_cur(pe, k, b)
                            need(pe, t_drained, fill_t(k, "logits", b, -1))
                            for j in range(TILES):
                                ins = mm(ps_t[:, j * E:(j + 1) * E], xc(b, j), w["wr"][:, :], start=True, stop=True)
                            ins.then_inc(logits_filled, 1)
                        if v == 5 and t.has(1):
                            b = t + 1
                            pe.wait_ge(pack_ready, b.times(1, o0 + 1))
                            need(pe, t_drained, fill_t(k, "gate", b, -1))
                            for j in range(TILES):
                                ins = nc.tensor.transpose(ps_t[0:96, j * P:(j + 1) * P], gate_pack[:, j, :], ident[:, :])
                            ins.then_inc(gate_filled, 1)
                        if v == 6 and t.has(-1):
                            ln_transpose(pe, k, t + -1)

                def ssm(t):
                    if t.has(1):
                        b = t + 1
                        pe.wait_ge(scanned, b.times(1, 1))
                        need(pe, stats_ready, b.times(1, NB * ln_no[k] - 1))
                        for j in range(TILES):
                            ins = mm(ps_b[:, b.par, j * D:(j + 1) * D], states[b.par][:, j * P:(j + 1) * P], w["s_wc"][:, :], start=True, stop=True)
                        ins.then_inc(y_filled, 1)
                    if t.has(2):
                        b = t + 2
                        has_cur(pe, k, b)
                        need(pe, scanned, b.times(1, -1))
                        mm(ps_a[:, b.par, 0:TOK], w["s_wb"][:, :], xc(b), start=True, stop=True).then_inc(ub_filled, 1)
                    if t.has(-1):
                        ln_transpose(pe, k, t + -1)

                def mix(t):
                    if t.has(0):
                        pe.wait_ge(ksq_ready, t.times(1, o0 + 1))
                        need(pe, stats_ready, t.times(1, NB * ln_no[k] - 1))
                        for j in range(TILES):
                            ins = mm(ps_b[:, t.par, j * D:(j + 1) * D], k_sq[t.par][:, j * P:(j + 1) * P], w["m_wv"][:, :], start=True, stop=True)
                        ins.then_inc(o_filled, 1)
                    if t.has(1):
                        b = t + 1
                        pe.wait_ge(mixx_ready, b.times(1, o0 + 1))
                        need(pe, rsig_ready, b.times(1, o0))
                        need(pe, krelu_ready, b.times(1, o0))
                        for j in range(TILES):
                            mm(ps_a[:, 0, j * D:(j + 1) * D], mix_x[b.par][:, 0, j * P:(j + 1) * P], w["m_wr"][:, :], start=True, stop=True)
                        mm(ps_a[:, 1, 0:TOK], w["m_wk"][:, :], mix_x[b.par][:, 1, :], start=True, stop=True).then_inc(rk_filled, 1)
                    if t.has(-1) and not last:
                        ln_transpose(pe, k, t + -1)

                if k == 3:
                    pe.wait_ge(setup_pool, 4)
                    pe.wait_ge(setup_done, 1)
                    pe.wait_ge(setup_dma, 48)
                body = {"out_a": out_a, "moe": moe, "ssm": ssm, "mix": mix}.get(kind, attn)
                f, l, lo, trips = SWEEP[kind]
                if kind == "out_a":
                    for i in range(2):
                        pe.wait_ge(ctx_sent[i], 16 * SPAN * (NB // 2))
                    for t in range(f, l + 1):
                        out_a(At(None, t))
                else:
                    sweep(pe, None, 0, body, f, l, lo, trips)


def kernel(**inputs):
    import numpy as _np
    import concourse.bacc as _bacc
    from concourse import mybir as _mybir
    from concourse.bass_utils import run_bass_kernel_spmd as _run

    a = {n: _np.asarray(v) for n, v in inputs.items()}
    tb_len = a["L0_attn_a_time_bias"].shape[-1]
    pos = _np.arange(TOK)
    idx = _np.clip(pos[None, :] - pos[:, None] + tb_len // 2, 0, tb_len - 1)
    order = pos.reshape(-1, SPAN).T.reshape(-1)
    idx = idx[order][:, order]
    tb = a["L0_attn_a_time_bias"].reshape(-1)
    perm = _np.arange(D).reshape(H // 2, 2, HD).transpose(1, 2, 0).reshape(-1)
    perm_qk = _np.concatenate([perm, D + perm])
    perm_qkv = _np.concatenate([perm_qk, _np.arange(2 * D, 3 * D)])
    qk_scale = _np.stack([_np.tile(a["L0_attn_b_q_scale"], H)[perm], _np.tile(a["L0_attn_b_k_scale"], H)[perm]])
    swap = _np.arange(2 * D).reshape(2 * H, 2, HD // 2)[:, ::-1].reshape(-1)
    inv_freq = (1.0 / _np.float32(10000.0) ** (_np.arange(HD // 2, dtype=_np.float32) / _np.float32(HD // 2))).astype(_np.float32)
    freqs = (_np.arange(TOK, dtype=_np.float32)[:, None] * inv_freq[None, :]).astype(_np.float32)
    turn = _np.float32(HD ** -0.25)
    cos, sin = (_np.cos(freqs) * turn).astype(_np.float32), (_np.sin(freqs) * turn).astype(_np.float32)
    arrays = {
        "x": a["L0_attn_a_x"],
        "a_wq": a["L0_attn_a_Wq"].T[:, perm], "a_wk": a["L0_attn_a_Wk"].T[:, perm], "a_wv": a["L0_attn_a_Wv"].T, "a_wo": a["L0_attn_a_Wo"].T,
        "a_bq": a["L0_attn_a_bq"][perm], "a_bk": a["L0_attn_a_bk"][perm], "a_bv": a["L0_attn_a_bv"], "a_bo": a["L0_attn_a_bo"],
        "et": a["L0_attn_a_et_gate"].reshape(1), "is": a["L0_attn_a_is_gate"].reshape(1),
        "bias_q": tb[idx], "bias_k": tb[idx.T],
        "b_wqkv": a["L0_attn_b_Wqkv"][:, perm_qkv], "b_wproj": a["L0_attn_b_Wproj"], "b_bproj": a["L0_attn_b_bproj"],
        "qk_scale": qk_scale,
        "wr": a["L0_ffn_Wr"], "br": a["L0_ffn_br"], "w1": a["L0_ffn_W1"], "b1": a["L0_ffn_b1"],
        "g1": a["L0_ffn_g1"].T, "be1": a["L0_ffn_be1"].T, "w2": a["L0_ffn_W2"], "b2": a["L0_ffn_b2"],
        "log_a": a["L1_attn_a_log_a"], "s_wb": a["L1_attn_a_W_b"].T, "s_wc": a["L1_attn_a_W_c"].T,
        "s_gamma": a["L1_attn_a_gamma"], "s_beta": a["L1_attn_a_beta"],
        "c_wqkv": a["L1_attn_b_w_qkv"][:, perm_qkv], "c_wswap": a["L1_attn_b_w_qkv"][:, swap][:, perm_qk], "c_wout": a["L1_attn_b_w_out"],
        "m_wr": a["L1_ffn_W_r"].T, "m_wk": a["L1_ffn_W_k"].T, "m_wv": a["L1_ffn_W_v"].T,
        "mu_r": a["L1_ffn_mu_r"], "mu_k": a["L1_ffn_mu_k"],
        "rope_cos": _np.concatenate([cos, cos], axis=1), "rope_sin": _np.concatenate([-sin, sin], axis=1),
    }
    nc = _bacc.Bacc("TRN2", target_bir_lowering=False, num_devices=1)
    io, ins = {}, {}
    for name, v in arrays.items():
        v = _np.ascontiguousarray(v)
        ins["in_" + name] = v
        io[name] = nc.dram_tensor("in_" + name, v.shape, _mybir.dt.from_np(v.dtype), kind="ExternalInput").ap()
    out = nc.dram_tensor("out_x", a["L0_attn_a_x"].shape, _mybir.dt.float32, kind="ExternalOutput").ap()
    hybrid_kernel(nc, io, out)
    r = _run(nc, [ins], core_ids=[0])
    return r.results[0]["out_x"]
```
